# Optimizing a Trainium2 kernel written in Bass

```python
import numpy as np
import jax
import jax.numpy as jnp

def _softmax(x, axis=-1):
    return jax.nn.softmax(x, axis=axis)

def _gelu(x):
    return jax.nn.gelu(x, approximate=True)

def _silu(x):
    return jax.nn.silu(x)

def _sigmoid(x):
    return jax.nn.sigmoid(x)

def _layernorm(x, axis=-1, eps=1e-05):
    m = jnp.mean(x, axis=axis, keepdims=True)
    v = jnp.var(x, axis=axis, keepdims=True)
    return (x - m) / jnp.sqrt(v + eps)

def _scatter_add(tgt, idx, src, axis=0):
    return tgt.at[idx].add(src)

def _segment_sum(src, seg, n):
    return jax.ops.segment_sum(src, seg, n)
kernel_name = 'mk_lm_tower_d1_tok_ids256_r4_ca94a4'

def setup_inputs(seed: int=0):
    np.random.seed(seed)
    _w = jnp.asarray

    def _rec_inputs():
        import jax
        import jax.numpy as jnp
        _rk = jax.random.key(seed)
        x = jax.random.randint(jax.random.fold_in(_rk, 1), (2, 1024), 0, 127999, jnp.int32)
        return x
    x = _rec_inputs()

    def _L0_tok_setup():
        import jax, jax.numpy as jnp
        import numpy as np
        L = 1000000000.0
        key = jax.random.key(seed)
        k1, k2, k3 = jax.random.split(key, 3)
        V, D = (32000, 64)
        B, S = (32, 512)
        input_ids = jax.random.randint(k1, (B, S), 0, V, dtype=jnp.int64)
        embedding = jax.random.uniform(k2, (V, D), dtype=jnp.float32)
        gates = jax.random.uniform(k3, (V,), dtype=jnp.float32) * D
        return {'input_ids': input_ids, 'embedding': embedding, 'gates': gates}
    _L0_tok_all = _L0_tok_setup()
    _L0_tok_in = {k: v for k, v in _L0_tok_all.items() if k in ('embedding', 'gates')}
    del _L0_tok_all

    def _L0_attn_setup():
        import jax, jax.numpy as jnp
        from jax import lax
        import numpy as np
        B_, L_, D_ = (8, 128, 64)
        NL, N, DC, E = (2, 16, 4, 2)
        DI = E * D_
        DTR = (D_ + 15) // 16
        EPS = 1e-05

        def layernorm(x, g, b):
            m = jnp.mean(x, -1, keepdims=True)
            v = jnp.mean((x - m) ** 2, -1, keepdims=True)
            return (x - m) * lax.rsqrt(v + EPS) * g + b

        def rmsnorm(x, w):
            return x * lax.rsqrt(jnp.mean(x * x, -1, keepdims=True) + EPS) * w

        def mamba_block(x, inproj, convw, convb, xproj, dtw, dtb, Alog, Dp, outw):
            Bb = x.shape[0]
            xi, z = jnp.split(x @ inproj.T, 2, axis=-1)
            xc = lax.conv_general_dilated(xi.transpose(0, 2, 1), convw[:, None, :], (1,), [(DC - 1, 0)], dimension_numbers=('NCH', 'OIH', 'NCH'), feature_group_count=DI)
            xi = jax.nn.silu((xc + convb[None, :, None]).transpose(0, 2, 1))
            dbc = xi @ xproj.T
            delta = jax.nn.softplus(dbc[..., :DTR] @ dtw.T + dtb)
            Bm = dbc[..., DTR:DTR + N]
            Cm = dbc[..., DTR + N:]
            A = -jnp.exp(Alog)
            dA = jnp.exp(delta[..., None] * A)
            bx = (delta * xi)[..., None] * Bm[:, :, None, :]

            def step(h, t):
                da, b_, c = t
                h = da * h + b_
                return (h, jnp.einsum('bdn,bn->bd', h, c))
            h0 = jnp.zeros((Bb, DI, N), x.dtype)
            _, ys = lax.scan(step, h0, (dA.transpose(1, 0, 2, 3), bx.transpose(1, 0, 2, 3), Cm.transpose(1, 0, 2)))
            y = ys.transpose(1, 0, 2) + Dp * xi
            return y * jax.nn.silu(z) @ outw.T

        def mamba(x, inproj, convw, convb, xproj, dtw, dtb, Alog, Dp, outw, rms):
            for l in range(NL):
                x = x + mamba_block(rmsnorm(x, rms[l]), inproj[l], convw[l], convb[l], xproj[l], dtw[l], dtb[l], Alog[l], Dp[l], outw[l])
            return x

        def hmss(x, ln_g, ln_b, w1, b1, w2, b2, w3, b3, down_w, down_b, hconv_w, hconv_b, f_inproj, f_convw, f_convb, f_xproj, f_dtw, f_dtb, f_Alog, f_D, f_outw, f_rms, b_inproj, b_convw, b_convb, b_xproj, b_dtw, b_dtb, b_Alog, b_D, b_outw, b_rms):
            xl = layernorm(x, ln_g, ln_b)
            x1 = xl @ w1.T + b1
            x2 = xl @ w2.T + b2
            xc = lax.conv_general_dilated(x1.transpose(0, 2, 1), hconv_w, (1,), [(1, 1)], dimension_numbers=('NCH', 'OIH', 'NCH')) + hconv_b[None, :, None]
            xc = xc.transpose(0, 2, 1)
            xf = mamba(xc, f_inproj, f_convw, f_convb, f_xproj, f_dtw, f_dtb, f_Alog, f_D, f_outw, f_rms)
            xb = jnp.flip(mamba(jnp.flip(xc, 1), b_inproj, b_convw, b_convb, b_xproj, b_dtw, b_dtb, b_Alog, b_D, b_outw, b_rms), 1)
            d = jnp.concatenate([xf, xb], -1) @ down_w.T + down_b
            d = layernorm(d, ln_g, ln_b) * x2
            return d @ w3.T + b3 + x
        key = jax.random.key(seed)
        ki = iter(jax.random.split(key, 80))

        def r(shape, s=0.02):
            return jax.random.normal(next(ki), shape, jnp.float32) * s

        def mp(pfx):
            return {pfx + 'inproj': r((NL, 2 * DI, D_)), pfx + 'convw': r((NL, DI, DC)), pfx + 'convb': r((NL, DI)), pfx + 'xproj': r((NL, DTR + 2 * N, DI)), pfx + 'dtw': r((NL, DI, DTR)), pfx + 'dtb': r((NL, DI)), pfx + 'Alog': jnp.tile(jnp.log(jnp.arange(1, N + 1, dtype=jnp.float32)), (NL, DI, 1)), pfx + 'D': jnp.ones((NL, DI), jnp.float32), pfx + 'outw': r((NL, D_, DI)), pfx + 'rms': jnp.ones((NL, D_), jnp.float32)}
        inp = {'x': jax.random.normal(next(ki), (B_, L_, D_), jnp.float32), 'ln_g': jnp.ones((D_,), jnp.float32), 'ln_b': jnp.zeros((D_,), jnp.float32), 'w1': r((D_, D_)), 'b1': jnp.zeros((D_,), jnp.float32), 'w2': r((D_, D_)), 'b2': jnp.zeros((D_,), jnp.float32), 'w3': r((D_, D_)), 'b3': jnp.zeros((D_,), jnp.float32), 'down_w': r((D_, 2 * D_)), 'down_b': jnp.zeros((D_,), jnp.float32), 'hconv_w': r((D_, D_, 3)), 'hconv_b': jnp.zeros((D_,), jnp.float32)}
        inp.update(mp('f_'))
        inp.update(mp('b_'))
        return inp
    _L0_attn_all = _L0_attn_setup()
    _L0_attn_in = {k: v for k, v in _L0_attn_all.items() if k in ('ln_g', 'ln_b', 'w1', 'b1', 'w2', 'b2', 'w3', 'b3', 'down_w', 'down_b', 'hconv_w', 'hconv_b', 'f_inproj', 'f_convw', 'f_convb', 'f_xproj', 'f_dtw', 'f_dtb', 'f_Alog', 'f_D', 'f_outw', 'f_rms', 'b_inproj', 'b_convw', 'b_convb', 'b_xproj', 'b_dtw', 'b_dtb', 'b_Alog', 'b_D', 'b_outw', 'b_rms')}
    del _L0_attn_all

    def _L0_ffn_setup():
        import jax, jax.numpy as jnp
        import numpy as np
        TOP_K = 6
        LN_EPS = 1e-05
        key = jax.random.key(seed)
        ks = jax.random.split(key, 4)
        B, S, D, E = (2, 64, 64, 64)
        x = jax.random.normal(ks[0], (B, S, D), dtype=jnp.float32)
        gate_w = jax.random.normal(ks[1], (E, D), dtype=jnp.float32) * 0.02
        lattice_weights = jax.random.normal(ks[2], (E, D, D), dtype=jnp.float32) * 0.02
        out_w = jax.random.normal(ks[3], (D, D), dtype=jnp.float32) * 0.02
        out_b = jnp.zeros((D,), dtype=jnp.float32)
        ln_g = jnp.ones((D,), dtype=jnp.float32)
        ln_b = jnp.zeros((D,), dtype=jnp.float32)
        return {'x': x, 'gate_w': gate_w, 'lattice_weights': lattice_weights, 'out_w': out_w, 'out_b': out_b, 'ln_g': ln_g, 'ln_b': ln_b}
    _L0_ffn_all = _L0_ffn_setup()
    _L0_ffn_in = {k: v for k, v in _L0_ffn_all.items() if k in ('gate_w', 'lattice_weights', 'out_w', 'out_b', 'ln_g', 'ln_b')}
    del _L0_ffn_all
    return {'x': x, 'L0_tok_embedding': _L0_tok_in['embedding'], 'L0_tok_gates': _L0_tok_in['gates'], 'L0_attn_ln_g': _L0_attn_in['ln_g'], 'L0_attn_ln_b': _L0_attn_in['ln_b'], 'L0_attn_w1': _L0_attn_in['w1'], 'L0_attn_b1': _L0_attn_in['b1'], 'L0_attn_w2': _L0_attn_in['w2'], 'L0_attn_b2': _L0_attn_in['b2'], 'L0_attn_w3': _L0_attn_in['w3'], 'L0_attn_b3': _L0_attn_in['b3'], 'L0_attn_down_w': _L0_attn_in['down_w'], 'L0_attn_down_b': _L0_attn_in['down_b'], 'L0_attn_hconv_w': _L0_attn_in['hconv_w'], 'L0_attn_hconv_b': _L0_attn_in['hconv_b'], 'L0_attn_f_inproj': _L0_attn_in['f_inproj'], 'L0_attn_f_convw': _L0_attn_in['f_convw'], 'L0_attn_f_convb': _L0_attn_in['f_convb'], 'L0_attn_f_xproj': _L0_attn_in['f_xproj'], 'L0_attn_f_dtw': _L0_attn_in['f_dtw'], 'L0_attn_f_dtb': _L0_attn_in['f_dtb'], 'L0_attn_f_Alog': _L0_attn_in['f_Alog'], 'L0_attn_f_D': _L0_attn_in['f_D'], 'L0_attn_f_outw': _L0_attn_in['f_outw'], 'L0_attn_f_rms': _L0_attn_in['f_rms'], 'L0_attn_b_inproj': _L0_attn_in['b_inproj'], 'L0_attn_b_convw': _L0_attn_in['b_convw'], 'L0_attn_b_convb': _L0_attn_in['b_convb'], 'L0_attn_b_xproj': _L0_attn_in['b_xproj'], 'L0_attn_b_dtw': _L0_attn_in['b_dtw'], 'L0_attn_b_dtb': _L0_attn_in['b_dtb'], 'L0_attn_b_Alog': _L0_attn_in['b_Alog'], 'L0_attn_b_D': _L0_attn_in['b_D'], 'L0_attn_b_outw': _L0_attn_in['b_outw'], 'L0_attn_b_rms': _L0_attn_in['b_rms'], 'L0_ffn_gate_w': _L0_ffn_in['gate_w'], 'L0_ffn_lattice_weights': _L0_ffn_in['lattice_weights'], 'L0_ffn_out_w': _L0_ffn_in['out_w'], 'L0_ffn_out_b': _L0_ffn_in['out_b'], 'L0_ffn_ln_g': _L0_ffn_in['ln_g'], 'L0_ffn_ln_b': _L0_ffn_in['ln_b']}

def reference(x, L0_tok_embedding, L0_tok_gates, L0_attn_ln_g, L0_attn_ln_b, L0_attn_w1, L0_attn_b1, L0_attn_w2, L0_attn_b2, L0_attn_w3, L0_attn_b3, L0_attn_down_w, L0_attn_down_b, L0_attn_hconv_w, L0_attn_hconv_b, L0_attn_f_inproj, L0_attn_f_convw, L0_attn_f_convb, L0_attn_f_xproj, L0_attn_f_dtw, L0_attn_f_dtb, L0_attn_f_Alog, L0_attn_f_D, L0_attn_f_outw, L0_attn_f_rms, L0_attn_b_inproj, L0_attn_b_convw, L0_attn_b_convb, L0_attn_b_xproj, L0_attn_b_dtw, L0_attn_b_dtb, L0_attn_b_Alog, L0_attn_b_D, L0_attn_b_outw, L0_attn_b_rms, L0_ffn_gate_w, L0_ffn_lattice_weights, L0_ffn_out_w, L0_ffn_out_b, L0_ffn_ln_g, L0_ffn_ln_b):
    import jax
    import jax.numpy as jnp

    def _L0_tok_ref(input_ids, embedding, gates):
        import jax, jax.numpy as jnp
        import numpy as np
        L = 1000000000.0
        D = embedding.shape[1]
        index_array = jnp.arange(D, dtype=embedding.dtype)
        vec = embedding[input_ids]
        g = gates[input_ids]
        frac = g * L - jnp.floor(g * L)
        soft = frac / L * jnp.tanh(g)
        hard = (index_array[None, None, :] < g[..., None]).astype(embedding.dtype)
        mask = hard + soft[..., None]
        return vec * mask

    def _L0_attn_ref(x, ln_g, ln_b, w1, b1, w2, b2, w3, b3, down_w, down_b, hconv_w, hconv_b, f_inproj, f_convw, f_convb, f_xproj, f_dtw, f_dtb, f_Alog, f_D, f_outw, f_rms, b_inproj, b_convw, b_convb, b_xproj, b_dtw, b_dtb, b_Alog, b_D, b_outw, b_rms):
        import jax, jax.numpy as jnp
        from jax import lax
        import numpy as np
        B_, L_, D_ = (8, 128, 64)
        NL, N, DC, E = (2, 16, 4, 2)
        DI = E * D_
        DTR = (D_ + 15) // 16
        EPS = 1e-05

        def layernorm(x, g, b):
            m = jnp.mean(x, -1, keepdims=True)
            v = jnp.mean((x - m) ** 2, -1, keepdims=True)
            return (x - m) * lax.rsqrt(v + EPS) * g + b

        def rmsnorm(x, w):
            return x * lax.rsqrt(jnp.mean(x * x, -1, keepdims=True) + EPS) * w

        def mamba_block(x, inproj, convw, convb, xproj, dtw, dtb, Alog, Dp, outw):
            Bb = x.shape[0]
            xi, z = jnp.split(x @ inproj.T, 2, axis=-1)
            xc = lax.conv_general_dilated(xi.transpose(0, 2, 1), convw[:, None, :], (1,), [(DC - 1, 0)], dimension_numbers=('NCH', 'OIH', 'NCH'), feature_group_count=DI)
            xi = jax.nn.silu((xc + convb[None, :, None]).transpose(0, 2, 1))
            dbc = xi @ xproj.T
            delta = jax.nn.softplus(dbc[..., :DTR] @ dtw.T + dtb)
            Bm = dbc[..., DTR:DTR + N]
            Cm = dbc[..., DTR + N:]
            A = -jnp.exp(Alog)
            dA = jnp.exp(delta[..., None] * A)
            bx = (delta * xi)[..., None] * Bm[:, :, None, :]

            def step(h, t):
                da, b_, c = t
                h = da * h + b_
                return (h, jnp.einsum('bdn,bn->bd', h, c))
            h0 = jnp.zeros((Bb, DI, N), x.dtype)
            _, ys = lax.scan(step, h0, (dA.transpose(1, 0, 2, 3), bx.transpose(1, 0, 2, 3), Cm.transpose(1, 0, 2)))
            y = ys.transpose(1, 0, 2) + Dp * xi
            return y * jax.nn.silu(z) @ outw.T

        def mamba(x, inproj, convw, convb, xproj, dtw, dtb, Alog, Dp, outw, rms):
            for l in range(NL):
                x = x + mamba_block(rmsnorm(x, rms[l]), inproj[l], convw[l], convb[l], xproj[l], dtw[l], dtb[l], Alog[l], Dp[l], outw[l])
            return x

        def hmss(x, ln_g, ln_b, w1, b1, w2, b2, w3, b3, down_w, down_b, hconv_w, hconv_b, f_inproj, f_convw, f_convb, f_xproj, f_dtw, f_dtb, f_Alog, f_D, f_outw, f_rms, b_inproj, b_convw, b_convb, b_xproj, b_dtw, b_dtb, b_Alog, b_D, b_outw, b_rms):
            xl = layernorm(x, ln_g, ln_b)
            x1 = xl @ w1.T + b1
            x2 = xl @ w2.T + b2
            xc = lax.conv_general_dilated(x1.transpose(0, 2, 1), hconv_w, (1,), [(1, 1)], dimension_numbers=('NCH', 'OIH', 'NCH')) + hconv_b[None, :, None]
            xc = xc.transpose(0, 2, 1)
            xf = mamba(xc, f_inproj, f_convw, f_convb, f_xproj, f_dtw, f_dtb, f_Alog, f_D, f_outw, f_rms)
            xb = jnp.flip(mamba(jnp.flip(xc, 1), b_inproj, b_convw, b_convb, b_xproj, b_dtw, b_dtb, b_Alog, b_D, b_outw, b_rms), 1)
            d = jnp.concatenate([xf, xb], -1) @ down_w.T + down_b
            d = layernorm(d, ln_g, ln_b) * x2
            return d @ w3.T + b3 + x
        return hmss(x, ln_g, ln_b, w1, b1, w2, b2, w3, b3, down_w, down_b, hconv_w, hconv_b, f_inproj, f_convw, f_convb, f_xproj, f_dtw, f_dtb, f_Alog, f_D, f_outw, f_rms, b_inproj, b_convw, b_convb, b_xproj, b_dtw, b_dtb, b_Alog, b_D, b_outw, b_rms)

    def _L0_ffn_ref(x, gate_w, lattice_weights, out_w, out_b, ln_g, ln_b):
        import jax, jax.numpy as jnp
        import numpy as np
        TOP_K = 6
        LN_EPS = 1e-05
        logits = jnp.einsum('bsd,ed->bse', x, gate_w)
        top_logits, indices = jax.lax.top_k(logits, TOP_K)
        scores = jax.nn.softmax(top_logits, axis=-1)
        W_sel = lattice_weights[indices]
        xW = jnp.einsum('bsd,bskde->bske', x, W_sel)
        lattice_out = jnp.einsum('bske,bsk->bse', xW, scores)
        proj = jnp.einsum('bsd,ed->bse', lattice_out, out_w) + out_b
        h = x + proj
        mu = jnp.mean(h, axis=-1, keepdims=True)
        var = jnp.mean(jnp.square(h - mu), axis=-1, keepdims=True)
        return (h - mu) * jax.lax.rsqrt(var + LN_EPS) * ln_g + ln_b
    h = _L0_tok_ref(x, L0_tok_embedding, L0_tok_gates)
    h = h + _L0_attn_ref(_layernorm(h, axis=-1), L0_attn_ln_g, L0_attn_ln_b, L0_attn_w1, L0_attn_b1, L0_attn_w2, L0_attn_b2, L0_attn_w3, L0_attn_b3, L0_attn_down_w, L0_attn_down_b, L0_attn_hconv_w, L0_attn_hconv_b, L0_attn_f_inproj, L0_attn_f_convw, L0_attn_f_convb, L0_attn_f_xproj, L0_attn_f_dtw, L0_attn_f_dtb, L0_attn_f_Alog, L0_attn_f_D, L0_attn_f_outw, L0_attn_f_rms, L0_attn_b_inproj, L0_attn_b_convw, L0_attn_b_convb, L0_attn_b_xproj, L0_attn_b_dtw, L0_attn_b_dtb, L0_attn_b_Alog, L0_attn_b_D, L0_attn_b_outw, L0_attn_b_rms)
    h = h + _L0_ffn_ref(_layernorm(h, axis=-1), L0_ffn_gate_w, L0_ffn_lattice_weights, L0_ffn_out_w, L0_ffn_out_b, L0_ffn_ln_g, L0_ffn_ln_b)
    return h

_drawn_inputs = setup_inputs


def setup_inputs(seed=0):
    import zlib

    import numpy as np

    out = dict(_drawn_inputs(seed))
    spreads = {'L0_attn_ln_g': (1.0, 0.6),
     'L0_attn_ln_b': (0.0, 0.8),
     'L0_attn_b1': (0.0, 0.8),
     'L0_attn_b2': (0.0, 0.533),
     'L0_attn_b3': (0.0, 0.1),
     'L0_attn_down_b': (0.0, 0.8),
     'L0_attn_hconv_b': (0.0, 2.0),
     'L0_attn_f_D': (1.0, 0.6),
     'L0_attn_f_rms': (1.0, 0.6),
     'L0_attn_b_D': (1.0, 0.6),
     'L0_attn_b_rms': (1.0, 0.6),
     'L0_ffn_out_b': (0.0, 0.1),
     'L0_ffn_ln_g': (1.0, 0.2),
     'L0_ffn_ln_b': (0.0, 0.1)}
    factors = {'L0_attn_w1': 8.0,
     'L0_attn_w2': 2.673,
     'L0_attn_down_w': 8.0,
     'L0_attn_hconv_w': 8.0,
     'L0_attn_f_inproj': 8.0,
     'L0_attn_f_convw': 8.0,
     'L0_attn_f_convb': 47.385,
     'L0_attn_f_xproj': 40.645,
     'L0_attn_f_dtb': 64.0,
     'L0_attn_f_Alog': 64.0,
     'L0_attn_f_outw': 8.0,
     'L0_attn_b_inproj': 8.0,
     'L0_attn_b_convw': 8.0,
     'L0_attn_b_convb': 44.268,
     'L0_attn_b_xproj': 38.372,
     'L0_attn_b_dtb': 64.0,
     'L0_attn_b_Alog': 64.0,
     'L0_attn_b_outw': 8.0,
     'L0_ffn_gate_w': 8.0,
     'L0_ffn_lattice_weights': 8.0,
     'L0_ffn_out_w': 8.0,
     'L0_attn_f_dtw': 8.0,
     'L0_attn_b_dtw': 8.0}
    for name, (base, spread) in spreads.items():
        noise = np.random.default_rng([zlib.crc32(name.encode()), seed]).standard_normal(out[name].shape)
        drawn = base * np.exp(spread * noise) if base else spread * noise
        out[name] = jnp.asarray(drawn.astype(out[name].dtype))
    for name, factor in factors.items():
        out[name] = (out[name] * factor).astype(out[name].dtype)
    return out
```

```python
from contextlib import ExitStack

import concourse.bass as bass
from concourse import mybir

F32 = mybir.dt.float32
F32R = mybir.dt.float32r
I32 = mybir.dt.int32
U32 = mybir.dt.uint32
ALU = mybir.AluOpType
ACT = mybir.ActivationFunctionType
AX_X = mybir.AxisListType.X

P = 128
V, D = 32000, 64
NB, T = 2, 1024
J = T // P
NC = NB * J
HALF = NC // 2 * D
DI, NS, TAPS, RANK = 128, 16, 4, 4
GR = P // NS
NG = DI // GR
H = 512
BLOCKS = 4
STEPS = 2 * NG
E, TOPK = 64, 6
ES, DS = 16, 8
NE, ND = E // ES, D // DS
NZ = NB * NE * ND
EPS = 1e-5
GATE_L = 1e9
BIG = 3.0e38
LOG_MOST = 80.0

WX, WZ, CW, XB, XC, X4, DTW = 0, 128, 256, 512, 640, 768, 896
RMS, CONVB, DTB, WPACK = 1024, 1025, 1026, 1027
RES = NG + 1
IDN, SUM, ONE, IOTA, CEPS, C1, CPACK = 0, 128, 256, 384, 448, 449, 450
SEL, SELE, SPACK = 0, 1024, 1536
W1, W2, W3, DOWN, GATEW, OUTW, HCONV = 0, 64, 128, 192, 256, 320, 384
LNG, LNB, B1, HB, MPACK = 576, 577, 578, 579, 580
R_B2, R_DOWNB, R_LNG, R_LNB, R_B3, R_OUTB, R_FG, R_FB = range(8)

DA_RING, U_RING, DTA_RING, HC_RING, H_RING = 2, 3, 8, 8, 8
AHEAD = 4
CUT = 9
PER_BLOCK = 25
ARENA = 34000
ZRING = 6
K_DT, K_MS, K_XI, K_Z, K_DP, K_BC = 0, 1, 3, 5, 7, 9


def group_of(k):
    return (k % 4) * 4 + k // 4


def step_no(unit, s):
    return 2 * STEPS * unit[0] + STEPS * unit[1] + s


def unit_no(unit):
    return 2 * unit[0] + unit[1]


def prep_no(unit, k):
    return PER_BLOCK * unit[0] + 12 * unit[1] + k + 1


def x_at(i, b):
    return (NB * (i % 2) + b) * T


def x_no(slot, b, half):
    return 4 * slot + 2 * b + half + 1


def run_slots(loop, slot, prepare):
    for s in range(STEPS):
        prepare((0, 0), s)
    for s in range(-AHEAD, CUT):
        slot((0, 0), None, (0, 1), s)
        if s >= 0:
            prepare((0, 1), s)

    def rest_of_block(i, last):
        for s in range(CUT, STEPS):
            slot((i, 0), None, (i, 1), s)
            prepare((i, 1), s)
        for s in range(STEPS):
            slot((i, 1), (i, 0), None if last else (i + 1, 0), s)
            if not last:
                prepare((i + 1, 0), s)
        for s in range(CUT):
            slot(None if last else (i + 1, 0), (i, 1), None if last else (i + 1, 1), s)
            if not last:
                prepare((i + 1, 1), s)

    with loop(0, BLOCKS - 1) as i:
        rest_of_block(i, False)
    rest_of_block(BLOCKS - 1, True)


def tower_kernel(nc, ids, table, wpack, outw, res, consts, spack, mpack, rows, lattice, out):
    with ExitStack() as ctx:
        def sb(name, shape, dt=F32):
            return ctx.enter_context(nc.sbuf_tensor(name, shape, dt))

        def sem(name):
            return ctx.enter_context(nc.semaphore(name))

        stack = [sb(f"stack{b}", [P, 4 * T], F32R) for b in range(NB)]
        hi, lo = sb("hi", [P, T], F32R), sb("lo", [P, T], F32R)
        sel = sb("sel", [P, SPACK], F32R)

        bank = [ctx.enter_context(nc.psum_tensor(f"bank{i}", [P, H], F32)) for i in range(8)]
        da_bank, u_bank, y_bank, p_bank = bank[0:2], bank[2:5], bank[5:7], bank[7]

        cst = sb("cst", [P, CPACK])
        mix = sb("mix", [P, MPACK])
        row = sb("row", [P, 8 * D])
        reside = sb("reside", [P, BLOCKS * RES])
        alog = sb("alog", [P, BLOCKS * NG])
        neg_a = sb("neg_a", [P, BLOCKS * NG])
        last_h = sb("last_h", [P, NG])
        a_cur, a_next = sb("a_cur", [P, NG]), sb("a_next", [P, NG])
        wraw = sb("wraw", [P, WPACK])
        out_w = sb("out_w", [P, D])
        w_xi = sb("w_xi", [P, 2 * DI])
        w_z = sb("w_z", [D, DI])
        w_dt = sb("w_dt", [P, DI])
        h = sb("h", [P, NC * D])
        hn = sb("hn", [P, NC * D])
        x2 = sb("x2", [P, NC * D])
        idx_i = sb("idx_i", [P, NC], I32)
        idx_f = sb("idx_f", [P, NC])
        idx_g = sb("idx_g", [P, NC])
        idx_u = sb("idx_u", [P, NC], U32)
        whole_i = sb("whole_i", [P, NC], I32)
        small = sb("small", [P, 12 * NC])
        top8 = sb("top8", [P, NC * 8])

        arena = sb("arena", [P, ARENA])
        place = [0]

        def cut(n):
            place[0] += n
            assert place[0] <= 45600
            return arena[:, place[0] - n:place[0]]

        xs = cut(2 * NB * T)
        xn2 = cut(T + 4)
        scr_a, scr_b, scr_c = cut(T), cut(T), cut(T)
        after_xs = place[0]
        xi = [cut(T) for _ in range(NB)]
        sz = [cut(T) for _ in range(NB)]
        dl, uu = cut(T), cut(T)
        brep = [cut(T) for _ in range(NB)]
        crep = [cut(T) for _ in range(NB)]
        hcr = [cut(H) for _ in range(HC_RING)]
        yz = [cut(H) for _ in range(2)]
        dta = [cut(H) for _ in range(DTA_RING)]
        hst_all = cut(H_RING * H)
        hst = [hst_all[:, k * H:(k + 1) * H] for k in range(H_RING)]
        place[0] = after_xs
        work_a, work_b, feat_t, x1p = cut(T), cut(T), cut(NB * T), cut(NB * (T + 2))
        xcat = cut(NB * T)
        tok = cut(NC * (D + 1))
        sel_raw = cut(SPACK)
        place[0] = 0
        xrep, srep = cut(ND * NB * T), cut(NE * NB * T)
        zring_all = cut(ZRING * T)
        zring = [zring_all[:, k * T:(k + 1) * T] for k in range(ZRING)]
        lat = cut(NE * ND * D)
        x3, lat_t = cut(T), xrep[:, 0:T]
        x3_t = zring_all[0:D, 0:2 * T]
        rest_of_gate, chosen, weighed = (srep[:, k * T:(k + 1) * T] for k in range(3))
        ffn_a, ffn_b = hn[:, :], x2[:, :]
        x_stack, gate_stack = stack[0][:, 0:2 * T], stack[0][:, 2 * T:4 * T]

        def tiles(ap, w=D):
            return ap.rearrange("p (c d) -> p c d", d=w)

        def stat(n):
            return small[:, n * NC:(n + 1) * NC]

        def spread(ap, n=D):
            return ap.unsqueeze(2).to_broadcast([P, NC, n])

        def row_of(n, tiles_=NC):
            return row[:, n * D:(n + 1) * D].unsqueeze(1).to_broadcast([P, tiles_, D])

        def halves(ap):
            return [ap[:, 0:HALF], ap[:, HALF:2 * HALF]]

        ids_in, cst_in, mix_in, row_in, res_in, lat_in = (sem(n) for n in (
            "ids_in", "cst_in", "mix_in", "row_in", "res_in", "lat_in"))
        w_in, outw_in, shifted = sem("w_in"), sem("outw_in"), sem("shifted")
        hi_moved, lo_moved = sem("hi_moved"), sem("lo_moved")
        sel_in, sel_done = sem("sel_in"), sem("sel_done")
        idx_step, gathered, hard_step = sem("idx_step"), sem("gathered"), sem("hard_step")
        tanh_done, h_done = sem("tanh_done"), sem("h_done")
        ln_step, ln_square, ln_rstd, ln_log = sem("ln_step"), sem("ln_square"), sem("ln_rstd"), sem("ln_log")
        xl_turned, xl_kept, x1_made, x1_kept = sem("xl_turned"), sem("xl_kept"), sem("x1_made"), sem("x1_kept")
        x1_zero, x2_made, x2_kept, conv_made = sem("x1_zero"), sem("x2_made"), sem("x2_kept"), sem("conv_made")
        a_capped, a_exp, a_neg, a_copied, a_fetched, xn_zero = sem("a_capped"), sem("a_exp"), sem("a_neg"), sem("a_copied"), sem("a_fetched"), sem("xn_zero")
        x_ready, x_squared, r_ready = sem("x_ready"), sem("x_squared"), sem("r_ready")
        xn_ready, w_scaled = sem("xn_ready"), sem("w_scaled")
        prep_mm, prep_read = sem("prep_mm"), sem("prep_read")
        dt_abs, dt_exp, dt_log, dt_made, u_made, hi_made, lo_made = (sem(n) for n in (
            "dt_abs", "dt_exp", "dt_log", "dt_made", "u_made", "hi_made", "lo_made"))
        da_mm, u_mm, dta_ready = sem("da_mm"), sem("u_mm"), sem("dta_ready")
        last_saved = sem("last_saved")
        bx_done, scan_done, hc_done, hc_summed = sem("bx_done"), sem("scan_done"), sem("hc_done"), sem("hc_summed")
        yd_done, yz_done, out_mm = sem("yd_done"), sem("yz_done"), sem("out_mm")
        cat_done, down_made, down_step = sem("cat_done"), sem("down_made"), sem("down_step")
        q_turned, q_kept, y3_made = sem("q_turned"), sem("q_kept"), sem("y3_made")
        x3_turned, x3_kept, gate_made, gate_step = sem("x3_turned"), sem("x3_kept"), sem("gate_made"), sem("gate_step")
        gate_exp, rep_made = sem("gate_exp"), sem("rep_made")
        gate_turned, gate_high, gate_low = sem("gate_turned"), sem("gate_high"), sem("gate_low")
        x3_high, x3_low = sem("x3_high"), sem("x3_low")
        rep_act, rep_dve = sem("rep_act"), sem("rep_dve")
        z_dve, z_pool, z_used = sem("z_dve"), sem("z_pool"), sem("z_used")
        lat_act, lat_dve, proj_made, end_step = sem("lat_act"), sem("lat_dve"), sem("proj_made"), sem("end_step")
        top_done, out_ready, stored = sem("top_done"), sem("out_ready"), sem("stored")

        x3_v, gate_v = tiles(x3), tiles(ffn_b)
        pool_z = [n for n in range(NZ) if n % 3 == 2]
        dve_z = [n for n in range(NZ) if n % 3 != 2]
        REP_ORDER = [(part, q) for b in range(NB)
                     for part in (0, *range(NE, NE + ND), *range(1, NE)) for q in (2 * b, 2 * b + 1)]
        NREP = len(REP_ORDER)
        REP_BANKS = 6
        REP_DVE = [r for r in range(NREP) if r % 3 == 2]
        REP_ACT = [r for r in range(NREP) if r % 3 != 2]

        def spread_until(eng, r):
            eng.wait_ge(rep_act, sum(k < r for k in REP_ACT))
            eng.wait_ge(rep_dve, sum(k < r for k in REP_DVE))

        def spread_ready(eng, m):
            b, n = divmod(m, NE * ND)
            ei, di = divmod(n, ND)
            spread_until(eng, 2 * (b * (NE + ND) + (di + 2 if ei == 0 else ND + ei + 1)))

        def factors(m):
            b, n = divmod(m, NE * ND)
            ei, di = divmod(n, ND)
            return (xrep[:, (NB * di + b) * T:(NB * di + b + 1) * T],
                    srep[:, (NB * ei + b) * T:(NB * ei + b + 1) * T])

        def rep_dst(r):
            part, q = REP_ORDER[r]
            base = srep[:, part * NB * T:(part + 1) * NB * T] if part < NE else \
                xrep[:, (part - NE) * NB * T:(part - NE + 1) * NB * T]
            return base[:, q * H:(q + 1) * H]

        block = ctx.enter_context(nc.Block())

        @block.sync
        def _(sp):
            sp.dma_start(idx_i[:, :], ids.rearrange("b (p j) -> p b j", j=J)).then_inc(ids_in, 16)
            sp.dma_start(cst[:, :], consts).then_inc(cst_in, 16)
            sp.dma_start(mix[:, :], mpack).then_inc(mix_in, 16)
            sp.dma_start(row[:, :], rows).then_inc(row_in, 16)
            sp.dma_start(reside[:, :], res).then_inc(res_in, 16)
            sp.dma_start(sel_raw, spack).then_inc(sel_in, 16)
            sp.dma_start(wraw[:, :], wpack[0:P, :]).then_inc(w_in, 16)
            sp.dma_start(out_w[:, :], outw[0:P, :]).then_inc(outw_in, 16)

            def shift(unit):
                sp.wait_ge(xn_ready, unit_no(unit) + 1)
                sp.dma_start(xn2[D:2 * D, 2:2 + T], xn2[0:D, 3:3 + T]).then_inc(shifted, 16)

            def stack_up(unit, which):
                for k, (part, made, moved) in enumerate(((hi, hi_made, hi_moved), (lo, lo_made, lo_moved))):
                    sp.wait_ge(made, 2 * unit_no(unit) + which + 1)
                    for side in range(2):
                        cols = slice((2 * which + side) * T, (2 * which + side + 1) * T)
                        sp.dma_start(stack[unit[1]][k * D:(k + 1) * D, cols].bitcast(F32),
                                     part[side * D:(side + 1) * D, :].bitcast(F32)).then_inc(moved, 16)

            def moves(unit):
                shift(unit)
                stack_up(unit, 0)
                stack_up(unit, 1)

            moves((0, 0))
            with sp.Fori(0, BLOCKS - 1) as i:
                moves((i, 1))
                sp.wait_ge(prep_read, PER_BLOCK * i + PER_BLOCK)
                sp.dma_start(wraw[:, :], wpack[bass.ds(i * P + P, P), :]).then_inc(w_in, 16)
                moves((i + 1, 0))
                sp.wait_ge(out_mm, 4 * i + 4)
                sp.dma_start(out_w[:, :], outw[bass.ds(i * P + P, P), :]).then_inc(outw_in, 16)
            moves((BLOCKS - 1, 1))
            sp.wait_ge(cat_done, 4)
            sp.wait_ge(down_made, 2)
            sp.dma_start(lat, lattice).then_inc(lat_in, 16)
            sp.wait_ge(out_ready, 1)
            for b in range(NB):
                sp.dma_start(out[b].rearrange("(p j) d -> p (j d)", j=J), ffn_a[:, b * J * D:(b + 1) * J * D]) \
                    .then_inc(stored, 16)
            sp.wait_ge(stored, 32)

        @block.gpsimd
        def _(pool):
            pool.wait_ge(idx_step, 5)
            for c in range(NC):
                nc.gpsimd.indirect_dma_start(
                    tok[:, c * (D + 1):(c + 1) * (D + 1)], None, table[:, :],
                    bass.IndirectOffsetOnAxis(ap=idx_u[:, c:c + 1], axis=0)).then_inc(gathered, 16)

            def slot(cur, prev, nxt, s):
                unit, t = (cur, s - 1) if s >= 1 else (prev, STEPS - 1)
                if s < 0 or unit is None:
                    return
                b, half = unit[1], t // NG
                n = step_no(unit, t)
                pool.wait_ge(scan_done, n + 1)
                if not (isinstance(n, int) and n < HC_RING):
                    pool.wait_ge(hc_summed, n + 1 - HC_RING)
                nc.gpsimd.tensor_tensor(hcr[t % HC_RING], hst[t % H_RING], crep[b][:, half * H:(half + 1) * H],
                                        ALU.mult).then_inc(hc_done, 1)

            def prepare(unit, s):
                i, b = unit
                w = unit_no(unit)
                if s == 5:
                    pool.wait_ge(r_ready, w + 1)
                    if not isinstance(i, int) or w > 0:
                        last = (i, 0) if b else (i - 1, 1)
                        pool.wait_ge(prep_read, prep_no(last, K_Z + 1))
                    nc.gpsimd.tensor_tensor(xn2[0:D, 3:3 + T], xs[0:D, bass.ds(x_at(i, b), T)],
                                            scr_c[0:D, :], ALU.mult).then_inc(xn_ready, 1)
                if s == 19:
                    pool.wait_ge(dt_log, w + 1)
                    nc.gpsimd.tensor_tensor(dl, dl, scr_c, ALU.add).then_inc(dt_made, 1)
                if s == 20:
                    pool.wait_ge(dt_made, w + 1)
                    nc.gpsimd.tensor_tensor(uu, dl, xi[b], ALU.mult).then_inc(u_made, 1)

            run_slots(pool.Fori, slot, prepare)

            for n in pool_z:
                spread_ready(pool, n)
                if n >= ZRING:
                    pool.wait_ge(z_used, n + 1 - ZRING)
                nc.gpsimd.tensor_tensor(zring[n % ZRING], *factors(n), ALU.mult).then_inc(z_pool, 1)

        @block.scalar
        def _(act):
            eps, one = cst[:, CEPS:CEPS + 1], cst[:, C1:C1 + 1]

            def norm(n, src, sq):
                act.wait_ge(ln_step, 5 * n + 3)
                nc.scalar.activation(sq, src, ACT.Square).then_inc(ln_square, 1)
                act.wait_ge(ln_step, 5 * n + 4)
                nc.scalar.activation(stat(1), stat(0), ACT.Ln, bias=eps, scale=1.0 / D).then_inc(ln_log, 1)
                act.wait_ge(ln_log, n + 1)
                nc.scalar.activation(stat(2), stat(1), ACT.Exp, scale=-0.5).then_inc(ln_rstd, 1)

            act.wait_ge(a_capped, 1)
            nc.scalar.activation(alog[:, :], alog[:, :], ACT.Exp).then_inc(a_exp, 1)
            act.wait_ge(sel_in, 16)
            nc.scalar.copy(sel[:, :], sel_raw).then_inc(sel_done, 1)
            act.wait_ge(gathered, 16 * NC)
            nc.scalar.activation(stat(3), tiles(tok, D + 1)[:, :, D], ACT.Tanh).then_inc(tanh_done, 1)
            act.wait_ge(cst_in, 16)
            norm(0, work_a, work_b)
            norm(1, work_a, work_b)
            act.wait_ge(mix_in, 16)
            for q in range(4):
                act.wait_ge(xl_turned, q + 1)
                nc.scalar.activation(feat_t[0:D, q * H:(q + 1) * H], bank[q][0:D, :], ACT.Identity,
                                     bias=mix[0:D, LNB:LNB + 1], scale=mix[0:D, LNG:LNG + 1]).then_inc(xl_kept, 1)
            x1_v = x1p.rearrange("p (b t) -> p b t", b=NB)[0:D, :, 1:1 + T] \
                .rearrange("p b (t j) -> p b j t", j=J)
            for q in range(4):
                act.wait_ge(x1_made, q + 1)
                b, j = divmod(4 * q, J)
                nc.scalar.activation(x1_v[:, b, j:j + 4, :], bank[4 + q][0:D, :].rearrange("p (j t) -> p j t", j=4),
                                     ACT.Identity, bias=mix[0:D, B1:B1 + 1]).then_inc(x1_kept, 1)
            act.wait_ge(a_neg, 1)
            nc.scalar.copy(a_cur[:, :], neg_a[:, 0:NG]).then_inc(a_copied, 1)

            def prepare(unit, s):
                i, b = unit
                w = unit_no(unit)
                if s == 0:
                    act.wait_ge(x_ready, x_no(i, b, 1))
                    nc.scalar.activation(scr_a[0:D, :], xs[0:D, bass.ds(x_at(i, b), T)], ACT.Square) \
                        .then_inc(x_squared, 1)
                if s == 2 and b == 0:
                    act.wait_ge(prep_mm, prep_no(unit, K_DT))
                    nc.scalar.copy(w_dt[:, :], y_bank[0][:, 0:DI]).then_inc(prep_read, 1)
                if s == 3:
                    for half, src in enumerate((p_bank, y_bank[0])):
                        act.wait_ge(prep_mm, prep_no(unit, K_MS + half))
                        nc.scalar.activation(scr_b[0:D, half * H:(half + 1) * H], src[0:D, :], ACT.Ln,
                                             bias=eps[0:D, :]).then_inc(prep_read, 1)
                    act.wait_ge(prep_read, prep_no(unit, K_MS + 1))
                    nc.scalar.activation(scr_c[0:D, :], scr_b[0:D, :], ACT.Exp, scale=-0.5).then_inc(r_ready, 1)
                if s == 6 and b == 0 and not isinstance(i, int):
                    nc.scalar.copy(a_next[:, :], neg_a[:, bass.ds(i * NG, NG)]).then_inc(a_fetched, 1)
                if s == 10:
                    for k, dst in ((K_XI, xi[b]), (K_XI + 1, xi[b]), (K_Z, sz[b]), (K_Z + 1, sz[b])):
                        half = (k - K_XI) % 2
                        src = (p_bank, y_bank[1])[half]
                        act.wait_ge(prep_mm, prep_no(unit, k))
                        if k < K_Z:
                            nc.scalar.activation(dst[:, half * H:(half + 1) * H], src[:, :], ACT.Silu,
                                                 bias=wraw[:, CONVB:CONVB + 1]).then_inc(prep_read, 1)
                        else:
                            nc.scalar.activation(dst[:, half * H:(half + 1) * H], src[:, :], ACT.Silu) \
                                .then_inc(prep_read, 1)
                if s in (14, 15):
                    half = s - 14
                    src = (p_bank, y_bank[1])[half]
                    act.wait_ge(prep_mm, prep_no(unit, K_DP + half))
                    nc.scalar.activation(scr_a[:, half * H:(half + 1) * H], src[:, :], ACT.Abs,
                                         bias=wraw[:, DTB:DTB + 1]).then_inc(dt_abs, 1)
                    nc.scalar.activation(dl[:, half * H:(half + 1) * H], src[:, :], ACT.Relu,
                                         bias=wraw[:, DTB:DTB + 1]).then_inc(prep_read, 1)
                if s == 16:
                    act.wait_ge(dt_abs, 2 * w + 2)
                    nc.scalar.activation(scr_b[:, :], scr_a[:, :], ACT.Exp, scale=-1.0).then_inc(dt_exp, 1)
                if s == 17:
                    act.wait_ge(dt_exp, w + 1)
                    nc.scalar.activation(scr_c[:, :], scr_b[:, :], ACT.Ln, bias=one).then_inc(dt_log, 1)
                if s in (21, 25):
                    k = (s - 21) // 4
                    act.wait_ge(u_made if k else dt_made, w + 1)
                    if k or not (isinstance(i, int) and w == 0):
                        act.wait_ge(hi_moved, 64 * w + 32 * k)
                        act.wait_ge(lo_made, 2 * w + k)
                    nc.scalar.copy(hi[:, :], uu if k else dl).then_inc(hi_made, 1)
                if s in (24, 26):
                    half = (s - 24) // 2
                    for k, (dst, src) in enumerate(((brep[b], p_bank), (crep[b], y_bank[0]))):
                        act.wait_ge(prep_mm, prep_no(unit, K_BC + 2 * half + k))
                        nc.scalar.copy(dst[:, half * H:(half + 1) * H], src[:, :]).then_inc(prep_read, 1)

            def slot(cur, prev, nxt, s):
                unit, t = (cur, s + AHEAD) if s + AHEAD < STEPS else (nxt, s + AHEAD - STEPS)
                if unit is None:
                    return
                if t == 0 and unit[1] == 0 and not isinstance(unit[0], int):
                    act.wait_ge(a_fetched, unit[0])
                    act.wait_ge(dta_ready, step_no(unit, 0))
                    nc.scalar.copy(a_cur[:, :], a_next[:, :]).then_inc(a_copied, 1)
                    act.wait_ge(a_copied, unit[0] + 1)
                elif t == 0 and unit[1] == 0:
                    act.wait_ge(a_copied, 1)
                g = group_of(t % NG)
                n = step_no(unit, t)
                act.wait_ge(da_mm, n + 1)
                if not (isinstance(n, int) and n < DTA_RING):
                    act.wait_ge(scan_done, n + 1 - DTA_RING)
                nc.scalar.activation(dta[t % DTA_RING], da_bank[t % DA_RING][:, :], ACT.Exp,
                                     scale=a_cur[:, g:g + 1]).then_inc(dta_ready, 1)

            run_slots(act.Fori, slot, prepare)

            act.wait_ge(x_ready, x_no(BLOCKS + 1, 1, 1))
            for b in range(NB):
                nc.scalar.copy(xcat[0:D, b * T:(b + 1) * T],
                               xs[0:D, x_at(0, b):x_at(0, b) + T]).then_inc(cat_done, 1)
            norm(2, work_a, work_b)
            for q in range(4):
                act.wait_ge(q_turned, q + 1)
                nc.scalar.copy(feat_t[0:D, q * H:(q + 1) * H], bank[q][0:D, :]).then_inc(q_kept, 1)
            norm(3, x3, ffn_a)
            for q in range(4):
                act.wait_ge(x3_turned, q + 1)
                nc.scalar.copy(x3_t[:, q * H:(q + 1) * H], bank[q][0:D, :]).then_inc(x3_kept, 1)
                nc.scalar.copy(x_stack[0:D, q * H:(q + 1) * H], bank[q][0:D, :]).then_inc(x3_high, 1)
            act.wait_ge(gate_step, 3)
            nc.scalar.activation(ffn_a, ffn_a, ACT.Exp).then_inc(gate_exp, 1)
            for q in range(4):
                act.wait_ge(gate_turned, q + 1)
                nc.scalar.copy(gate_stack[0:D, q * H:(q + 1) * H], bank[q][0:D, :]).then_inc(gate_high, 1)
            for r in REP_ACT:
                act.wait_ge(rep_made, r + 1)
                nc.scalar.copy(rep_dst(r), bank[r % REP_BANKS][:, :]).then_inc(rep_act, 1)
            act.wait_ge(z_used, NZ)
            nc.scalar.copy(lat_t[:, 0:H], bank[6][:, :]).then_inc(lat_act, 1)
            norm(4, ffn_a, ffn_b)

        @block.vector
        def _(dve):
            def norm(n, src, cen, sq, dst):
                nc.vector.tensor_reduce(stat(4), tiles(src), AX_X, ALU.add).then_inc(ln_step, 1)
                dve.wait_ge(ln_step, 5 * n + 1)
                nc.vector.tensor_scalar(stat(5), stat(4), -1.0 / D, None, ALU.mult).then_inc(ln_step, 1)
                dve.wait_ge(ln_step, 5 * n + 2)
                nc.vector.tensor_tensor(tiles(cen), tiles(src), spread(stat(5)), ALU.add).then_inc(ln_step, 1)
                dve.wait_ge(ln_square, n + 1)
                nc.vector.tensor_reduce(stat(0), tiles(sq), AX_X, ALU.add).then_inc(ln_step, 1)
                dve.wait_ge(ln_rstd, n + 1)
                nc.vector.tensor_tensor(tiles(dst), tiles(cen), spread(stat(2)), ALU.mult).then_inc(ln_step, 1)

            dve.wait_ge(ids_in, 16)
            nc.vector.tensor_copy(idx_f[:, :], idx_i[:, :]).then_inc(idx_step, 1)
            dve.wait_ge(idx_step, 1)
            nc.vector.tensor_scalar(idx_g[:, :], idx_f[:, :], 0.0, float(V), ALU.is_lt, ALU.mult).then_inc(idx_step, 1)
            dve.wait_ge(idx_step, 2)
            nc.vector.tensor_tensor(idx_f[:, :], idx_f[:, :], idx_g[:, :], ALU.add).then_inc(idx_step, 1)
            dve.wait_ge(idx_step, 3)
            nc.vector.tensor_scalar(idx_g[:, :], idx_f[:, :], 0.0, float(V - 1), ALU.max, ALU.min).then_inc(idx_step, 1)
            dve.wait_ge(idx_step, 4)
            nc.vector.tensor_copy(idx_u[:, :], idx_g[:, :]).then_inc(idx_step, 1)
            nc.vector.memset(xn2[:, :], 0.0).then_inc(xn_zero, 1)
            nc.vector.memset(x1p[:, :], 0.0).then_inc(x1_zero, 1)
            dve.wait_ge(res_in, 16)
            nc.vector.tensor_scalar(alog[:, :].rearrange("p (i g) -> p i g", g=NG),
                                    reside[:, :].rearrange("p (i g) -> p i g", g=RES)[:, :, 0:NG],
                                    LOG_MOST, None, ALU.min).then_inc(a_capped, 1)
            dve.wait_ge(a_exp, 1)
            nc.vector.tensor_scalar(neg_a[:, :], alog[:, :], -1.0, None, ALU.mult).then_inc(a_neg, 1)

            g = tiles(tok, D + 1)[:, :, D]
            dve.wait_ge(gathered, 16 * NC)
            nc.vector.tensor_scalar(stat(6), g, GATE_L, 2.0 ** 23, ALU.mult, ALU.min).then_inc(hard_step, 1)
            dve.wait_ge(hard_step, 1)
            nc.vector.tensor_scalar(stat(6), stat(6), -2.0 ** 23, None, ALU.max).then_inc(hard_step, 1)
            dve.wait_ge(hard_step, 2)
            nc.vector.tensor_copy(whole_i[:, :], stat(6)).then_inc(hard_step, 1)
            dve.wait_ge(hard_step, 3)
            nc.vector.tensor_copy(stat(7), whole_i[:, :]).then_inc(hard_step, 1)
            dve.wait_ge(hard_step, 4)
            nc.vector.tensor_tensor(stat(6), stat(6), stat(7), ALU.subtract).then_inc(hard_step, 1)
            dve.wait_ge(hard_step, 5)
            nc.vector.scalar_tensor_tensor(stat(7), stat(6), 0.0, stat(6), ALU.is_lt, ALU.add).then_inc(hard_step, 1)
            dve.wait_ge(hard_step, 6)
            dve.wait_ge(tanh_done, 1)
            nc.vector.scalar_tensor_tensor(stat(8), stat(7), 1.0 / GATE_L, stat(3), ALU.mult, ALU.mult) \
                .then_inc(hard_step, 1)
            dve.wait_ge(cst_in, 16)
            nc.vector.tensor_tensor(tiles(work_a), cst[:, IOTA:IOTA + D].unsqueeze(1).to_broadcast([P, NC, D]),
                                    spread(g), ALU.is_lt).then_inc(hard_step, 1)
            dve.wait_ge(hard_step, 8)
            nc.vector.tensor_tensor(tiles(work_b), tiles(work_a), spread(stat(8)), ALU.add).then_inc(hard_step, 1)
            dve.wait_ge(hard_step, 9)
            nc.vector.tensor_tensor(tiles(h[:, :]), tiles(tok, D + 1)[:, :, 0:D], tiles(work_b), ALU.mult) \
                .then_inc(h_done, 1)
            dve.wait_ge(h_done, 1)
            norm(0, h[:, :], work_a, work_b, hn[:, :])
            dve.wait_ge(ln_step, 5)
            norm(1, hn[:, :], work_a, work_b, work_b)

            dve.wait_ge(row_in, 16)
            dve.wait_ge(x2_made, 2)
            for q in range(2):
                nc.vector.tensor_tensor(tiles(halves(x2)[q]), tiles(bank[q][:, :]), row_of(R_B2, J), ALU.add) \
                    .then_inc(x2_kept, 1)
            for q in range(4):
                dve.wait_ge(conv_made, q + 1)
                nc.vector.tensor_scalar(xs[0:D, q * H:(q + 1) * H], bank[2 + q][0:D, :], mix[0:D, HB:HB + 1], None,
                                        ALU.add).then_inc(x_ready, 1)
            for b in range(NB):
                dve.wait_ge(x_ready, 2 * b + 2)
                nc.vector.tensor_copy(xs[0:D, (NB + b) * T:(NB + b + 1) * T],
                                      xs[0:D, b * T:(b + 1) * T][:, ::-1]).then_inc(x_ready, 2)

            def prepare(unit, s):
                i, b = unit
                w = unit_no(unit)
                if s == 6 and b == 0:
                    dve.wait_ge(w_in, 16 * i + 16)
                    nc.vector.scalar_tensor_tensor(
                        w_xi[:, :].rearrange("p (a d) -> p a d", a=2),
                        wraw[:, WX:WX + DI].unsqueeze(1).to_broadcast([P, 2, DI]), wraw[:, RMS:RMS + 1],
                        wraw[:, CW:CW + 2 * DI].rearrange("p (a d) -> p a d", a=2), ALU.mult, ALU.mult)
                    nc.vector.tensor_scalar(w_z[:, :], wraw[0:D, WZ:WZ + DI], wraw[0:D, RMS:RMS + 1], None,
                                            ALU.mult).then_inc(w_scaled, 1)
                if s in (22, 26):
                    k = (s - 22) // 4
                    dve.wait_ge(hi_made, 2 * w + k + 1)
                    if k or not (isinstance(i, int) and w == 0):
                        dve.wait_ge(lo_moved, 64 * w + 32 * k)
                    nc.vector.tensor_tensor(lo[:, :], uu if k else dl, hi[:, :].bitcast(F32), ALU.subtract) \
                        .then_inc(lo_made, 1)

            def finish(unit, half):
                i, b = unit
                cols = slice(half * H, (half + 1) * H)
                n = 2 * unit_no(unit) + half
                dve.wait_ge(hc_summed, step_no(unit, NG * (half + 1)))
                nc.vector.scalar_tensor_tensor(yz[half], xi[b][:, cols],
                                               reside[:, bass.ds(i * RES + NG, 1)], y_bank[half][:, :],
                                               ALU.mult, ALU.add).then_inc(yd_done, 1)
                dve.wait_ge(yd_done, n + 1)
                nc.vector.tensor_tensor(yz[half], yz[half], sz[b][:, cols], ALU.mult).then_inc(yz_done, 1)

            def add_out(unit, half):
                i, b = unit
                dve.wait_ge(out_mm, 2 * unit_no(unit) + half + 1)
                nc.vector.tensor_tensor(xs[0:D, bass.ds(x_at(i, b) + half * H, H)],
                                        xs[0:D, bass.ds(x_at(i, b) + half * H, H)], y_bank[half][0:D, :],
                                        ALU.add).then_inc(x_ready, 1)

            def scan(unit, t):
                half, k = divmod(t, NG)
                n = step_no(unit, t)
                if not (isinstance(n, int) and n < H_RING):
                    dve.wait_ge(hc_done, n + 1 - H_RING)
                if half == 1:
                    initial = last_h[:, k:k + 1]
                    dve.wait_ge(last_saved, 4 * unit_no(unit) + k // 4 + 1)
                else:
                    initial = 0.0
                dve.wait_ge(bx_done, n + 1)
                dve.wait_ge(dta_ready, n + 1)
                nc.vector.tensor_tensor_scan(hst[t % H_RING], dta[t % DTA_RING], u_bank[t % U_RING][:, :], initial,
                                             ALU.mult, ALU.add).then_inc(scan_done, 1)

            def slot(cur, prev, nxt, s):
                if s < 0:
                    return
                if cur is not None:
                    n = step_no(cur, s)
                    half = s // NG
                    dve.wait_ge(u_mm, n + 1)
                    nc.vector.tensor_tensor(u_bank[s % U_RING][:, :], u_bank[s % U_RING][:, :],
                                            brep[cur[1]][:, half * H:(half + 1) * H], ALU.mult).then_inc(bx_done, 1)
                if s >= 1 and cur is not None:
                    scan(cur, s - 1)
                if 5 <= s <= NG + 1 and s % 4 == 1 and cur is not None:
                    k = s - 5
                    dve.wait_ge(scan_done, step_no(cur, k + 4))
                    nc.vector.tensor_copy(
                        last_h[:, k:k + 4],
                        hst_all.rearrange("p (k t) -> p k t", t=H)[:, k % H_RING:k % H_RING + 4, H - 1]) \
                        .then_inc(last_saved, 1)
                if s == 0 and prev is not None:
                    scan(prev, STEPS - 1)
                if s == 20 and cur is not None:
                    finish(cur, 0)
                if s == 22 and cur is not None:
                    add_out(cur, 0)
                if s == 4 and prev is not None:
                    finish(prev, 1)
                if s == 6 and prev is not None:
                    add_out(prev, 1)

            run_slots(dve.Fori, slot, prepare)

            dve.wait_ge(x_ready, x_no(BLOCKS + 1, 1, 1))
            for b in range(NB):
                nc.vector.tensor_copy(xcat[D:2 * D, b * T:(b + 1) * T],
                                      xs[0:D, x_at(1, b):x_at(1, b) + T][:, ::-1]) \
                    .then_inc(cat_done, 1)
            for q in range(2):
                dve.wait_ge(down_made, q + 1)
                last = nc.vector.tensor_tensor(tiles(halves(work_b)[q]), tiles(bank[q][:, :]), row_of(R_DOWNB, J),
                                               ALU.add).then_inc(down_step, 1)
            dve.wait_ge(down_step, 2)
            norm(2, work_b, work_a, work_b, work_b)
            dve.wait_ge(ln_step, 15)
            nc.vector.tensor_tensor(tiles(work_a), tiles(work_b), row_of(R_LNG), ALU.mult).then_inc(down_step, 1)
            dve.wait_ge(down_step, 3)
            nc.vector.tensor_tensor(tiles(work_b), tiles(work_a), row_of(R_LNB), ALU.add).then_inc(down_step, 1)
            dve.wait_ge(down_step, 4)
            nc.vector.tensor_tensor(work_a, work_b, x2[:, :], ALU.mult).then_inc(down_step, 1)
            nc.vector.tensor_tensor(tiles(hn[:, :]), tiles(hn[:, :]), row_of(R_B3), ALU.add).then_inc(down_step, 1)
            dve.wait_ge(down_step, 6)
            nc.vector.tensor_tensor(h[:, :], h[:, :], hn[:, :], ALU.add).then_inc(down_step, 1)
            dve.wait_ge(down_step, 7)
            for q in range(2):
                dve.wait_ge(y3_made, q + 1)
                nc.vector.tensor_tensor(halves(h)[q], halves(h)[q], bank[4 + q][:, :], ALU.add).then_inc(down_step, 1)
            dve.wait_ge(down_step, 9)
            norm(3, h[:, :], x3, ffn_a, x3)

            for q in range(4):
                dve.wait_ge(x3_high, q + 1)
                nc.vector.tensor_tensor(x_stack[D:2 * D, q * H:(q + 1) * H], bank[q][0:D, :],
                                        x_stack[0:D, q * H:(q + 1) * H].bitcast(F32), ALU.subtract).then_inc(x3_low, 1)
            for q in range(2):
                dve.wait_ge(gate_made, q + 1)
                nc.vector.tensor_copy(halves(ffn_b)[q], bank[4 + q][:, :]).then_inc(gate_step, 1)
            dve.wait_ge(gate_step, 2)
            for c in range(NC):
                last = nc.vector.max(top8[:, 8 * c:8 * c + 8], ffn_b[:, c * D:(c + 1) * D])
            last.then_inc(top_done, 1)
            dve.wait_ge(top_done, 1)
            top_v = top8[:, :].rearrange("p (c k) -> p c k", k=8)
            nc.vector.tensor_tensor(tiles(ffn_a), gate_v, top_v[:, :, 0:1].to_broadcast([P, NC, D]), ALU.subtract) \
                .then_inc(gate_step, 1)
            dve.wait_ge(gate_step, 3)
            nc.vector.memset(top_v[:, :, TOPK:8], BIG).then_inc(gate_step, 1)
            dve.wait_ge(gate_step, 4)
            for c in range(NC):
                last = nc.vector.match_replace(rest_of_gate[:, c * D:(c + 1) * D], top8[:, 8 * c:8 * c + 8],
                                               ffn_b[:, c * D:(c + 1) * D], -BIG)
            last.then_inc(gate_step, 1)
            dve.wait_ge(gate_step, 5)
            nc.vector.tensor_tensor(chosen, rest_of_gate, ffn_b, ALU.not_equal).then_inc(gate_step, 1)
            dve.wait_ge(gate_step, 6)
            dve.wait_ge(gate_exp, 1)
            nc.vector.tensor_tensor(weighed, chosen, ffn_a, ALU.mult).then_inc(gate_step, 1)
            dve.wait_ge(gate_step, 7)
            nc.vector.tensor_reduce(stat(9), tiles(weighed), AX_X, ALU.add).then_inc(gate_step, 1)
            dve.wait_ge(gate_step, 8)
            nc.vector.reciprocal(stat(10), stat(9)).then_inc(gate_step, 1)
            dve.wait_ge(gate_step, 9)
            nc.vector.tensor_tensor(gate_v, tiles(weighed), spread(stat(10)), ALU.mult).then_inc(gate_step, 1)
            for q in range(4):
                dve.wait_ge(gate_high, q + 1)
                nc.vector.tensor_tensor(gate_stack[D:2 * D, q * H:(q + 1) * H], bank[q][0:D, :],
                                        gate_stack[0:D, q * H:(q + 1) * H].bitcast(F32), ALU.subtract) \
                    .then_inc(gate_low, 1)
            for r in REP_DVE:
                dve.wait_ge(rep_made, r + 1)
                nc.vector.tensor_copy(rep_dst(r), bank[r % REP_BANKS][:, :]).then_inc(rep_dve, 1)
            for n in dve_z:
                spread_ready(dve, n)
                if n >= ZRING:
                    dve.wait_ge(z_used, n + 1 - ZRING)
                nc.vector.tensor_tensor(zring[n % ZRING], *factors(n), ALU.mult).then_inc(z_dve, 1)
            dve.wait_ge(z_used, NZ)
            nc.vector.tensor_copy(lat_t[:, H:2 * H], bank[7][:, :]).then_inc(lat_dve, 1)
            nc.vector.tensor_tensor(x3_v, x3_v, row_of(R_OUTB), ALU.add).then_inc(end_step, 1)
            dve.wait_ge(end_step, 1)
            for q in range(4):
                cols = slice(q * HALF // 2, (q + 1) * HALF // 2)
                dve.wait_ge(proj_made, q + 1)
                nc.vector.tensor_tensor(ffn_b[:, cols], x3[:, cols], bank[2 + q][:, 0:HALF // 2], ALU.add) \
                    .then_inc(end_step, 1)
            dve.wait_ge(end_step, 5)
            norm(4, ffn_b, ffn_a, ffn_b, x3)
            dve.wait_ge(ln_step, 25)
            nc.vector.tensor_tensor(tiles(ffn_b), x3_v, row_of(R_FG), ALU.mult).then_inc(end_step, 1)
            dve.wait_ge(end_step, 6)
            nc.vector.tensor_tensor(tiles(x3), tiles(ffn_b), row_of(R_FB), ALU.add).then_inc(end_step, 1)
            dve.wait_ge(end_step, 7)
            nc.vector.tensor_tensor(ffn_a, x3, h[:, :], ALU.add).then_inc(out_ready, 1)

        @block.tensor
        def _(pe):
            ident = cst[:, IDN:IDN + P]

            def turn(src, q, made):
                for m in range(4):
                    c = 4 * q + m
                    last = nc.tensor.transpose(bank[q][0:D, m * P:(m + 1) * P], src[:, c * D:(c + 1) * D], ident)
                last.then_inc(made, 1)

            pe.wait_ge(cst_in, 16)
            pe.wait_ge(sel_done, 1)
            pe.wait_ge(ln_step, 10)
            for q in range(4):
                turn(work_b, q, xl_turned)
            pe.wait_ge(mix_in, 16)
            for q in range(4):
                pe.wait_ge(xl_kept, q + 1)
                nc.tensor.matmul(bank[4 + q][0:D, :], mix[0:D, W1:W1 + D], feat_t[0:D, q * H:(q + 1) * H],
                                 start=True, stop=True).then_inc(x1_made, 1)
            for q in range(2):
                for m in range(J):
                    c = J * q + m
                    last = nc.tensor.matmul(bank[q][:, m * D:(m + 1) * D], feat_t[0:D, c * P:(c + 1) * P],
                                            mix[0:D, W2:W2 + D], start=True, stop=True)
                last.then_inc(x2_made, 1)
            pe.wait_ge(x1_kept, 4)
            pe.wait_ge(x1_zero, 1)
            for q in range(4):
                b, half = divmod(q, 2)
                for k in range(3):
                    first = b * (T + 2) + half * H + k
                    last = nc.tensor.matmul(bank[2 + q][0:D, :], mix[0:D, HCONV + k * D:HCONV + (k + 1) * D],
                                            x1p[0:D, first:first + H], start=(k == 0), stop=(k == 2))
                last.then_inc(conv_made, 1)

            def product(unit, k, dst, lhs, rhs, more=None, back=2):
                n = prep_no(unit, k)
                if not (isinstance(n, int) and n <= back):
                    pe.wait_ge(prep_read, n - back)
                if more is None:
                    nc.tensor.matmul(dst, lhs, rhs, start=True, stop=True).then_inc(prep_mm, 1)
                else:
                    nc.tensor.matmul(dst, lhs, rhs, start=True, stop=False)
                    nc.tensor.matmul(dst, more[0], more[1], start=False, stop=True).then_inc(prep_mm, 1)

            def prepare(unit, s):
                i, b = unit
                w = unit_no(unit)
                if s == 1 and b == 0:
                    if isinstance(i, int) and w == 0:
                        pe.wait_ge(x_ready, 8)
                    pe.wait_ge(w_in, 16 * i + 16)
                    product(unit, K_DT, y_bank[0][:, 0:DI], wraw[0:RANK, X4:X4 + DI], wraw[0:RANK, DTW:DTW + DI],
                            back=1)
                if s in (2, 3):
                    half = s - 2
                    pe.wait_ge(x_squared, w + 1)
                    product(unit, K_MS + half, (p_bank, y_bank[0])[half][:, :], cst[0:D, ONE:ONE + P],
                            scr_a[0:D, half * H:(half + 1) * H], back=1 if b and half == 0 else 2)
                alt = (p_bank, y_bank[1])
                if s in (8, 9):
                    half = s - 8
                    o = half * H
                    if half == 0:
                        if b == 0:
                            pe.wait_ge(w_scaled, i + 1)
                        pe.wait_ge(xn_ready, w + 1)
                        pe.wait_ge(shifted, 16 * w + 16)
                    else:
                        pe.wait_ge(x_ready, x_no(i + 1, b, 1))
                    product(unit, K_XI + half, alt[half][:, :], w_xi[:, 0:DI], xn2[:, o:o + H],
                            (w_xi[:, DI:2 * DI], xn2[:, o + 2:o + 2 + H]))
                if s == 11:
                    for half in range(2):
                        o = half * H + 3
                        product(unit, K_Z + half, alt[half][:, :], w_z[:, :], xn2[0:D, o:o + H])
                if s in (12, 13):
                    half = s - 12
                    o = half * H
                    product(unit, K_DP + half, alt[half][:, :], w_dt[:, :], xi[b][:, o:o + H])
                if s in (23, 25):
                    half = (s - 23) // 2
                    o = half * H
                    product(unit, K_BC + 2 * half, p_bank[:, :], wraw[:, XB:XB + P], xi[b][:, o:o + H])
                    if half == 0 and not (isinstance(i, int) and w == 0):
                        last = (i, 0) if b else (i - 1, 1)
                        pe.wait_ge(x_ready, x_no(last[0] + 2, last[1], 0))
                    product(unit, K_BC + 2 * half + 1, y_bank[0][:, :], wraw[:, XC:XC + P], xi[b][:, o:o + H])

            def spread_step(unit, which, t, dst):
                half, k = divmod(t, NG)
                side, g = divmod(group_of(k), NG // 2)
                first = (2 * which + side) * T + half * H
                return nc.tensor.matmul(dst[:, :], sel[:, SEL + g * P:SEL + (g + 1) * P],
                                        stack[unit[1]][:, first:first + H], start=True, stop=True)

            def sum_states(unit, t0):
                half, k0 = divmod(t0, NG)
                n = step_no(unit, t0 + 3)
                pe.wait_ge(hc_done, n + 1)
                if k0 == 0:
                    if not (isinstance(unit[0], int) and unit_no(unit) == 0):
                        last = (unit[0], 0) if unit[1] else (unit[0] - 1, 1)
                        pe.wait_ge(x_ready, x_no(last[0] + 2, last[1], half))
                    if isinstance(unit[0], int) and unit == (BLOCKS - 1, 1):
                        pe.wait_ge(prep_read, prep_no(unit, K_BC + 3))
                    else:
                        nxt = (unit[0] + 1, 0) if unit[1] else (unit[0], 1)
                        pe.wait_ge(prep_read, prep_no(nxt, K_DP + 1 if half else K_MS + 1))
                for k in range(k0, k0 + 4):
                    q, m = divmod(group_of(k), 4)
                    last = nc.tensor.matmul(y_bank[half][32 * q:32 * q + 32, :],
                                            cst[:, SUM + m * 32:SUM + (m + 1) * 32], hcr[(t0 + k - k0) % HC_RING],
                                            start=(k0 == 0), stop=(k0 == NG - 4), tile_position=(0, 32 * q))
                last.then_inc(hc_summed, 4)

            def out_product(unit, half):
                pe.wait_ge(yz_done, 2 * unit_no(unit) + half + 1)
                if unit[1] == 0 and half == 0:
                    pe.wait_ge(outw_in, 16 * unit[0] + 16)
                nc.tensor.matmul(y_bank[half][0:D, :], out_w[:, :], yz[half], start=True, stop=True) \
                    .then_inc(out_mm, 1)

            def slot(cur, prev, nxt, s):
                unit, t = (cur, s + AHEAD) if s + AHEAD < STEPS else (nxt, s + AHEAD - STEPS)
                if unit is not None:
                    n = step_no(unit, t)
                    if t == 0:
                        pe.wait_ge(hi_moved, 64 * unit_no(unit) + 32)
                        pe.wait_ge(lo_moved, 64 * unit_no(unit) + 32)
                    if not (isinstance(n, int) and n < DA_RING):
                        pe.wait_ge(dta_ready, n + 1 - DA_RING)
                    spread_step(unit, 0, t, da_bank[t % DA_RING]).then_inc(da_mm, 1)
                unit, t = (cur, s + 1) if s + 1 < STEPS else (nxt, 0)
                if unit is not None and s + 1 >= 0:
                    n = step_no(unit, t)
                    if t == 0:
                        pe.wait_ge(hi_moved, 64 * unit_no(unit) + 64)
                        pe.wait_ge(lo_moved, 64 * unit_no(unit) + 64)
                    back = U_RING if t >= U_RING else t + STEPS - (STEPS - 1 - (STEPS - 1 - t) % U_RING)
                    if not (isinstance(n, int) and n < U_RING):
                        pe.wait_ge(scan_done, n + 1 - back)
                    spread_step(unit, 1, t, u_bank[t % U_RING]).then_inc(u_mm, 1)
                if s >= 6 and s % 4 == 2 and cur is not None:
                    sum_states(cur, s - 6)
                if s == 2 and prev is not None:
                    sum_states(prev, STEPS - 4)
                if s == 21 and cur is not None:
                    out_product(cur, 0)
                if s == 5 and prev is not None:
                    out_product(prev, 1)

            run_slots(pe.Fori, slot, prepare)

            pe.wait_ge(cat_done, 4)
            xcat_v = xcat.rearrange("p (b t j) -> p b j t", b=NB, j=J)
            for q in range(2):
                for m in range(J):
                    last = nc.tensor.matmul(bank[q][:, m * D:(m + 1) * D], xcat_v[:, q, m, :],
                                            mix[:, DOWN:DOWN + D], start=True, stop=True)
                last.then_inc(down_made, 1)
            pe.wait_ge(down_step, 5)
            for q in range(4):
                turn(work_a, q, q_turned)
            for q in range(2):
                pe.wait_ge(q_kept, 2 * q + 2)
                for m in range(J):
                    c = J * q + m
                    last = nc.tensor.matmul(bank[4 + q][:, m * D:(m + 1) * D], feat_t[0:D, c * P:(c + 1) * P],
                                            mix[0:D, W3:W3 + D], start=True, stop=True)
                last.then_inc(y3_made, 1)
            pe.wait_ge(ln_step, 20)
            for q in range(4):
                turn(x3, q, x3_turned)
            for q in range(2):
                pe.wait_ge(x3_kept, 2 * q + 2)
                for m in range(J):
                    c = J * q + m
                    last = nc.tensor.matmul(bank[4 + q][:, m * D:(m + 1) * D], x3_t[0:D, c * P:(c + 1) * P],
                                            mix[0:D, GATEW:GATEW + D], start=True, stop=True)
                last.then_inc(gate_made, 1)
            pe.wait_ge(gate_step, 10)
            pe.wait_ge(x3_low, 4)
            for q in range(4):
                turn(ffn_b, q, gate_turned)
            pe.wait_ge(gate_low, 4)
            for r in range(NREP):
                part, q = REP_ORDER[r]
                if r >= REP_BANKS:
                    spread_until(pe, r + 1 - REP_BANKS)
                if part < NE:
                    first, src = SELE + part * P, gate_stack
                else:
                    first, src = SEL + (part - NE) * P, x_stack
                nc.tensor.matmul(bank[r % REP_BANKS][:, :], sel[:, first:first + P], src[:, q * H:(q + 1) * H],
                                 start=True, stop=True).then_inc(rep_made, 1)
            pe.wait_ge(lat_in, 16)
            for m in range(NZ):
                b, n = divmod(m, NE * ND)
                if m in pool_z:
                    pe.wait_ge(z_pool, pool_z.index(m) + 1)
                else:
                    pe.wait_ge(z_dve, dve_z.index(m) + 1)
                for half in range(2):
                    last = nc.tensor.matmul(bank[6 + b][half * D:(half + 1) * D, :], lat[:, n * D:(n + 1) * D],
                                            zring[m % ZRING][:, half * H:(half + 1) * H],
                                            start=(n == 0), stop=(n == NE * ND - 1), tile_position=(0, half * D))
                last.then_inc(z_used, 1)
            pe.wait_ge(lat_act, 1)
            pe.wait_ge(lat_dve, 1)
            for q in range(4):
                b, half = divmod(q, 2)
                r_ = slice(half * D, (half + 1) * D)
                for m in range(4):
                    first = b * H + m * P
                    last = nc.tensor.matmul(bank[2 + q][:, m * D:(m + 1) * D], lat_t[r_, first:first + P],
                                            mix[r_, OUTW:OUTW + D], start=True, stop=True)
                last.then_inc(proj_made, 1)


def _block_weights(np, w, l):
    inproj, convw, xproj = w["inproj"][l], w["convw"][l], w["xproj"][l]
    pack = np.zeros((P, WPACK), np.float32)
    for a in range(2):
        r = slice(a * D, (a + 1) * D)
        pack[r, WX:WX + DI] = inproj[:DI].T
        pack[r, CW:CW + DI] = convw[:, a]
        pack[r, CW + DI:CW + 2 * DI] = convw[:, 2 + a]
        pack[r, RMS] = w["rms"][l]
    pack[:D, WZ:WZ + DI] = inproj[DI:].T
    pack[:, XB:XB + P] = np.repeat(xproj[RANK:RANK + NS].T, GR, axis=1)
    pack[:, XC:XC + P] = np.repeat(xproj[RANK + NS:].T, GR, axis=1)
    pack[:RANK, X4:X4 + DI] = xproj[:RANK]
    pack[:RANK, DTW:DTW + DI] = w["dtw"][l].T
    pack[:, CONVB], pack[:, DTB] = w["convb"][l], w["dtb"][l]
    res = np.zeros((P, RES), np.float32)
    res[:, :NG] = w["Alog"][l].reshape(NG, GR, NS).transpose(2, 1, 0).reshape(P, NG)
    res[:, NG] = w["D"][l]
    return pack, w["outw"][l].T, res


def kernel(**inputs):
    import numpy as np
    import concourse.bacc as bacc
    from concourse.bass_utils import run_bass_kernel_spmd as run

    a = {k: np.asarray(v) for k, v in inputs.items()}
    parts = []
    for l in range(2):
        for d in "fb":
            pre = f"L0_attn_{d}_"
            parts.append(_block_weights(np, {k[len(pre):]: v for k, v in a.items() if k.startswith(pre)}, l))
    consts = np.zeros((P, CPACK), np.float32)
    consts[:, IDN:IDN + P] = np.eye(P)
    spack = np.zeros((P, SPACK), np.float32)
    for r in range(P):
        for k in range(4):
            consts[r, SUM + k * 32 + k * GR + r % GR] = 1.0
        g, d = divmod(r % D, GR)
        spack[r, SEL + g * P + d:SEL + (g + 1) * P:GR] = 1.0
        k, e = divmod(r % D, ES)
        spack[r, SELE + k * P + e * DS:SELE + k * P + (e + 1) * DS] = 1.0
    consts[:, ONE:ONE + P] = 1.0 / D
    consts[:, IOTA:IOTA + D] = np.arange(D)
    consts[:, CEPS], consts[:, C1] = EPS, 1.0
    mp = np.zeros((P, MPACK), np.float32)
    t = "L0_attn_"
    mp[:D, W1:W1 + D], mp[:D, W2:W2 + D], mp[:D, W3:W3 + D] = a[t + "w1"].T, a[t + "w2"].T, a[t + "w3"].T
    mp[:, DOWN:DOWN + D] = a[t + "down_w"].T
    mp[:D, GATEW:GATEW + E] = a["L0_ffn_gate_w"].T
    mp[:D, OUTW:OUTW + D] = mp[D:, OUTW:OUTW + D] = a["L0_ffn_out_w"].T
    for k in range(3):
        mp[:D, HCONV + k * D:HCONV + (k + 1) * D] = a[t + "hconv_w"][:, :, k].T
    mp[:D, LNG], mp[:D, LNB], mp[:D, B1], mp[:D, HB] = a[t + "ln_g"], a[t + "ln_b"], a[t + "b1"], a[t + "hconv_b"]
    rows = np.concatenate([a[t + "b2"], a[t + "down_b"], a[t + "ln_g"], a[t + "ln_b"], a[t + "b3"],
                           a["L0_ffn_out_b"], a["L0_ffn_ln_g"], a["L0_ffn_ln_b"]])
    arrays = {
        "ids": np.ascontiguousarray(a["x"]),
        "table": np.concatenate([a["L0_tok_embedding"], a["L0_tok_gates"][:, None]], axis=1),
        "wpack": np.concatenate([p[0] for p in parts]),
        "outw": np.ascontiguousarray(np.concatenate([p[1] for p in parts])),
        "res": np.concatenate([p[2] for p in parts], axis=1),
        "consts": consts,
        "spack": spack,
        "mpack": mp,
        "rows": np.ascontiguousarray(np.broadcast_to(rows[None], (P, 8 * D))),
        "lattice": np.ascontiguousarray(a["L0_ffn_lattice_weights"].reshape(NE, ES, ND, DS, D)
                                        .transpose(1, 3, 0, 2, 4).reshape(P, NE * ND * D)),
    }
    nc = bacc.Bacc("TRN2", target_bir_lowering=False, num_devices=1)
    aps = [nc.dram_tensor("in_" + k, v.shape, mybir.dt.from_np(v.dtype), kind="ExternalInput").ap()
           for k, v in arrays.items()]
    out = nc.dram_tensor("out_0", (NB, T, D), F32, kind="ExternalOutput").ap()
    tower_kernel(nc, *aps, out)
    r = run(nc, [{"in_" + k: v for k, v in arrays.items()}], core_ids=[0])
    return r.results[0]["out_0"]
```

```python
from contextlib import ExitStack

import concourse.bass as bass
from concourse import mybir

F32 = mybir.dt.float32
F32R = mybir.dt.float32r
I32 = mybir.dt.int32
U32 = mybir.dt.uint32
ALU = mybir.AluOpType
ACT = mybir.ActivationFunctionType
AX_X = mybir.AxisListType.X

P = 128
V, D = 32000, 64
NB, T = 2, 1024
J = T // P
NC = NB * J
HALF = NC // 2 * D
DI, NS, TAPS, RANK = 128, 16, 4, 4
GR = P // NS
NG = DI // GR
H = 512
BLOCKS = 4
STEPS = 2 * NG
E, TOPK = 64, 6
ES, DS = 16, 8
NE, ND = E // ES, D // DS
NZ = NB * NE * ND
EPS = 1e-5
GATE_L = 1e9
BIG = 3.0e38
LOG_MOST = 80.0

WX, WZ, CW, XB, XC, X4, DTW = 0, 128, 256, 512, 640, 768, 896
RMS, CONVB, DTB, WPACK = 1024, 1025, 1026, 1027
RES = NG + 1
IDN, SUM, ONE, IOTA, CEPS, C1, CPACK = 0, 128, 256, 384, 448, 449, 450
SEL, SELE, SPACK = 0, 1024, 1536
W1, W2, W3, DOWN, GATEW, OUTW, HCONV = 0, 64, 128, 192, 256, 320, 384
LNG, LNB, B1, HB, MPACK = 576, 577, 578, 579, 580
R_B2, R_DOWNB, R_LNG, R_LNB, R_B3, R_OUTB, R_FG, R_FB = range(8)

DA_RING, U_RING, DTA_RING, HC_RING, H_RING = 2, 3, 8, 8, 8
AHEAD = 4
LEAD = {5: 1, 6: 2, 7: 2, 8: 1, 15: 1, 16: 2, 17: 2, 18: 1}
CUT = 9
CLOSE = 7
PER_BLOCK = 25
ARENA = 34000
ZRING = 6
END = 12
K_XI, K_Z, K_DT, K_DP, K_MS, K_BC = range(6)


def group_of(k):
    return (k % 4) * 4 + k // 4


def step_no(unit, s):
    return 2 * STEPS * unit[0] + STEPS * unit[1] + s


def unit_no(unit):
    return 2 * unit[0] + unit[1]


def prep_no(unit, kind, k=0):
    i, b = unit
    if kind == K_MS:
        if isinstance(i, int) and unit == (0, 0):
            return k + 1
        i, b = (i, 0) if b else (i - 1, 1)
    first = 0 if b else 1
    at = {K_XI: 2 * k, K_Z: 2 * k + 1, K_DT: 4, K_DP: 4 + first + k, K_MS: 6 + first + k,
          K_BC: 8 + first + k}[kind]
    if isinstance(i, int) and (i, b) == (BLOCKS - 1, 1) and kind == K_BC:
        at -= 2
    return 2 + PER_BLOCK * i + 13 * b + at + 1


def x_at(i, b):
    return (NB * (i % 2) + b) * T


def x_no(slot, b, half):
    return 4 * slot + 2 * b + half + 1


def factor_steps(cur, nxt, s):
    def until(x):
        return x + AHEAD + LEAD.get(x, 0)
    first = until(s - 1) + 1 if s > -AHEAD else 0
    return [(u, t % STEPS) for t in range(first, until(s) + 1) for u in ((cur if t < STEPS else nxt),) if u is not None]


def run_slots(loop, slot, prepare, normalise, close):
    for s in range(CUT, STEPS):
        normalise((0, 0), s)
    for s in range(STEPS):
        prepare((0, 0), s)
        if s >= CUT:
            normalise((0, 1), s)
    for s in range(-AHEAD, CUT):
        slot((0, 0), None, (0, 1), s)
        if s >= 0:
            prepare((0, 1), s)

    def rest_of_block(i, last):
        for s in range(CUT, STEPS):
            slot((i, 0), None, (i, 1), s)
            prepare((i, 1), s)
            if not last:
                normalise((i + 1, 0), s)
        for s in range(STEPS):
            slot((i, 1), (i, 0), None if last else (i + 1, 0), s)
            if not last:
                prepare((i + 1, 0), s)
                if s >= CUT:
                    normalise((i + 1, 1), s)
            elif s >= CLOSE:
                close(0, s - CLOSE)
        for s in range(CUT):
            slot(None if last else (i + 1, 0), (i, 1), None if last else (i + 1, 1), s)
            if not last:
                prepare((i + 1, 1), s)
            else:
                close(0, s + STEPS - CLOSE)

    with loop(0, BLOCKS - 1) as i:
        rest_of_block(i, False)
    rest_of_block(BLOCKS - 1, True)


def tower_kernel(nc, ids, table, wpack, outw, res, consts, spack, mpack, rows, lattice, out):
    with ExitStack() as ctx:
        def sb(name, shape, dt=F32):
            return ctx.enter_context(nc.sbuf_tensor(name, shape, dt))

        def sem(name):
            return ctx.enter_context(nc.semaphore(name))

        stack = [sb(f"stack{b}", [P, 4 * T], F32R) for b in range(NB)]
        hi, lo = sb("hi", [P, T], F32R), sb("lo", [P, T], F32R)
        sel = sb("sel", [P, SPACK], F32R)

        bank = [ctx.enter_context(nc.psum_tensor(f"bank{i}", [P, H], F32)) for i in range(8)]
        da_bank, u_bank, y_bank, p_bank = bank[0:2], bank[2:5], bank[5:7], bank[7]

        cst = sb("cst", [P, CPACK])
        mix = sb("mix", [P, MPACK])
        row = sb("row", [P, 8 * D])
        reside = sb("reside", [P, BLOCKS * RES])
        alog = sb("alog", [P, BLOCKS * NG])
        neg_a = sb("neg_a", [P, BLOCKS * NG])
        last_h = sb("last_h", [P, NG])
        a_cur, a_next = sb("a_cur", [P, NG]), sb("a_next", [P, NG])
        wraw = sb("wraw", [P, WPACK])
        out_w = sb("out_w", [P, D])
        w_xi = sb("w_xi", [P, 2 * DI])
        w_z = sb("w_z", [D, DI])
        w_dt = sb("w_dt", [P, DI])
        h = sb("h", [P, NC * D])
        hn = sb("hn", [P, NC * D])
        x2 = sb("x2", [P, NC * D])
        idx_i = sb("idx_i", [P, NC], I32)
        idx_f = sb("idx_f", [P, NC])
        idx_g = sb("idx_g", [P, NC])
        idx_u = sb("idx_u", [P, NC], U32)
        whole_i = sb("whole_i", [P, NC], I32)
        small = sb("small", [P, 12 * NC])
        top8 = sb("top8", [P, NC * 8])

        arena = sb("arena", [P, ARENA])
        place = [0]

        def cut(n):
            place[0] += n
            assert place[0] <= 45600
            return arena[:, place[0] - n:place[0]]

        xs = cut(2 * NB * T)
        after_xs = place[0]
        xn2 = cut(T + 4)
        scr_a, scr_b, scr_c, scr_r = cut(T), cut(T), cut(T), cut(T)
        dl, uu = cut(T), cut(T)
        xi, sz, brep, crep = [cut(T)], [cut(T)], [cut(T)], [cut(T)]
        after_spare = place[0]
        for tensor in (xi, sz, brep, crep):
            tensor.append(cut(T))
        before_steps = place[0]
        hcr = [cut(H) for _ in range(HC_RING)]
        yz = [cut(H) for _ in range(2)]
        dta = [cut(H) for _ in range(DTA_RING)]
        hst_all = cut(H_RING * H)
        hst = [hst_all[:, k * H:(k + 1) * H] for k in range(H_RING)]
        place[0] = before_steps
        work_a, work_b, feat_t, x1p = cut(T), cut(T), cut(NB * T), cut(NB * (T + 2))
        tok = cut(NC * (D + 1))
        sel_raw = cut(SPACK)
        place[0] = after_xs
        lat = cut(NE * ND * D)
        c_cat, c_feat = [cut(T) for _ in range(NB)], [cut(T) for _ in range(NB)]
        c_a, c_b, c_rest, c_weighed, c_x = ([cut(J * D) for _ in range(NB)] for _ in range(5))
        assert place[0] <= after_spare
        c_mean = [hn[:, b * J * D:(b + 1) * J * D] for b in range(NB)]
        c_gate = [x2[:, b * J * D:(b + 1) * J * D] for b in range(NB)]
        srep = [xs[:, k * T:(k + 1) * T] for k in range(NE)]
        place[0] = after_spare
        xrep = [cut(T) for _ in range(ND)]
        zring = [cut(T) for _ in range(ZRING)]
        x_stack, gate_stack = stack[0][:, 0:2 * T], stack[0][:, 2 * T:4 * T]

        def tiles(ap, w=D):
            return ap.rearrange("p (c d) -> p c d", d=w)

        def stat(n):
            return small[:, n * NC:(n + 1) * NC]

        def spread(ap, n=D):
            return ap.unsqueeze(2).to_broadcast([P, NC, n])

        def row_of(n, tiles_=NC):
            return row[:, n * D:(n + 1) * D].unsqueeze(1).to_broadcast([P, tiles_, D])

        def stat_of(b, n):
            return small[:, n * NC + b * J:n * NC + (b + 1) * J]

        def of_tile(ap):
            return ap.unsqueeze(2).to_broadcast([P, J, D])

        def halves(ap):
            return [ap[:, 0:HALF], ap[:, HALF:2 * HALF]]

        ids_in, cst_in, mix_in, row_in, res_in, lat_in = (sem(n) for n in (
            "ids_in", "cst_in", "mix_in", "row_in", "res_in", "lat_in"))
        w_in, outw_in, shifted = sem("w_in"), sem("outw_in"), sem("shifted")
        hi_moved, lo_moved = sem("hi_moved"), sem("lo_moved")
        sel_in, sel_done = sem("sel_in"), sem("sel_done")
        idx_step, gathered, hard_step = sem("idx_step"), sem("gathered"), sem("hard_step")
        tanh_done, h_done = sem("tanh_done"), sem("h_done")
        ln_step, ln_square, ln_rstd, ln_log = sem("ln_step"), sem("ln_square"), sem("ln_rstd"), sem("ln_log")
        xl_turned, xl_kept, x1_made, x1_kept = sem("xl_turned"), sem("xl_kept"), sem("x1_made"), sem("x1_kept")
        x1_zero, x2_made, x2_kept, conv_made = sem("x1_zero"), sem("x2_made"), sem("x2_kept"), sem("conv_made")
        a_capped, a_exp, a_neg, a_copied, a_fetched, xn_zero = sem("a_capped"), sem("a_exp"), sem("a_neg"), sem("a_copied"), sem("a_fetched"), sem("xn_zero")
        x_ready, x_squared, r_ready = sem("x_ready"), sem("x_squared"), sem("r_ready")
        xn_ready, w_scaled, xi_ready, z_ready = sem("xn_ready"), sem("w_scaled"), sem("xi_ready"), sem("z_ready")
        prep_mm, prep_read = sem("prep_mm"), sem("prep_read")
        dt_abs, dt_exp, dt_log, dt_made, u_made, hi_made, lo_made = (sem(n) for n in (
            "dt_abs", "dt_exp", "dt_log", "dt_made", "u_made", "hi_made", "lo_made"))
        da_mm, u_mm, dta_ready = sem("da_mm"), sem("u_mm"), sem("dta_ready")
        last_saved = sem("last_saved")
        bx_done, scan_done, hc_done, hc_summed = sem("bx_done"), sem("scan_done"), sem("hc_done"), sem("hc_summed")
        yd_done, yz_done, out_mm = sem("yd_done"), sem("yz_done"), sem("out_mm")
        cat_act, cat_dve, down_made, down_step = sem("cat_act"), sem("cat_dve"), sem("down_made"), sem("down_step")
        q_turned, q_kept, y3_made = sem("q_turned"), sem("q_kept"), sem("y3_made")
        x3_turned, x3_kept, gate_made, gate_step = sem("x3_turned"), sem("x3_kept"), sem("gate_made"), sem("gate_step")
        gate_exp, rep_made, rep_kept = sem("gate_exp"), sem("rep_made"), sem("rep_kept")
        gate_turned, gate_high, gate_low = sem("gate_turned"), sem("gate_high"), sem("gate_low")
        x3_high, x3_low = sem("x3_high"), sem("x3_low")
        z_dve, z_pool, z_used = sem("z_dve"), sem("z_pool"), sem("z_used")
        lat_kept, proj_made, end_step = sem("lat_kept"), sem("proj_made"), sem("end_step")
        top_done, out_ready, stored = sem("top_done"), sem("out_ready"), sem("stored")

        NZB = NZ // NB
        CLOSING = {0: (0, 1), 2: (2, 3), 3: (4, 5), 4: (6, 7), 8: (8, 9), 9: (10, 11), 10: (12,), 11: (13,),
                   13: (14, 15, 17), 15: (18, 19), 19: (20, 21), 20: (22,), 23: (23, 24), 25: (25,), 26: (26, 27),
                   28: (28, 29, 30), 29: (31,), 31: (32,)}
        ENDING = {1: (0, 1), 2: (3,), 4: (4, 5, 6), 6: (7, 8), 10: (9,), 11: (10, 11)}
        FFN_STEPS, dve_z, pool_z = [], [], []
        made = 0
        for step in range(32):
            dve_too = step not in CLOSING or step in (10, 11, 20, 29)
            mine = ([dve_z] if dve_too else []) + ([pool_z] if step * 15 // 32 > (step - 1) * 15 // 32 >= 0 else [])
            mine = mine[:NZB - made]
            for who in mine:
                who.append(made)
                made += 1
            FFN_STEPS.append((range(made - len(mine), made), CLOSING.get(step, ()), ()))
        assert made == NZB
        step = 0
        while made < NZ:
            mine = ([dve_z] + ([pool_z] if step % 5 in (1, 3, 4) else []))[:NZ - made]
            for who in mine:
                who.append(made)
                made += 1
            FFN_STEPS.append((range(made - len(mine), made), (), [(0, k) for k in ENDING.get(step, ())]))
            step += 1
        FFN_STEPS += [((), (), [(1, k)]) for k in range(END)]
        SPREAD_AT = {0: [(0, 0), (0, NE), (0, NE + 1), (0, NE + 2)], 5: [], 6: [(0, 1)], 14: [(0, 2)], 21: [(0, 3)],
                     NZB: [(1, 0), (1, NE + 6), (1, NE + 7), (1, 1)], NZB + 8: [(1, 2)], NZB + 16: [(1, 3)]}
        for k in range(5):
            SPREAD_AT[k + 1] = [(0, NE + k + 3)]
        for k in range(6):
            SPREAD_AT[26 + k] = [(1, NE + k)]
        SPREADS = [part for m in sorted(SPREAD_AT) for part in SPREAD_AT[m]]
        REP_BANKS = 5

        def factors(m):
            b, n = divmod(m, NZB)
            ei, di = divmod(n, ND)
            after = max(SPREADS.index((b, NE + di)), SPREADS.index((b, ei))) + 1
            return xrep[di], srep[ei], 2 * after

        def products_until(eng, m):
            if sum(k < m for k in dve_z):
                eng.wait_ge(z_dve, sum(k < m for k in dve_z))
            if sum(k < m for k in pool_z):
                eng.wait_ge(z_pool, sum(k < m for k in pool_z))

        def second_bank(b, k):
            return bank[5] if b or k > 16 else bank[6]

        block = ctx.enter_context(nc.Block())

        @block.sync
        def _(sp):
            sp.dma_start(idx_i[:, :], ids.rearrange("b (p j) -> p b j", j=J)).then_inc(ids_in, 16)
            sp.dma_start(cst[:, :], consts).then_inc(cst_in, 16)
            sp.dma_start(mix[:, :], mpack).then_inc(mix_in, 16)
            sp.dma_start(row[:, :], rows).then_inc(row_in, 16)
            sp.dma_start(reside[:, :], res).then_inc(res_in, 16)
            sp.dma_start(sel_raw, spack).then_inc(sel_in, 16)
            sp.dma_start(wraw[:, :], wpack[0:P, :]).then_inc(w_in, 16)
            sp.dma_start(out_w[:, :], outw[0:P, :]).then_inc(outw_in, 16)

            def shift(unit):
                sp.wait_ge(xn_ready, unit_no(unit) + 1)
                sp.dma_start(xn2[D:2 * D, 2:2 + T], xn2[0:D, 3:3 + T]).then_inc(shifted, 16)

            def stack_up(unit, which):
                for k, (part, made, moved) in enumerate(((hi, hi_made, hi_moved), (lo, lo_made, lo_moved))):
                    sp.wait_ge(made, 2 * unit_no(unit) + which + 1)
                    for side in range(2):
                        cols = slice((2 * which + side) * T, (2 * which + side + 1) * T)
                        sp.dma_start(stack[unit[1]][k * D:(k + 1) * D, cols].bitcast(F32),
                                     part[side * D:(side + 1) * D, :].bitcast(F32)).then_inc(moved, 16)

            def moves(unit, after):
                stack_up(unit, 0)
                stack_up(unit, 1)
                if after is not None:
                    shift(after)

            shift((0, 0))
            moves((0, 0), (0, 1))
            with sp.Fori(0, BLOCKS - 1) as i:
                moves((i, 1), (i + 1, 0))
                sp.wait_ge(prep_read, prep_no((i, 1), K_BC, 3))
                sp.dma_start(wraw[:, :], wpack[bass.ds(i * P + P, P), :]).then_inc(w_in, 16)
                moves((i + 1, 0), (i + 1, 1))
                sp.wait_ge(out_mm, 4 * i + 4)
                sp.dma_start(out_w[:, :], outw[bass.ds(i * P + P, P), :]).then_inc(outw_in, 16)
            moves((BLOCKS - 1, 1), None)
            sp.wait_ge(lo_moved, 64 * 2 * BLOCKS)
            sp.wait_ge(hi_moved, 64 * 2 * BLOCKS)
            sp.wait_ge(prep_read, prep_no((BLOCKS - 1, 1), K_BC, 3))
            sp.wait_ge(yz_done, 4 * BLOCKS - 2)
            sp.dma_start(lat, lattice).then_inc(lat_in, 16)
            for b in range(NB):
                sp.wait_ge(out_ready, b + 1)
                sp.dma_start(out[b].rearrange("(p j) d -> p (j d)", j=J), c_mean[b]).then_inc(stored, 16)
            sp.wait_ge(stored, 32)

        @block.gpsimd
        def _(pool):
            pool.wait_ge(idx_step, 5)
            for c in range(NC):
                nc.gpsimd.indirect_dma_start(
                    tok[:, c * (D + 1):(c + 1) * (D + 1)], None, table[:, :],
                    bass.IndirectOffsetOnAxis(ap=idx_u[:, c:c + 1], axis=0)).then_inc(gathered, 16)

            def slot(cur, prev, nxt, s):
                unit, t = (cur, s - 1) if s >= 1 else (prev, STEPS - 1)
                if s < 0 or unit is None:
                    return
                b, half = unit[1], t // NG
                n = step_no(unit, t)
                pool.wait_ge(scan_done, n + 1)
                if not (isinstance(n, int) and n < HC_RING):
                    pool.wait_ge(hc_summed, n + 1 - HC_RING)
                nc.gpsimd.tensor_tensor(hcr[t % HC_RING], hst[t % H_RING], crep[b][:, half * H:(half + 1) * H],
                                        ALU.mult).then_inc(hc_done, 1)

            def normalise(unit, s):
                i, b = unit
                w = unit_no(unit)
                if s == 23:
                    pool.wait_ge(r_ready, w + 1)
                    if not isinstance(i, int) or w > 0:
                        last = (i, 0) if b else (i - 1, 1)
                        pool.wait_ge(prep_read, prep_no(last, K_Z, 1))
                    nc.gpsimd.tensor_tensor(xn2[0:D, 3:3 + T], xs[0:D, bass.ds(x_at(i, b), T)],
                                            scr_r[0:D, :], ALU.mult).then_inc(xn_ready, 1)

            def prepare(unit, s):
                b, w = unit[1], unit_no(unit)
                if s == 18:
                    pool.wait_ge(dt_log, w + 1)
                    nc.gpsimd.tensor_tensor(dl, dl, scr_c, ALU.add).then_inc(dt_made, 1)
                if s == 20:
                    pool.wait_ge(dt_made, w + 1)
                    nc.gpsimd.tensor_tensor(uu, dl, xi[b], ALU.mult).then_inc(u_made, 1)

            run_slots(pool.Fori, slot, prepare, normalise, lambda b, k: None)

            for m in pool_z:
                x, scores, after = factors(m)
                pool.wait_ge(rep_kept, after)
                if m >= ZRING:
                    pool.wait_ge(z_used, m + 1 - ZRING)
                nc.gpsimd.tensor_tensor(zring[m % ZRING], x, scores, ALU.mult).then_inc(z_pool, 1)

        @block.scalar
        def _(act):
            eps, one = cst[:, CEPS:CEPS + 1], cst[:, C1:C1 + 1]

            def norm(n, src, sq):
                act.wait_ge(ln_step, 5 * n + 3)
                nc.scalar.activation(sq, src, ACT.Square).then_inc(ln_square, 1)
                act.wait_ge(ln_step, 5 * n + 4)
                nc.scalar.activation(stat(1), stat(0), ACT.Ln, bias=eps, scale=1.0 / D).then_inc(ln_log, 1)
                act.wait_ge(ln_log, n + 1)
                nc.scalar.activation(stat(2), stat(1), ACT.Exp, scale=-0.5).then_inc(ln_rstd, 1)

            def deviation(n, b):
                act.wait_ge(ln_step, 5 * n + 4)
                nc.scalar.activation(stat_of(b, 1), stat_of(b, 0), ACT.Ln, bias=eps, scale=1.0 / D) \
                    .then_inc(ln_log, 1)
                act.wait_ge(ln_log, n + 1)
                nc.scalar.activation(stat_of(b, 2), stat_of(b, 1), ACT.Exp, scale=-0.5).then_inc(ln_rstd, 1)

            def square(n, src, sq):
                act.wait_ge(ln_step, 5 * n + 3)
                nc.scalar.activation(sq, src, ACT.Square).then_inc(ln_square, 1)

            act.wait_ge(a_capped, 1)
            nc.scalar.activation(alog[:, :], alog[:, :], ACT.Exp).then_inc(a_exp, 1)
            act.wait_ge(sel_in, 16)
            nc.scalar.copy(sel[:, :], sel_raw).then_inc(sel_done, 1)
            act.wait_ge(gathered, 16 * NC)
            nc.scalar.activation(stat(3), tiles(tok, D + 1)[:, :, D], ACT.Tanh).then_inc(tanh_done, 1)
            act.wait_ge(cst_in, 16)
            norm(0, work_a, work_b)
            norm(1, work_a, work_b)
            act.wait_ge(mix_in, 16)
            for q in range(4):
                act.wait_ge(xl_turned, q + 1)
                nc.scalar.activation(feat_t[0:D, q * H:(q + 1) * H], bank[q][0:D, :], ACT.Identity,
                                     bias=mix[0:D, LNB:LNB + 1], scale=mix[0:D, LNG:LNG + 1]).then_inc(xl_kept, 1)
            x1_v = x1p.rearrange("p (b t) -> p b t", b=NB)[0:D, :, 1:1 + T] \
                .rearrange("p b (t j) -> p b j t", j=J)
            for q in range(4):
                act.wait_ge(x1_made, q + 1)
                b, j = divmod(4 * q, J)
                nc.scalar.activation(x1_v[:, b, j:j + 4, :], bank[4 + q][0:D, :].rearrange("p (j t) -> p j t", j=4),
                                     ACT.Identity, bias=mix[0:D, B1:B1 + 1]).then_inc(x1_kept, 1)
            act.wait_ge(a_neg, 1)
            nc.scalar.copy(a_cur[:, :], neg_a[:, 0:NG]).then_inc(a_copied, 1)

            def normalise(unit, s):
                i, b = unit
                w = unit_no(unit)
                if s == 10:
                    act.wait_ge(x_ready, x_no(i, b, 1))
                    if not isinstance(i, int) or w > 0:
                        act.wait_ge(xn_ready, w)
                    nc.scalar.activation(scr_r[0:D, :], xs[0:D, bass.ds(x_at(i, b), T)], ACT.Square) \
                        .then_inc(x_squared, 1)
                if s == 17:
                    for half, src in enumerate((p_bank, y_bank[1])):
                        act.wait_ge(prep_mm, prep_no(unit, K_MS, half))
                        nc.scalar.activation(scr_r[0:D, half * H:(half + 1) * H], src[0:D, :], ACT.Ln,
                                             bias=eps[0:D, :]).then_inc(prep_read, 1)
                    act.wait_ge(prep_read, prep_no(unit, K_MS, 1))
                    nc.scalar.activation(scr_r[0:D, :], scr_r[0:D, :], ACT.Exp, scale=-0.5).then_inc(r_ready, 1)

            def prepare(unit, s):
                i, b = unit
                w = unit_no(unit)
                later = not (isinstance(i, int) and w < 2)
                if s == 2:
                    act.wait_ge(prep_mm, prep_no(unit, K_XI, 0))
                    nc.scalar.activation(xi[b][:, 0:H], p_bank[:, :], ACT.Identity,
                                         bias=wraw[:, CONVB:CONVB + 1]).then_inc(prep_read, 1)
                if s == 3:
                    act.wait_ge(prep_mm, prep_no(unit, K_Z, 0))
                    nc.scalar.copy(sz[b][:, 0:H], y_bank[0][:, :]).then_inc(prep_read, 1)
                if s == 5:
                    if later:
                        act.wait_ge(yz_done, 2 * w - 2)
                    act.wait_ge(prep_mm, prep_no(unit, K_XI, 1))
                    nc.scalar.activation(xi[b][:, H:2 * H], p_bank[:, :], ACT.Identity,
                                         bias=wraw[:, CONVB:CONVB + 1]).then_inc(prep_read, 1)
                    act.wait_ge(prep_mm, prep_no(unit, K_Z, 1))
                    nc.scalar.copy(sz[b][:, H:2 * H], y_bank[0][:, :]).then_inc(prep_read, 1)
                if s == 7:
                    if b == 0:
                        act.wait_ge(prep_mm, prep_no(unit, K_DT))
                        nc.scalar.copy(w_dt[:, :], p_bank[:, 0:DI]).then_inc(prep_read, 1)
                    act.wait_ge(prep_read, prep_no(unit, K_Z, 1))
                    nc.scalar.activation(xi[b], xi[b], ACT.Silu).then_inc(xi_ready, 1)
                    nc.scalar.activation(sz[b], sz[b], ACT.Silu).then_inc(z_ready, 1)
                if s == 8 and b == 0 and not isinstance(i, int):
                    nc.scalar.copy(a_next[:, :], neg_a[:, bass.ds(i * NG, NG)]).then_inc(a_fetched, 1)
                if s in (12, 13):
                    half = s - 12
                    src = (p_bank, y_bank[1])[half]
                    act.wait_ge(prep_mm, prep_no(unit, K_DP, half))
                    nc.scalar.activation(scr_a[:, half * H:(half + 1) * H], src[:, :], ACT.Abs,
                                         bias=wraw[:, DTB:DTB + 1]).then_inc(dt_abs, 1)
                    nc.scalar.activation(dl[:, half * H:(half + 1) * H], src[:, :], ACT.Relu,
                                         bias=wraw[:, DTB:DTB + 1]).then_inc(prep_read, 1)
                if s == 14:
                    act.wait_ge(dt_abs, 2 * w + 2)
                    nc.scalar.activation(scr_b[:, :], scr_a[:, :], ACT.Exp, scale=-1.0).then_inc(dt_exp, 1)
                if s == 17:
                    act.wait_ge(dt_exp, w + 1)
                    nc.scalar.activation(scr_c[:, :], scr_b[:, :], ACT.Ln, bias=one).then_inc(dt_log, 1)
                if s in (21, 25):
                    k = (s - 21) // 4
                    act.wait_ge(u_made if k else dt_made, w + 1)
                    if k or not (isinstance(i, int) and w == 0):
                        act.wait_ge(hi_moved, 64 * w + 32 * k)
                        act.wait_ge(lo_made, 2 * w + k)
                    nc.scalar.copy(hi[:, :], uu if k else dl).then_inc(hi_made, 1)
                if s in (24, 26):
                    half = (s - 24) // 2
                    for k, (dst, src) in enumerate(((brep[b], p_bank), (crep[b], y_bank[0]))):
                        act.wait_ge(prep_mm, prep_no(unit, K_BC, 2 * half + k))
                        nc.scalar.copy(dst[:, half * H:(half + 1) * H], src[:, :]).then_inc(prep_read, 1)

            def factor(unit, t):
                if t == 0 and unit[1] == 0 and not isinstance(unit[0], int):
                    act.wait_ge(a_fetched, unit[0])
                    act.wait_ge(dta_ready, step_no(unit, 0))
                    nc.scalar.copy(a_cur[:, :], a_next[:, :]).then_inc(a_copied, 1)
                    act.wait_ge(a_copied, unit[0] + 1)
                elif t == 0 and unit[1] == 0:
                    act.wait_ge(a_copied, 1)
                g = group_of(t % NG)
                n = step_no(unit, t)
                act.wait_ge(da_mm, n + 1)
                if not (isinstance(n, int) and n < DTA_RING):
                    act.wait_ge(scan_done, n + 1 - DTA_RING)
                nc.scalar.activation(dta[t % DTA_RING], da_bank[t % DA_RING][:, :], ACT.Exp,
                                     scale=a_cur[:, g:g + 1]).then_inc(dta_ready, 1)

            def slot(cur, prev, nxt, s):
                for unit, t in factor_steps(cur, nxt, s):
                    factor(unit, t)

            def close(b, k):
                n = 2 + 2 * b
                if k == 0:
                    act.wait_ge(x_ready, x_no(BLOCKS + 1, b, 1))
                    act.wait_ge(prep_read, prep_no((BLOCKS - 1, 1), K_BC, 3))
                    nc.scalar.copy(c_cat[b][0:D, :], xs[0:D, x_at(0, b):x_at(0, b) + T]).then_inc(cat_act, 1)
                if k == 5:
                    square(n, c_a[b], c_b[b])
                if k == 7:
                    deviation(n, b)
                if k == 12:
                    for half, src in enumerate((p_bank, second_bank(b, k))):
                        act.wait_ge(q_turned, 2 * b + half + 1)
                        nc.scalar.copy(c_feat[b][0:D, half * H:(half + 1) * H], src[0:D, :]).then_inc(q_kept, 1)
                if k == 17:
                    square(n + 1, c_x[b], c_mean[b])
                if k == 19:
                    deviation(n + 1, b)
                if k == 22:
                    for half, src in enumerate((p_bank, second_bank(b, k))):
                        act.wait_ge(x3_turned, 2 * b + half + 1)
                        nc.scalar.copy(c_feat[b][0:D, half * H:(half + 1) * H], src[0:D, :]).then_inc(x3_kept, 1)
                        cols = slice((2 * b + half) * H, (2 * b + half + 1) * H)
                        nc.scalar.copy(x_stack[0:D, cols], src[0:D, :]).then_inc(x3_high, 1)
                if k == 27:
                    act.wait_ge(gate_step, 9 * b + 2)
                    nc.scalar.activation(c_mean[b], c_mean[b], ACT.Exp).then_inc(gate_exp, 1)
                if k == 31:
                    for half, src in enumerate((p_bank, second_bank(b, k))):
                        act.wait_ge(gate_turned, 2 * b + half + 1)
                        cols = slice((2 * b + half) * H, (2 * b + half + 1) * H)
                        nc.scalar.copy(gate_stack[0:D, cols], src[0:D, :]).then_inc(gate_high, 1)

            def end(b, k):
                if k == 1:
                    act.wait_ge(z_used, NZB * (b + 1))
                    nc.scalar.copy(c_feat[b][:, 0:H], bank[6 + b][:, :]).then_inc(lat_kept, 1)
                if k == 6:
                    square(6 + b, c_a[b], c_b[b])
                if k == 8:
                    deviation(6 + b, b)

            run_slots(act.Fori, slot, prepare, normalise, close)

            for products, closing, ends in FFN_STEPS:
                for b, part in (part for m in products for part in SPREAD_AT.get(m, ())):
                    dst = srep[part] if part < NE else xrep[part - NE]
                    if (b, part) == (0, 0):
                        act.wait_ge(cat_act, 2)
                        act.wait_ge(cat_dve, 2)
                    if b:
                        products_until(act, (part + 1) * ND if part < NE else NZB - ND + part - NE + 1)
                    for half in range(2):
                        r_ = 2 * SPREADS.index((b, part)) + half
                        act.wait_ge(rep_made, r_ + 1)
                        nc.scalar.copy(dst[:, half * H:(half + 1) * H], bank[r_ % REP_BANKS][:, :]) \
                            .then_inc(rep_kept, 1)
                for k in closing:
                    close(1, k)
                for b, k in ends:
                    end(b, k)

        @block.vector
        def _(dve):
            def norm(n, src, cen, sq, dst):
                nc.vector.tensor_reduce(stat(4), tiles(src), AX_X, ALU.add).then_inc(ln_step, 1)
                dve.wait_ge(ln_step, 5 * n + 1)
                nc.vector.tensor_scalar(stat(5), stat(4), -1.0 / D, None, ALU.mult).then_inc(ln_step, 1)
                dve.wait_ge(ln_step, 5 * n + 2)
                nc.vector.tensor_tensor(tiles(cen), tiles(src), spread(stat(5)), ALU.add).then_inc(ln_step, 1)
                dve.wait_ge(ln_square, n + 1)
                nc.vector.tensor_reduce(stat(0), tiles(sq), AX_X, ALU.add).then_inc(ln_step, 1)
                dve.wait_ge(ln_rstd, n + 1)
                nc.vector.tensor_tensor(tiles(dst), tiles(cen), spread(stat(2)), ALU.mult).then_inc(ln_step, 1)

            def centre(n, b, src, cen):
                nc.vector.tensor_reduce(stat_of(b, 4), tiles(src), AX_X, ALU.add).then_inc(ln_step, 1)
                dve.wait_ge(ln_step, 5 * n + 1)
                nc.vector.tensor_scalar(stat_of(b, 5), stat_of(b, 4), -1.0 / D, None, ALU.mult).then_inc(ln_step, 1)
                dve.wait_ge(ln_step, 5 * n + 2)
                nc.vector.tensor_tensor(tiles(cen), tiles(src), of_tile(stat_of(b, 5)), ALU.add).then_inc(ln_step, 1)

            def sum_squares(n, b, sq):
                dve.wait_ge(ln_square, n + 1)
                nc.vector.tensor_reduce(stat_of(b, 0), tiles(sq), AX_X, ALU.add).then_inc(ln_step, 1)

            def scale(n, b, cen, dst):
                dve.wait_ge(ln_rstd, n + 1)
                nc.vector.tensor_tensor(tiles(dst), tiles(cen), of_tile(stat_of(b, 2)), ALU.mult).then_inc(ln_step, 1)

            dve.wait_ge(ids_in, 16)
            nc.vector.tensor_copy(idx_f[:, :], idx_i[:, :]).then_inc(idx_step, 1)
            dve.wait_ge(idx_step, 1)
            nc.vector.tensor_scalar(idx_g[:, :], idx_f[:, :], 0.0, float(V), ALU.is_lt, ALU.mult).then_inc(idx_step, 1)
            dve.wait_ge(idx_step, 2)
            nc.vector.tensor_tensor(idx_f[:, :], idx_f[:, :], idx_g[:, :], ALU.add).then_inc(idx_step, 1)
            dve.wait_ge(idx_step, 3)
            nc.vector.tensor_scalar(idx_g[:, :], idx_f[:, :], 0.0, float(V - 1), ALU.max, ALU.min).then_inc(idx_step, 1)
            dve.wait_ge(idx_step, 4)
            nc.vector.tensor_copy(idx_u[:, :], idx_g[:, :]).then_inc(idx_step, 1)
            nc.vector.memset(xn2[:, :], 0.0).then_inc(xn_zero, 1)
            nc.vector.memset(x1p[:, :], 0.0).then_inc(x1_zero, 1)
            dve.wait_ge(res_in, 16)
            nc.vector.tensor_scalar(alog[:, :].rearrange("p (i g) -> p i g", g=NG),
                                    reside[:, :].rearrange("p (i g) -> p i g", g=RES)[:, :, 0:NG],
                                    LOG_MOST, None, ALU.min).then_inc(a_capped, 1)
            dve.wait_ge(a_exp, 1)
            nc.vector.tensor_scalar(neg_a[:, :], alog[:, :], -1.0, None, ALU.mult).then_inc(a_neg, 1)

            g = tiles(tok, D + 1)[:, :, D]
            dve.wait_ge(gathered, 16 * NC)
            nc.vector.tensor_scalar(stat(6), g, GATE_L, 2.0 ** 23, ALU.mult, ALU.min).then_inc(hard_step, 1)
            dve.wait_ge(hard_step, 1)
            nc.vector.tensor_scalar(stat(6), stat(6), -2.0 ** 23, None, ALU.max).then_inc(hard_step, 1)
            dve.wait_ge(hard_step, 2)
            nc.vector.tensor_copy(whole_i[:, :], stat(6)).then_inc(hard_step, 1)
            dve.wait_ge(hard_step, 3)
            nc.vector.tensor_copy(stat(7), whole_i[:, :]).then_inc(hard_step, 1)
            dve.wait_ge(hard_step, 4)
            nc.vector.tensor_tensor(stat(6), stat(6), stat(7), ALU.subtract).then_inc(hard_step, 1)
            dve.wait_ge(hard_step, 5)
            nc.vector.scalar_tensor_tensor(stat(7), stat(6), 0.0, stat(6), ALU.is_lt, ALU.add).then_inc(hard_step, 1)
            dve.wait_ge(hard_step, 6)
            dve.wait_ge(tanh_done, 1)
            nc.vector.scalar_tensor_tensor(stat(8), stat(7), 1.0 / GATE_L, stat(3), ALU.mult, ALU.mult) \
                .then_inc(hard_step, 1)
            dve.wait_ge(cst_in, 16)
            nc.vector.tensor_tensor(tiles(work_a), cst[:, IOTA:IOTA + D].unsqueeze(1).to_broadcast([P, NC, D]),
                                    spread(g), ALU.is_lt).then_inc(hard_step, 1)
            dve.wait_ge(hard_step, 8)
            nc.vector.tensor_tensor(tiles(work_b), tiles(work_a), spread(stat(8)), ALU.add).then_inc(hard_step, 1)
            dve.wait_ge(hard_step, 9)
            nc.vector.tensor_tensor(tiles(h[:, :]), tiles(tok, D + 1)[:, :, 0:D], tiles(work_b), ALU.mult) \
                .then_inc(h_done, 1)
            dve.wait_ge(h_done, 1)
            norm(0, h[:, :], work_a, work_b, hn[:, :])
            dve.wait_ge(ln_step, 5)
            norm(1, hn[:, :], work_a, work_b, work_b)

            dve.wait_ge(row_in, 16)
            dve.wait_ge(x2_made, 2)
            for q in range(2):
                nc.vector.tensor_tensor(tiles(halves(x2)[q]), tiles(bank[q][:, :]), row_of(R_B2, J), ALU.add) \
                    .then_inc(x2_kept, 1)
            for q in range(4):
                dve.wait_ge(conv_made, q + 1)
                nc.vector.tensor_scalar(xs[0:D, q * H:(q + 1) * H], bank[2 + q][0:D, :], mix[0:D, HB:HB + 1], None,
                                        ALU.add).then_inc(x_ready, 1)
            for b in range(NB):
                dve.wait_ge(x_ready, 2 * b + 2)
                nc.vector.tensor_copy(xs[0:D, (NB + b) * T:(NB + b + 1) * T],
                                      xs[0:D, b * T:(b + 1) * T][:, ::-1]).then_inc(x_ready, 2)

            def prepare(unit, s):
                i, b = unit
                w = unit_no(unit)
                if s == 0 and b == 0:
                    dve.wait_ge(w_in, 16 * i + 16)
                    nc.vector.scalar_tensor_tensor(
                        w_xi[:, :].rearrange("p (a d) -> p a d", a=2),
                        wraw[:, WX:WX + DI].unsqueeze(1).to_broadcast([P, 2, DI]), wraw[:, RMS:RMS + 1],
                        wraw[:, CW:CW + 2 * DI].rearrange("p (a d) -> p a d", a=2), ALU.mult, ALU.mult)
                    nc.vector.tensor_scalar(w_z[:, :], wraw[0:D, WZ:WZ + DI], wraw[0:D, RMS:RMS + 1], None,
                                            ALU.mult).then_inc(w_scaled, 1)
                if s in (22, 26):
                    k = (s - 22) // 4
                    dve.wait_ge(hi_made, 2 * w + k + 1)
                    if k or not (isinstance(i, int) and w == 0):
                        dve.wait_ge(lo_moved, 64 * w + 32 * k)
                    nc.vector.tensor_tensor(lo[:, :], uu if k else dl, hi[:, :].bitcast(F32), ALU.subtract) \
                        .then_inc(lo_made, 1)

            def finish(unit, half):
                i, b = unit
                cols = slice(half * H, (half + 1) * H)
                n = 2 * unit_no(unit) + half
                dve.wait_ge(hc_summed, step_no(unit, NG * (half + 1)))
                if half == 0:
                    dve.wait_ge(z_ready, unit_no(unit) + 1)
                nc.vector.scalar_tensor_tensor(yz[half], xi[b][:, cols],
                                               reside[:, bass.ds(i * RES + NG, 1)], y_bank[half][:, :],
                                               ALU.mult, ALU.add).then_inc(yd_done, 1)
                dve.wait_ge(yd_done, n + 1)
                nc.vector.tensor_tensor(yz[half], yz[half], sz[b][:, cols], ALU.mult).then_inc(yz_done, 1)

            def add_out(unit, half):
                i, b = unit
                dve.wait_ge(out_mm, 2 * unit_no(unit) + half + 1)
                nc.vector.tensor_tensor(xs[0:D, bass.ds(x_at(i, b) + half * H, H)],
                                        xs[0:D, bass.ds(x_at(i, b) + half * H, H)], y_bank[half][0:D, :],
                                        ALU.add).then_inc(x_ready, 1)

            def scan(unit, t):
                half, k = divmod(t, NG)
                n = step_no(unit, t)
                if not (isinstance(n, int) and n < H_RING):
                    dve.wait_ge(hc_done, n + 1 - H_RING)
                if half == 1:
                    initial = last_h[:, k:k + 1]
                    dve.wait_ge(last_saved, 4 * unit_no(unit) + k // 4 + 1)
                else:
                    initial = 0.0
                dve.wait_ge(bx_done, n + 1)
                dve.wait_ge(dta_ready, n + 1)
                nc.vector.tensor_tensor_scan(hst[t % H_RING], dta[t % DTA_RING], u_bank[t % U_RING][:, :], initial,
                                             ALU.mult, ALU.add).then_inc(scan_done, 1)

            def slot(cur, prev, nxt, s):
                if s < 0:
                    return
                if cur is not None:
                    n = step_no(cur, s)
                    half = s // NG
                    dve.wait_ge(u_mm, n + 1)
                    nc.vector.tensor_tensor(u_bank[s % U_RING][:, :], u_bank[s % U_RING][:, :],
                                            brep[cur[1]][:, half * H:(half + 1) * H], ALU.mult).then_inc(bx_done, 1)
                if s >= 1 and cur is not None:
                    scan(cur, s - 1)
                if 5 <= s <= NG + 1 and s % 4 == 1 and cur is not None:
                    k = s - 5
                    dve.wait_ge(scan_done, step_no(cur, k + 4))
                    nc.vector.tensor_copy(
                        last_h[:, k:k + 4],
                        hst_all.rearrange("p (k t) -> p k t", t=H)[:, k % H_RING:k % H_RING + 4, H - 1]) \
                        .then_inc(last_saved, 1)
                if s == 0 and prev is not None:
                    scan(prev, STEPS - 1)
                if s == 20 and cur is not None:
                    finish(cur, 0)
                if s == 22 and cur is not None:
                    add_out(cur, 0)
                if s == 4 and prev is not None:
                    finish(prev, 1)
                if s == 6 and prev is not None:
                    add_out(prev, 1)

            def close(b, k):
                mine = slice(b * J * D, (b + 1) * J * D)
                n, d0, g0 = 2 + 2 * b, 7 * b, 9 * b
                if k == 0:
                    dve.wait_ge(x_ready, x_no(BLOCKS + 1, b, 1))
                    dve.wait_ge(prep_read, prep_no((BLOCKS - 1, 1), K_BC, 3))
                    nc.vector.tensor_copy(c_cat[b][D:2 * D, :], xs[0:D, x_at(1, b):x_at(1, b) + T][:, ::-1]) \
                        .then_inc(cat_dve, 1)
                if k == 2:
                    dve.wait_ge(down_made, b + 1)
                    nc.vector.tensor_tensor(tiles(c_b[b]), tiles(p_bank[:, :]), row_of(R_DOWNB, J), ALU.add) \
                        .then_inc(down_step, 1)
                if k == 3:
                    dve.wait_ge(down_step, d0 + 1)
                    centre(n, b, c_b[b], c_a[b])
                if k == 4:
                    nc.vector.tensor_tensor(tiles(hn[:, mine]), tiles(hn[:, mine]), row_of(R_B3, J), ALU.add) \
                        .then_inc(down_step, 1)
                if k == 5:
                    dve.wait_ge(down_step, d0 + 2)
                    nc.vector.tensor_tensor(h[:, mine], h[:, mine], hn[:, mine], ALU.add).then_inc(down_step, 1)
                if k == 6:
                    sum_squares(n, b, c_b[b])
                if k == 8:
                    scale(n, b, c_a[b], c_b[b])
                    dve.wait_ge(ln_step, 5 * n + 5)
                    nc.vector.tensor_tensor(tiles(c_a[b]), tiles(c_b[b]), row_of(R_LNG, J), ALU.mult) \
                        .then_inc(down_step, 1)
                if k == 9:
                    dve.wait_ge(down_step, d0 + 4)
                    nc.vector.tensor_tensor(tiles(c_b[b]), tiles(c_a[b]), row_of(R_LNB, J), ALU.add) \
                        .then_inc(down_step, 1)
                if k == 10:
                    dve.wait_ge(down_step, d0 + 5)
                    nc.vector.tensor_tensor(c_a[b], c_b[b], x2[:, mine], ALU.mult).then_inc(down_step, 1)
                if k == 14:
                    dve.wait_ge(y3_made, b + 1)
                    nc.vector.tensor_tensor(h[:, mine], h[:, mine], p_bank[:, :], ALU.add).then_inc(down_step, 1)
                if k == 15:
                    dve.wait_ge(down_step, d0 + 7)
                    centre(n + 1, b, h[:, mine], c_x[b])
                if k == 18:
                    sum_squares(n + 1, b, c_mean[b])
                if k == 20:
                    scale(n + 1, b, c_x[b], c_x[b])
                if k == 23:
                    for half, src in enumerate((p_bank, second_bank(b, k))):
                        cols = slice((2 * b + half) * H, (2 * b + half + 1) * H)
                        dve.wait_ge(x3_high, 2 * b + half + 1)
                        nc.vector.tensor_tensor(x_stack[D:2 * D, cols], src[0:D, :], x_stack[0:D, cols].bitcast(F32),
                                                ALU.subtract).then_inc(x3_low, 1)
                top = top8[:, b * J * 8:(b + 1) * J * 8]
                top_v = top.rearrange("p (c k) -> p c k", k=8)
                if k == 25:
                    dve.wait_ge(gate_made, b + 1)
                    nc.vector.tensor_copy(c_gate[b], p_bank[:, :]).then_inc(gate_step, 1)
                    dve.wait_ge(gate_step, g0 + 1)
                    for c in range(J):
                        last = nc.vector.max(top[:, 8 * c:8 * c + 8], c_gate[b][:, c * D:(c + 1) * D])
                    last.then_inc(top_done, 1)
                if k == 26:
                    dve.wait_ge(top_done, b + 1)
                    nc.vector.tensor_tensor(tiles(c_mean[b]), tiles(c_gate[b]),
                                            top_v[:, :, 0:1].to_broadcast([P, J, D]), ALU.subtract) \
                        .then_inc(gate_step, 1)
                    dve.wait_ge(gate_step, g0 + 2)
                    nc.vector.memset(top_v[:, :, TOPK:8], BIG).then_inc(gate_step, 1)
                    dve.wait_ge(gate_step, g0 + 3)
                    for c in range(J):
                        last = nc.vector.match_replace(c_rest[b][:, c * D:(c + 1) * D], top[:, 8 * c:8 * c + 8],
                                                       c_gate[b][:, c * D:(c + 1) * D], -BIG)
                    last.then_inc(gate_step, 1)
                if k == 27:
                    dve.wait_ge(gate_step, g0 + 4)
                    nc.vector.tensor_tensor(c_b[b], c_rest[b], c_gate[b], ALU.not_equal).then_inc(gate_step, 1)
                if k == 28:
                    dve.wait_ge(gate_step, g0 + 5)
                    dve.wait_ge(gate_exp, b + 1)
                    nc.vector.tensor_tensor(c_weighed[b], c_b[b], c_mean[b], ALU.mult).then_inc(gate_step, 1)
                    dve.wait_ge(gate_step, g0 + 6)
                    nc.vector.tensor_reduce(stat_of(b, 9), tiles(c_weighed[b]), AX_X, ALU.add).then_inc(gate_step, 1)
                if k == 29:
                    dve.wait_ge(gate_step, g0 + 7)
                    nc.vector.reciprocal(stat_of(b, 10), stat_of(b, 9)).then_inc(gate_step, 1)
                    dve.wait_ge(gate_step, g0 + 8)
                    nc.vector.tensor_tensor(tiles(c_gate[b]), tiles(c_weighed[b]), of_tile(stat_of(b, 10)),
                                            ALU.mult).then_inc(gate_step, 1)
                if k == 32:
                    for half, src in enumerate((p_bank, second_bank(b, k))):
                        cols = slice((2 * b + half) * H, (2 * b + half + 1) * H)
                        dve.wait_ge(gate_high, 2 * b + half + 1)
                        nc.vector.tensor_tensor(gate_stack[D:2 * D, cols], src[0:D, :],
                                                gate_stack[0:D, cols].bitcast(F32), ALU.subtract) \
                            .then_inc(gate_low, 1)

            def end(b, k):
                mine = slice(b * J * D, (b + 1) * J * D)
                e0, n = 5 * b, 6 + b
                if k == 0:
                    nc.vector.tensor_tensor(tiles(c_x[b]), tiles(c_x[b]), row_of(R_OUTB, J), ALU.add) \
                        .then_inc(end_step, 1)
                if k == 4:
                    dve.wait_ge(end_step, e0 + 1)
                    for half, src in enumerate((bank[6 + b], bank[5])):
                        cols = slice(half * HALF // 2, (half + 1) * HALF // 2)
                        dve.wait_ge(proj_made, 2 * b + half + 1)
                        nc.vector.tensor_tensor(c_rest[b][:, cols], c_x[b][:, cols], src[:, 0:HALF // 2], ALU.add) \
                            .then_inc(end_step, 1)
                if k == 5:
                    dve.wait_ge(end_step, e0 + 3)
                    centre(n, b, c_rest[b], c_a[b])
                if k == 7:
                    sum_squares(n, b, c_b[b])
                if k == 9:
                    scale(n, b, c_a[b], c_b[b])
                    dve.wait_ge(ln_step, 5 * n + 5)
                    nc.vector.tensor_tensor(tiles(c_rest[b]), tiles(c_b[b]), row_of(R_FG, J), ALU.mult) \
                        .then_inc(end_step, 1)
                if k == 10:
                    dve.wait_ge(end_step, e0 + 4)
                    nc.vector.tensor_tensor(tiles(c_a[b]), tiles(c_rest[b]), row_of(R_FB, J), ALU.add) \
                        .then_inc(end_step, 1)
                if k == 11:
                    dve.wait_ge(end_step, e0 + 5)
                    nc.vector.tensor_tensor(c_mean[b], c_a[b], h[:, mine], ALU.add).then_inc(out_ready, 1)

            run_slots(dve.Fori, slot, prepare, lambda unit, s: None, close)

            for products, closing, ends in FFN_STEPS:
                for m in products:
                    if m in dve_z:
                        x, scores, after = factors(m)
                        dve.wait_ge(rep_kept, after)
                        if m >= ZRING:
                            dve.wait_ge(z_used, m + 1 - ZRING)
                        nc.vector.tensor_tensor(zring[m % ZRING], x, scores, ALU.mult).then_inc(z_dve, 1)
                for k in closing:
                    close(1, k)
                for b, k in ends:
                    end(b, k)

        @block.tensor
        def _(pe):
            ident = cst[:, IDN:IDN + P]

            def turn(src, q, made):
                for m in range(4):
                    c = 4 * q + m
                    last = nc.tensor.transpose(bank[q][0:D, m * P:(m + 1) * P], src[:, c * D:(c + 1) * D], ident)
                last.then_inc(made, 1)

            pe.wait_ge(cst_in, 16)
            pe.wait_ge(sel_done, 1)
            pe.wait_ge(ln_step, 10)
            for q in range(4):
                turn(work_b, q, xl_turned)
            pe.wait_ge(mix_in, 16)
            for q in range(4):
                pe.wait_ge(xl_kept, q + 1)
                nc.tensor.matmul(bank[4 + q][0:D, :], mix[0:D, W1:W1 + D], feat_t[0:D, q * H:(q + 1) * H],
                                 start=True, stop=True).then_inc(x1_made, 1)
            for q in range(2):
                for m in range(J):
                    c = J * q + m
                    last = nc.tensor.matmul(bank[q][:, m * D:(m + 1) * D], feat_t[0:D, c * P:(c + 1) * P],
                                            mix[0:D, W2:W2 + D], start=True, stop=True)
                last.then_inc(x2_made, 1)
            pe.wait_ge(x1_kept, 4)
            pe.wait_ge(x1_zero, 1)
            for q in range(4):
                b, half = divmod(q, 2)
                for k in range(3):
                    first = b * (T + 2) + half * H + k
                    last = nc.tensor.matmul(bank[2 + q][0:D, :], mix[0:D, HCONV + k * D:HCONV + (k + 1) * D],
                                            x1p[0:D, first:first + H], start=(k == 0), stop=(k == 2))
                last.then_inc(conv_made, 1)

            def product(n, dst, lhs, rhs, more=None, back=2):
                if not (isinstance(n, int) and n <= back):
                    pe.wait_ge(prep_read, n - back)
                if more is None:
                    nc.tensor.matmul(dst, lhs, rhs, start=True, stop=True).then_inc(prep_mm, 1)
                else:
                    nc.tensor.matmul(dst, lhs, rhs, start=True, stop=False)
                    nc.tensor.matmul(dst, more[0], more[1], start=False, stop=True).then_inc(prep_mm, 1)

            def normalise(unit, s):
                w = unit_no(unit)
                if s in (14, 15):
                    half = s - 14
                    pe.wait_ge(x_squared, w + 1)
                    product(prep_no(unit, K_MS, half), (p_bank, y_bank[1])[half][:, :], cst[0:D, ONE:ONE + P],
                            scr_r[0:D, half * H:(half + 1) * H])

            def prepare(unit, s):
                i, b = unit
                w = unit_no(unit)
                if s == 1:
                    if b == 0:
                        pe.wait_ge(w_scaled, i + 1)
                    pe.wait_ge(xn_ready, w + 1)
                    pe.wait_ge(shifted, 16 * w + 16)
                if s in (1, 3):
                    half = (s - 1) // 2
                    o = half * H
                    product(prep_no(unit, K_XI, half), p_bank[:, :], w_xi[:, 0:DI], xn2[:, o:o + H],
                            (w_xi[:, DI:2 * DI], xn2[:, o + 2:o + 2 + H]))
                if s in (2, 4):
                    half = (s - 2) // 2
                    if half == 0 and isinstance(i, int) and w == 0:
                        pe.wait_ge(x_ready, 8)
                    o = half * H + 3
                    product(prep_no(unit, K_Z, half), y_bank[0][:, :], w_z[:, :], xn2[0:D, o:o + H])
                if s == 6 and b == 0:
                    product(prep_no(unit, K_DT), p_bank[:, 0:DI], wraw[0:RANK, X4:X4 + DI],
                            wraw[0:RANK, DTW:DTW + DI])
                if s in (10, 11):
                    half = s - 10
                    o = half * H
                    if half == 0:
                        pe.wait_ge(xi_ready, w + 1)
                    else:
                        pe.wait_ge(x_ready, x_no(i + 1, b, 1))
                    product(prep_no(unit, K_DP, half), (p_bank, y_bank[1])[half][:, :], w_dt[:, :],
                            xi[b][:, o:o + H], back=1 if b == 0 and half == 0 else 2)
                if s in (23, 25):
                    half = (s - 23) // 2
                    o = half * H
                    product(prep_no(unit, K_BC, 2 * half), p_bank[:, :], wraw[:, XB:XB + P], xi[b][:, o:o + H])
                    if half == 0 and not (isinstance(i, int) and w == 0):
                        last = (i, 0) if b else (i - 1, 1)
                        pe.wait_ge(x_ready, x_no(last[0] + 2, last[1], 0))
                    product(prep_no(unit, K_BC, 2 * half + 1), y_bank[0][:, :], wraw[:, XC:XC + P],
                            xi[b][:, o:o + H])

            def spread_step(unit, which, t, dst):
                half, k = divmod(t, NG)
                side, g = divmod(group_of(k), NG // 2)
                first = (2 * which + side) * T + half * H
                return nc.tensor.matmul(dst[:, :], sel[:, SEL + g * P:SEL + (g + 1) * P],
                                        stack[unit[1]][:, first:first + H], start=True, stop=True)

            def sum_states(unit, t0):
                half, k0 = divmod(t0, NG)
                n = step_no(unit, t0 + 3)
                pe.wait_ge(hc_done, n + 1)
                if k0 == 0:
                    if not (isinstance(unit[0], int) and unit_no(unit) == 0):
                        last = (unit[0], 0) if unit[1] else (unit[0] - 1, 1)
                        pe.wait_ge(x_ready, x_no(last[0] + 2, last[1], half))
                    if isinstance(unit[0], int) and unit == (BLOCKS - 1, 1):
                        pe.wait_ge(prep_read, prep_no(unit, K_BC, 3))
                        if half == 1:
                            pe.wait_ge(q_kept, 2)
                    else:
                        nxt = (unit[0] + 1, 0) if unit[1] else (unit[0], 1)
                        kind = K_Z if half == 0 else K_DP if isinstance(nxt[0], int) and nxt == (BLOCKS - 1, 1) else K_MS
                        after = nxt if kind != K_MS else (nxt[0] + 1, 0) if nxt[1] else (nxt[0], 1)
                        pe.wait_ge(prep_read, prep_no(after, kind, 1))
                for k in range(k0, k0 + 4):
                    q, m = divmod(group_of(k), 4)
                    last = nc.tensor.matmul(y_bank[half][32 * q:32 * q + 32, :],
                                            cst[:, SUM + m * 32:SUM + (m + 1) * 32], hcr[(t0 + k - k0) % HC_RING],
                                            start=(k0 == 0), stop=(k0 == NG - 4), tile_position=(0, 32 * q))
                last.then_inc(hc_summed, 4)

            def out_product(unit, half):
                pe.wait_ge(yz_done, 2 * unit_no(unit) + half + 1)
                if unit[1] == 0 and half == 0:
                    pe.wait_ge(outw_in, 16 * unit[0] + 16)
                nc.tensor.matmul(y_bank[half][0:D, :], out_w[:, :], yz[half], start=True, stop=True) \
                    .then_inc(out_mm, 1)

            def slot(cur, prev, nxt, s):
                unit, t = (cur, s + 1) if s + 1 < STEPS else (nxt, 0)
                if unit is not None and s + 1 >= 0:
                    n = step_no(unit, t)
                    if t == 0:
                        pe.wait_ge(hi_moved, 64 * unit_no(unit) + 64)
                        pe.wait_ge(lo_moved, 64 * unit_no(unit) + 64)
                    back = U_RING if t >= U_RING else t + STEPS - (STEPS - 1 - (STEPS - 1 - t) % U_RING)
                    if not (isinstance(n, int) and n < U_RING):
                        pe.wait_ge(scan_done, n + 1 - back)
                    spread_step(unit, 1, t, u_bank[t % U_RING]).then_inc(u_mm, 1)
                for unit, t in factor_steps(cur, nxt, s):
                    n = step_no(unit, t)
                    if t == 0:
                        pe.wait_ge(hi_moved, 64 * unit_no(unit) + 32)
                        pe.wait_ge(lo_moved, 64 * unit_no(unit) + 32)
                    if not (isinstance(n, int) and n < DA_RING):
                        pe.wait_ge(dta_ready, n + 1 - DA_RING)
                    spread_step(unit, 0, t, da_bank[t % DA_RING]).then_inc(da_mm, 1)
                if s >= 6 and s % 4 == 2 and cur is not None:
                    sum_states(cur, s - 6)
                if s == 2 and prev is not None:
                    sum_states(prev, STEPS - 4)
                if s == 21 and cur is not None:
                    out_product(cur, 0)
                if s == 5 and prev is not None:
                    out_product(prev, 1)

            def turn_batch(src, b, k, made):
                for half, dst in enumerate((p_bank, second_bank(b, k))):
                    for m in range(4):
                        c = 4 * half + m
                        last = nc.tensor.transpose(dst[0:D, m * P:(m + 1) * P], src[:, c * D:(c + 1) * D], ident)
                    last.then_inc(made, 1)

            def close(b, k):
                if k == 1:
                    pe.wait_ge(cat_act, b + 1)
                    pe.wait_ge(cat_dve, b + 1)
                    if b == 0:
                        pe.wait_ge(prep_read, prep_no((BLOCKS - 1, 1), K_BC, 3))
                    else:
                        pe.wait_ge(gate_low, 2)
                    cat_v = c_cat[b].rearrange("p (t j) -> p j t", j=J)
                    for m in range(J):
                        last = nc.tensor.matmul(p_bank[:, m * D:(m + 1) * D], cat_v[:, m, :],
                                                mix[:, DOWN:DOWN + D], start=True, stop=True)
                    last.then_inc(down_made, 1)
                if k == 11:
                    pe.wait_ge(down_step, 7 * b + 6)
                    turn_batch(c_a[b], b, k, q_turned)
                if k == 13:
                    pe.wait_ge(q_kept, 2 * b + 2)
                    for m in range(J):
                        last = nc.tensor.matmul(p_bank[:, m * D:(m + 1) * D], c_feat[b][0:D, m * P:(m + 1) * P],
                                                mix[0:D, W3:W3 + D], start=True, stop=True)
                    last.then_inc(y3_made, 1)
                if k == 21:
                    if b == 0:
                        pe.wait_ge(x_ready, x_no(BLOCKS + 1, 1, 0))
                    pe.wait_ge(ln_step, 5 * (3 + 2 * b) + 5)
                    turn_batch(c_x[b], b, k, x3_turned)
                if k == 24:
                    pe.wait_ge(x3_kept, 2 * b + 2)
                    pe.wait_ge(x3_low, 2 * b + 1)
                    for m in range(J):
                        last = nc.tensor.matmul(p_bank[:, m * D:(m + 1) * D], c_feat[b][0:D, m * P:(m + 1) * P],
                                                mix[0:D, GATEW:GATEW + D], start=True, stop=True)
                    last.then_inc(gate_made, 1)
                if k == 30:
                    pe.wait_ge(gate_step, 9 * b + 9)
                    pe.wait_ge(x3_low, 2 * b + 2)
                    turn_batch(c_gate[b], b, k, gate_turned)

            def end(b, k):
                if k == 3:
                    pe.wait_ge(lat_kept, b + 1)
                    if b:
                        pe.wait_ge(end_step, 3)
                    for half, dst in enumerate((bank[6 + b], bank[5])):
                        r_ = slice(half * D, (half + 1) * D)
                        for m in range(4):
                            last = nc.tensor.matmul(dst[:, m * D:(m + 1) * D], c_feat[b][r_, m * P:(m + 1) * P],
                                                    mix[r_, OUTW:OUTW + D], start=True, stop=True)
                        last.then_inc(proj_made, 1)

            run_slots(pe.Fori, slot, prepare, normalise, close)

            def use_product(m):
                b, n = divmod(m, NZB)
                if m in pool_z:
                    pe.wait_ge(z_pool, pool_z.index(m) + 1)
                else:
                    pe.wait_ge(z_dve, dve_z.index(m) + 1)
                for half in range(2):
                    last = nc.tensor.matmul(bank[6 + b][half * D:(half + 1) * D, :], lat[:, n * D:(n + 1) * D],
                                            zring[m % ZRING][:, half * H:(half + 1) * H],
                                            start=(n == 0), stop=(n == NZB - 1), tile_position=(0, half * D))
                last.then_inc(z_used, 1)

            pe.wait_ge(x_ready, x_no(BLOCKS + 1, 1, 1))
            pe.wait_ge(x3_low, 2)
            pe.wait_ge(gate_low, 2)
            pe.wait_ge(lat_in, 16)
            used = 0
            for products, closing, ends in FFN_STEPS:
                for b, part in (part for m in products for part in SPREAD_AT.get(m, ())):
                    if (b, part) == (1, NE):
                        pe.wait_ge(x3_low, 4)
                    if (b, part) == (1, 0):
                        pe.wait_ge(gate_low, 4)
                    first, src = (SELE + part * P, gate_stack) if part < NE else (SEL + (part - NE) * P, x_stack)
                    for half in range(2):
                        r_ = 2 * SPREADS.index((b, part)) + half
                        if r_ >= REP_BANKS:
                            pe.wait_ge(rep_kept, r_ + 1 - REP_BANKS)
                        q = 2 * b + half
                        nc.tensor.matmul(bank[r_ % REP_BANKS][:, :], sel[:, first:first + P],
                                         src[:, q * H:(q + 1) * H], start=True, stop=True).then_inc(rep_made, 1)
                until = products[0] if products else NZ if ends and ends[0][0] else used
                for m in range(used, until):
                    use_product(m)
                used = until
                for k in closing:
                    close(1, k)
                for b, k in ends:
                    end(b, k)


def _block_weights(np, w, l):
    inproj, convw, xproj = w["inproj"][l], w["convw"][l], w["xproj"][l]
    pack = np.zeros((P, WPACK), np.float32)
    for a in range(2):
        r = slice(a * D, (a + 1) * D)
        pack[r, WX:WX + DI] = inproj[:DI].T
        pack[r, CW:CW + DI] = convw[:, a]
        pack[r, CW + DI:CW + 2 * DI] = convw[:, 2 + a]
        pack[r, RMS] = w["rms"][l]
    pack[:D, WZ:WZ + DI] = inproj[DI:].T
    pack[:, XB:XB + P] = np.repeat(xproj[RANK:RANK + NS].T, GR, axis=1)
    pack[:, XC:XC + P] = np.repeat(xproj[RANK + NS:].T, GR, axis=1)
    pack[:RANK, X4:X4 + DI] = xproj[:RANK]
    pack[:RANK, DTW:DTW + DI] = w["dtw"][l].T
    pack[:, CONVB], pack[:, DTB] = w["convb"][l], w["dtb"][l]
    res = np.zeros((P, RES), np.float32)
    res[:, :NG] = w["Alog"][l].reshape(NG, GR, NS).transpose(2, 1, 0).reshape(P, NG)
    res[:, NG] = w["D"][l]
    return pack, w["outw"][l].T, res


def kernel(**inputs):
    import numpy as np
    import concourse.bacc as bacc
    from concourse.bass_utils import run_bass_kernel_spmd as run

    a = {k: np.asarray(v) for k, v in inputs.items()}
    parts = []
    for l in range(2):
        for d in "fb":
            pre = f"L0_attn_{d}_"
            parts.append(_block_weights(np, {k[len(pre):]: v for k, v in a.items() if k.startswith(pre)}, l))
    consts = np.zeros((P, CPACK), np.float32)
    consts[:, IDN:IDN + P] = np.eye(P)
    spack = np.zeros((P, SPACK), np.float32)
    for r in range(P):
        for k in range(4):
            consts[r, SUM + k * 32 + k * GR + r % GR] = 1.0
        g, d = divmod(r % D, GR)
        spack[r, SEL + g * P + d:SEL + (g + 1) * P:GR] = 1.0
        k, e = divmod(r % D, ES)
        spack[r, SELE + k * P + e * DS:SELE + k * P + (e + 1) * DS] = 1.0
    consts[:, ONE:ONE + P] = 1.0 / D
    consts[:, IOTA:IOTA + D] = np.arange(D)
    consts[:, CEPS], consts[:, C1] = EPS, 1.0
    mp = np.zeros((P, MPACK), np.float32)
    t = "L0_attn_"
    mp[:D, W1:W1 + D], mp[:D, W2:W2 + D], mp[:D, W3:W3 + D] = a[t + "w1"].T, a[t + "w2"].T, a[t + "w3"].T
    mp[:, DOWN:DOWN + D] = a[t + "down_w"].T
    mp[:D, GATEW:GATEW + E] = a["L0_ffn_gate_w"].T
    mp[:D, OUTW:OUTW + D] = mp[D:, OUTW:OUTW + D] = a["L0_ffn_out_w"].T
    for k in range(3):
        mp[:D, HCONV + k * D:HCONV + (k + 1) * D] = a[t + "hconv_w"][:, :, k].T
    mp[:D, LNG], mp[:D, LNB], mp[:D, B1], mp[:D, HB] = a[t + "ln_g"], a[t + "ln_b"], a[t + "b1"], a[t + "hconv_b"]
    rows = np.concatenate([a[t + "b2"], a[t + "down_b"], a[t + "ln_g"], a[t + "ln_b"], a[t + "b3"],
                           a["L0_ffn_out_b"], a["L0_ffn_ln_g"], a["L0_ffn_ln_b"]])
    arrays = {
        "ids": np.ascontiguousarray(a["x"]),
        "table": np.concatenate([a["L0_tok_embedding"], a["L0_tok_gates"][:, None]], axis=1),
        "wpack": np.concatenate([p[0] for p in parts]),
        "outw": np.ascontiguousarray(np.concatenate([p[1] for p in parts])),
        "res": np.concatenate([p[2] for p in parts], axis=1),
        "consts": consts,
        "spack": spack,
        "mpack": mp,
        "rows": np.ascontiguousarray(np.broadcast_to(rows[None], (P, 8 * D))),
        "lattice": np.ascontiguousarray(a["L0_ffn_lattice_weights"].reshape(NE, ES, ND, DS, D)
                                        .transpose(1, 3, 0, 2, 4).reshape(P, NE * ND * D)),
    }
    nc = bacc.Bacc("TRN2", target_bir_lowering=False, num_devices=1)
    aps = [nc.dram_tensor("in_" + k, v.shape, mybir.dt.from_np(v.dtype), kind="ExternalInput").ap()
           for k, v in arrays.items()]
    out = nc.dram_tensor("out_0", (NB, T, D), F32, kind="ExternalOutput").ap()
    tower_kernel(nc, *aps, out)
    r = run(nc, [{"in_" + k: v for k, v in arrays.items()}], core_ids=[0])
    return r.results[0]["out_0"]
```

```python
from contextlib import ExitStack

import concourse.bass as bass
from concourse import mybir

F32 = mybir.dt.float32
F32R = mybir.dt.float32r
I32 = mybir.dt.int32
U32 = mybir.dt.uint32
ALU = mybir.AluOpType
ACT = mybir.ActivationFunctionType
AX_X = mybir.AxisListType.X

P = 128
V, D = 32000, 64
NB, T = 2, 1024
J = T // P
NC = NB * J
HALF = NC // 2 * D
DI, NS, RANK = 128, 16, 4
GR = P // NS
NG = DI // GR
H = 512
BLOCKS = 4
STEPS = 2 * NG
E, TOPK = 64, 6
ES, DS = 16, 8
NE, ND = E // ES, D // DS
NZ = NB * NE * ND
EPS = 1e-5
GATE_L = 1e9
BIG = 3.0e38
LOG_MOST = 80.0

WX, WZ, CW, XB, XC, X4, DTW = 0, 128, 256, 512, 640, 768, 896
RMS, CONVB, DTB, WPACK = 1024, 1025, 1026, 1027
RES = NG + 1
IDN, SUM, ONE, IOTA, CEPS, C1, CPACK = 0, 128, 256, 384, 448, 449, 450
SEL, SELE, SPACK = 0, 1024, 1536
W1, W2, W3, DOWN, GATEW, OUTW, HCONV = 0, 64, 128, 192, 256, 320, 384
LNG, LNB, B1, HB, MPACK = 512, 513, 514, 515, 516
R_B2, R_DOWNB, R_LNG, R_LNB, R_B3, R_OUTB, R_FG, R_FB = range(8)

DA_RING, U_RING, DTA_RING, HC_RING, H_RING = 2, 3, 8, 8, 8
AHEAD = 4
LEAD = {5: 1, 6: 2, 7: 2, 8: 1, 15: 1, 16: 2, 17: 2, 18: 1}
CUT = 9
CLOSE = 7
PER_BLOCK = 25
ARENA = 34000
ZRING = 6
END = 12
OPEN, OPEN_LAG = 18, 5
OPEN_AT, OPEN_LATE = {11: 13, 15: 14, 18: 15}, {7: 16, 8: 17}
K_XI, K_Z, K_DT, K_DP, K_MS, K_BC = range(6)


def group_of(k):
    return (k % 4) * 4 + k // 4


def step_no(unit, s):
    return 2 * STEPS * unit[0] + STEPS * unit[1] + s


def unit_no(unit):
    return 2 * unit[0] + unit[1]


def prep_no(unit, kind, k=0):
    i, b = unit
    if kind == K_MS:
        if isinstance(i, int) and unit == (0, 0):
            return k + 1
        i, b = (i, 0) if b else (i - 1, 1)
    first = 0 if b else 1
    at = {K_XI: 2 * k, K_Z: 2 * k + 1, K_DT: 4, K_DP: 4 + first + k, K_MS: 6 + first + k,
          K_BC: 8 + first + k}[kind]
    if isinstance(i, int) and (i, b) == (BLOCKS - 1, 1) and kind == K_BC:
        at -= 2
    return 2 + PER_BLOCK * i + 13 * b + at + 1


def x_at(i, b):
    return (NB * (i % 2) + b) * T


def x_no(slot, b, half):
    return 4 * slot + 2 * b + half + 1


def factor_steps(cur, nxt, s):
    def until(x):
        return x + AHEAD + LEAD.get(x, 0)
    first = until(s - 1) + 1 if s > -AHEAD else 0
    return [(u, t % STEPS) for t in range(first, until(s) + 1) for u in ((cur if t < STEPS else nxt),) if u is not None]


def run_slots(loop, slot, prepare, normalise, opening, close):
    for k in range(OPEN):
        opening(0, k)
        if k >= OPEN_LAG:
            opening(1, k - OPEN_LAG)
    for s in range(CUT, STEPS):
        normalise((0, 0), s)
        if s in OPEN_AT:
            opening(1, OPEN_AT[s])
    for s in range(STEPS):
        prepare((0, 0), s)
        if s in OPEN_LATE:
            opening(1, OPEN_LATE[s])
        if s >= CUT:
            normalise((0, 1), s)
    for s in range(-AHEAD, CUT):
        slot((0, 0), None, (0, 1), s)
        if s >= 0:
            prepare((0, 1), s)

    def rest_of_block(i, last):
        for s in range(CUT, STEPS):
            slot((i, 0), None, (i, 1), s)
            prepare((i, 1), s)
            if not last:
                normalise((i + 1, 0), s)
        for s in range(STEPS):
            slot((i, 1), (i, 0), None if last else (i + 1, 0), s)
            if not last:
                prepare((i + 1, 0), s)
                if s >= CUT:
                    normalise((i + 1, 1), s)
            elif s >= CLOSE:
                close(0, s - CLOSE)
        for s in range(CUT):
            slot(None if last else (i + 1, 0), (i, 1), None if last else (i + 1, 1), s)
            if not last:
                prepare((i + 1, 1), s)
            else:
                close(0, s + STEPS - CLOSE)

    with loop(0, BLOCKS - 1) as i:
        rest_of_block(i, False)
    rest_of_block(BLOCKS - 1, True)


def tower_kernel(nc, ids, table, wpack, outw, res, consts, spack, mpack, rows, lattice, out):
    with ExitStack() as ctx:
        def sb(name, shape, dt=F32):
            return ctx.enter_context(nc.sbuf_tensor(name, shape, dt))

        def sem(name):
            return ctx.enter_context(nc.semaphore(name))

        stack = [sb(f"stack{b}", [P, 4 * T], F32R) for b in range(NB)]
        hi, lo = sb("hi", [P, T], F32R), sb("lo", [P, T], F32R)
        sel = sb("sel", [P, SPACK], F32R)

        bank = [ctx.enter_context(nc.psum_tensor(f"bank{i}", [P, H], F32)) for i in range(8)]
        da_bank, u_bank, y_bank, p_bank = bank[0:2], bank[2:5], bank[5:7], bank[7]

        cst = sb("cst", [P, CPACK])
        mix = sb("mix", [P, MPACK])
        row = sb("row", [P, 8 * D])
        reside = sb("reside", [P, BLOCKS * RES])
        alog = sb("alog", [P, BLOCKS * NG])
        neg_a = sb("neg_a", [P, BLOCKS * NG])
        last_h = sb("last_h", [P, NG])
        a_cur, a_next = sb("a_cur", [P, NG]), sb("a_next", [P, NG])
        wraw = sb("wraw", [P, WPACK])
        out_w = sb("out_w", [P, D])
        w_xi = sb("w_xi", [P, 2 * DI])
        w_z = sb("w_z", [D, DI])
        w_dt = sb("w_dt", [P, DI])
        h = sb("h", [P, NC * D])
        hn = sb("hn", [P, NC * D])
        x2 = sb("x2", [P, NC * D])
        idx_i = sb("idx_i", [P, NC], I32)
        idx_f = sb("idx_f", [P, NC])
        idx_g = sb("idx_g", [P, NC])
        idx_u = sb("idx_u", [P, NC], U32)
        whole_i = sb("whole_i", [P, NC], I32)
        small = sb("small", [P, 12 * NC])
        top8 = sb("top8", [P, NC * 8])

        arena = sb("arena", [P, ARENA])
        place = [0]

        def cut(n):
            place[0] += n
            assert place[0] <= 45600
            return arena[:, place[0] - n:place[0]]

        xs = cut(2 * NB * T)
        after_xs = place[0]
        xn2 = cut(T + 4)
        scr_a, scr_b, scr_c, scr_r = cut(T), cut(T), cut(T), cut(T)
        dl, uu = cut(T), cut(T)
        xi, sz, brep, crep = [cut(T)], [cut(T)], [cut(T)], [cut(T)]
        after_spare = place[0]
        for tensor in (xi, sz, brep, crep):
            tensor.append(cut(T))
        before_steps = place[0]
        hcr = [cut(H) for _ in range(HC_RING)]
        yz = [cut(H) for _ in range(2)]
        dta = [cut(H) for _ in range(DTA_RING)]
        hst_all = cut(H_RING * H)
        hst = [hst_all[:, k * H:(k + 1) * H] for k in range(H_RING)]
        place[0] = before_steps
        o_a, o_b = ([cut(J * D) for _ in range(NB)] for _ in range(2))
        feat_t, x1p = cut(NB * T), cut(NB * (T + 2))
        tok = cut(NC * (D + 1))
        sel_raw = cut(SPACK)
        place[0] = after_xs
        lat = cut(NE * ND * D)
        c_cat, c_feat = [cut(T) for _ in range(NB)], [cut(T) for _ in range(NB)]
        c_a, c_b, c_rest, c_weighed, c_x = ([cut(J * D) for _ in range(NB)] for _ in range(5))
        assert place[0] <= after_spare
        c_mean = [hn[:, b * J * D:(b + 1) * J * D] for b in range(NB)]
        c_gate = [x2[:, b * J * D:(b + 1) * J * D] for b in range(NB)]
        place[0] = after_spare
        xrep = [cut(T) for _ in range(ND)]
        zring = [cut(T) for _ in range(ZRING)]
        srep = [cut(T), cut(T)] + [xs[:, k * T:(k + 1) * T] for k in range(NE - 2)]
        x_stack, gate_stack = stack[0][:, 0:2 * T], stack[0][:, 2 * T:4 * T]

        def tiles(ap, w=D):
            return ap.rearrange("p (c d) -> p c d", d=w)

        def tok_of(b):
            return tiles(tok, D + 1)[:, b * J:(b + 1) * J, :]

        def row_of(n, tiles_=NC):
            return row[:, n * D:(n + 1) * D].unsqueeze(1).to_broadcast([P, tiles_, D])

        def stat_of(b, n):
            return small[:, n * NC + b * J:n * NC + (b + 1) * J]

        def of_tile(ap):
            return ap.unsqueeze(2).to_broadcast([P, J, D])

        ids_in, cst_in, mix_in, row_in, res_in, lat_in = (sem(n) for n in (
            "ids_in", "cst_in", "mix_in", "row_in", "res_in", "lat_in"))
        w_in, outw_in, shifted = sem("w_in"), sem("outw_in"), sem("shifted")
        hi_moved, lo_moved = sem("hi_moved"), sem("lo_moved")
        sel_in, sel_done = sem("sel_in"), sem("sel_done")
        idx_step, hard_step = sem("idx_step"), sem("hard_step")
        gathered = [sem(f"gathered{b}") for b in range(NB)]
        tanh_done, h_done, h_more = sem("tanh_done"), sem("h_done"), sem("h_more")
        ln_step, ln_square, ln_rstd, ln_log = ([sem(f"{n}{b}") for b in range(NB)]
                                               for n in ("ln_step", "ln_square", "ln_rstd", "ln_log"))
        xl_turned, xl_kept, x1_made, x1_kept = sem("xl_turned"), sem("xl_kept"), sem("x1_made"), sem("x1_kept")
        x1_again, x1_zero, x2_made, x2_kept, conv_made = sem("x1_again"), sem("x1_zero"), sem("x2_made"), sem("x2_kept"), sem("conv_made")
        a_capped, a_exp, a_neg, a_copied, a_fetched, xn_zero = sem("a_capped"), sem("a_exp"), sem("a_neg"), sem("a_copied"), sem("a_fetched"), sem("xn_zero")
        x_ready, x_squared, r_ready = sem("x_ready"), sem("x_squared"), sem("r_ready")
        xn_ready, w_scaled, xi_ready, z_ready = sem("xn_ready"), sem("w_scaled"), sem("xi_ready"), sem("z_ready")
        prep_mm, prep_read = sem("prep_mm"), sem("prep_read")
        dt_abs, dt_exp, dt_log, dt_made, u_made, hi_made, lo_made = (sem(n) for n in (
            "dt_abs", "dt_exp", "dt_log", "dt_made", "u_made", "hi_made", "lo_made"))
        da_mm, u_mm, dta_ready = sem("da_mm"), sem("u_mm"), sem("dta_ready")
        last_saved = sem("last_saved")
        bx_done, scan_done, hc_done, hc_summed = sem("bx_done"), sem("scan_done"), sem("hc_done"), sem("hc_summed")
        yd_done, yz_done, out_mm = sem("yd_done"), sem("yz_done"), sem("out_mm")
        cat_act, cat_dve, down_made, down_step = sem("cat_act"), sem("cat_dve"), sem("down_made"), sem("down_step")
        q_turned, q_kept, y3_made = sem("q_turned"), sem("q_kept"), sem("y3_made")
        x3_turned, x3_kept, gate_made, gate_step = sem("x3_turned"), sem("x3_kept"), sem("gate_made"), sem("gate_step")
        gate_exp, rep_made, rep_kept = sem("gate_exp"), sem("rep_made"), sem("rep_kept")
        gate_turned, gate_high, gate_low = sem("gate_turned"), sem("gate_high"), sem("gate_low")
        x3_high, x3_low = sem("x3_high"), sem("x3_low")
        z_dve, z_pool, z_used = sem("z_dve"), sem("z_pool"), sem("z_used")
        lat_kept, proj_made, end_step = sem("lat_kept"), sem("proj_made"), sem("end_step")
        top_done, out_ready, stored = sem("top_done"), sem("out_ready"), sem("stored")

        NZB = NZ // NB
        CLOSING = {0: (0, 1), 3: (2, 3), 4: (5,), 5: (6, 7), 8: (8, 9), 9: (10, 11), 10: (12,), 11: (13,),
                   14: (14, 15, 17), 15: (18, 19), 19: (20, 21), 20: (22,), 22: (23, 24), 25: (25,), 26: (26, 27),
                   28: (28, 29, 30), 29: (31,), 31: (32,)}
        ENDING = {1: (0, 1), 2: (3,), 4: (4, 5, 6), 6: (7, 8), 10: (9,), 11: (10, 11)}
        FFN_STEPS, dve_z, pool_z = [], [], []
        made = 0
        for step in range(32):
            dve_too = step not in CLOSING or step in (4, 10, 11, 20, 29)
            mine = ([dve_z] if dve_too else []) + ([pool_z] if step * 14 // 32 > (step - 1) * 14 // 32 >= 0 else [])
            mine = mine[:NZB - made]
            for who in mine:
                who.append(made)
                made += 1
            FFN_STEPS.append((range(made - len(mine), made), CLOSING.get(step, ()), ()))
        assert made == NZB
        step = 0
        while made < NZ:
            mine = ([dve_z] + ([pool_z] if step % 5 in (1, 3, 4) else []))[:NZ - made]
            for who in mine:
                who.append(made)
                made += 1
            FFN_STEPS.append((range(made - len(mine), made), (), [(0, k) for k in ENDING.get(step, ())]))
            step += 1
        FFN_STEPS += [((), (), [(1, k)]) for k in range(END)]
        SPREAD_AT = {0: [(0, 0), (0, NE), (0, NE + 1), (0, NE + 2)], 6: [(0, 1)], 14: [(0, 2)], 21: [(0, 3)],
                     NZB: [(1, 0), (1, NE + 6), (1, NE + 7), (1, 1)], NZB + 8: [(1, 2)], NZB + 16: [(1, 3)]}
        for k in range(5):
            SPREAD_AT[k + 1] = [(0, NE + k + 3)]
        for k in range(6):
            SPREAD_AT[26 + k] = [(1, NE + k)]
        later = [[part for m in step[0] for part in SPREAD_AT.get(m, ())] for step in FFN_STEPS[1:]] + [[]]
        FFN_STEPS = [(products, parts, closing, ends) for (products, closing, ends), parts in zip(FFN_STEPS, later)]
        SPREADS = [part for m in sorted(SPREAD_AT) for part in SPREAD_AT[m]]
        REP_BANKS = 5

        def factors(m):
            b, n = divmod(m, NZB)
            ei, di = divmod(n, ND)
            after = max(SPREADS.index((b, NE + di)), SPREADS.index((b, ei))) + 1
            return xrep[di], srep[ei], 2 * after

        def products_until(eng, m):
            if sum(k < m for k in dve_z):
                eng.wait_ge(z_dve, sum(k < m for k in dve_z))
            if sum(k < m for k in pool_z):
                eng.wait_ge(z_pool, sum(k < m for k in pool_z))

        def second_bank(b, k):
            return bank[5] if b or k > 16 else bank[6]

        def pool_share_of_norm(eng, ops, unit, s):
            i, b = unit
            w = unit_no(unit)
            if s == 23:
                eng.wait_ge(r_ready, w + 1)
                if not isinstance(i, int) or w > 0:
                    last = (i, 0) if b else (i - 1, 1)
                    eng.wait_ge(prep_read, prep_no(last, K_Z, 1))
                ops.tensor_tensor(xn2[0:D, 3:3 + T], xs[0:D, bass.ds(x_at(i, b), T)],
                                  scr_r[0:D, :], ALU.mult).then_inc(xn_ready, 1)

        def pool_share(eng, ops, unit, s):
            b, w = unit[1], unit_no(unit)
            if s == 18:
                eng.wait_ge(dt_log, w + 1)
                ops.tensor_tensor(dl, dl, scr_c, ALU.add).then_inc(dt_made, 1)
            if s == 20:
                eng.wait_ge(dt_made, w + 1)
                ops.tensor_tensor(uu, dl, xi[b], ALU.mult).then_inc(u_made, 1)

        block = ctx.enter_context(nc.Block())

        @block.sync
        def _(sp):
            sp.dma_start(idx_i[:, :], ids.rearrange("b (p j) -> p b j", j=J)).then_inc(ids_in, 16)
            sp.dma_start(cst[:, :], consts).then_inc(cst_in, 16)
            sp.dma_start(mix[:, :], mpack).then_inc(mix_in, 16)
            sp.dma_start(row[:, :], rows).then_inc(row_in, 16)
            sp.dma_start(reside[:, :], res).then_inc(res_in, 16)
            sp.dma_start(sel_raw, spack).then_inc(sel_in, 16)
            sp.dma_start(wraw[:, :], wpack[0:P, :]).then_inc(w_in, 16)
            sp.dma_start(out_w[:, :], outw[0:P, :]).then_inc(outw_in, 16)

            def shift(unit):
                sp.wait_ge(xn_ready, unit_no(unit) + 1)
                sp.dma_start(xn2[D:2 * D, 2:2 + T], xn2[0:D, 3:3 + T]).then_inc(shifted, 16)

            def stack_up(unit, which):
                for k, (part, made, moved) in enumerate(((hi, hi_made, hi_moved), (lo, lo_made, lo_moved))):
                    sp.wait_ge(made, 2 * unit_no(unit) + which + 1)
                    for side in range(2):
                        cols = slice((2 * which + side) * T, (2 * which + side + 1) * T)
                        sp.dma_start(stack[unit[1]][k * D:(k + 1) * D, cols].bitcast(F32),
                                     part[side * D:(side + 1) * D, :].bitcast(F32)).then_inc(moved, 16)

            def moves(unit, after):
                stack_up(unit, 0)
                stack_up(unit, 1)
                if after is not None:
                    shift(after)

            shift((0, 0))
            moves((0, 0), (0, 1))
            with sp.Fori(0, BLOCKS - 1) as i:
                moves((i, 1), (i + 1, 0))
                sp.wait_ge(prep_read, prep_no((i, 1), K_BC, 3))
                sp.dma_start(wraw[:, :], wpack[bass.ds(i * P + P, P), :]).then_inc(w_in, 16)
                moves((i + 1, 0), (i + 1, 1))
                sp.wait_ge(out_mm, 4 * i + 4)
                sp.dma_start(out_w[:, :], outw[bass.ds(i * P + P, P), :]).then_inc(outw_in, 16)
            moves((BLOCKS - 1, 1), None)
            sp.wait_ge(lo_moved, 64 * 2 * BLOCKS)
            sp.wait_ge(hi_moved, 64 * 2 * BLOCKS)
            sp.wait_ge(prep_read, prep_no((BLOCKS - 1, 1), K_BC, 3))
            sp.wait_ge(yz_done, 4 * BLOCKS - 2)
            sp.dma_start(lat, lattice).then_inc(lat_in, 16)
            for b in range(NB):
                sp.wait_ge(out_ready, b + 1)
                sp.dma_start(out[b].rearrange("(p j) d -> p (j d)", j=J), c_mean[b]).then_inc(stored, 16)
            sp.wait_ge(stored, 32)

        @block.gpsimd
        def _(pool):
            pool.wait_ge(idx_step, 5)
            for c in range(NC):
                nc.gpsimd.indirect_dma_start(
                    tok[:, c * (D + 1):(c + 1) * (D + 1)], None, table[:, :],
                    bass.IndirectOffsetOnAxis(ap=idx_u[:, c:c + 1], axis=0)).then_inc(gathered[c // J], 16)

            def slot(cur, prev, nxt, s):
                unit, t = (cur, s - 1) if s >= 1 else (prev, STEPS - 1)
                if s < 0 or unit is None:
                    return
                b, half = unit[1], t // NG
                n = step_no(unit, t)
                pool.wait_ge(scan_done, n + 1)
                if not (isinstance(n, int) and n < HC_RING):
                    pool.wait_ge(hc_summed, n + 1 - HC_RING)
                nc.gpsimd.tensor_tensor(hcr[t % HC_RING], hst[t % H_RING], crep[b][:, half * H:(half + 1) * H],
                                        ALU.mult).then_inc(hc_done, 1)

            def normalise(unit, s):
                if not (isinstance(unit[0], int) and unit == (0, 0)):
                    pool_share_of_norm(pool, nc.gpsimd, unit, s)

            def prepare(unit, s):
                if not (isinstance(unit[0], int) and unit == (0, 0)):
                    pool_share(pool, nc.gpsimd, unit, s)

            run_slots(pool.Fori, slot, prepare, normalise, lambda b, k: None, lambda b, k: None)

            for m in pool_z:
                x, scores, after = factors(m)
                pool.wait_ge(rep_kept, after)
                if m >= ZRING:
                    pool.wait_ge(z_used, m + 1 - ZRING)
                nc.gpsimd.tensor_tensor(zring[m % ZRING], x, scores, ALU.mult).then_inc(z_pool, 1)

        @block.scalar
        def _(act):
            eps, one = cst[:, CEPS:CEPS + 1], cst[:, C1:C1 + 1]

            def deviation(n, b):
                act.wait_ge(ln_step[b], 5 * n + 4)
                nc.scalar.activation(stat_of(b, 1), stat_of(b, 0), ACT.Ln, bias=eps, scale=1.0 / D) \
                    .then_inc(ln_log[b], 1)
                act.wait_ge(ln_log[b], n + 1)
                nc.scalar.activation(stat_of(b, 2), stat_of(b, 1), ACT.Exp, scale=-0.5).then_inc(ln_rstd[b], 1)

            def square(n, b, src, sq):
                act.wait_ge(ln_step[b], 5 * n + 3)
                nc.scalar.activation(sq, src, ACT.Square).then_inc(ln_square[b], 1)

            act.wait_ge(a_capped, 1)
            nc.scalar.activation(alog[:, :], alog[:, :], ACT.Exp).then_inc(a_exp, 1)
            act.wait_ge(sel_in, 16)
            nc.scalar.copy(sel[:, :], sel_raw).then_inc(sel_done, 1)
            act.wait_ge(cst_in, 16)
            act.wait_ge(mix_in, 16)
            act.wait_ge(a_neg, 1)
            nc.scalar.copy(a_cur[:, :], neg_a[:, 0:NG]).then_inc(a_copied, 1)

            def opening(b, k):
                if k == 0:
                    act.wait_ge(gathered[b], 16 * J)
                    nc.scalar.activation(stat_of(b, 3), tok_of(b)[:, :, D], ACT.Tanh).then_inc(tanh_done, 1)
                if k in (3, 8):
                    square((k - 3) // 5, b, o_a[b], o_b[b])
                if k in (5, 10):
                    deviation((k - 5) // 5, b)
                if k == 13:
                    for half in range(2):
                        q = 2 * b + half
                        act.wait_ge(xl_turned, q + 1)
                        nc.scalar.activation(feat_t[0:D, q * H:(q + 1) * H], bank[half][0:D, :], ACT.Identity,
                                             bias=mix[0:D, LNB:LNB + 1], scale=mix[0:D, LNG:LNG + 1]) \
                            .then_inc(xl_kept, 1)
                if k == 15:
                    x1_v = x1p[0:D, b * (T + 2) + 1:b * (T + 2) + 1 + T].rearrange("p (t j) -> p j t", j=J)
                    for half in range(2):
                        act.wait_ge(x1_made, 2 * b + half + 1)
                        nc.scalar.activation(x1_v[:, 4 * half:4 * half + 4, :],
                                             bank[2 + half][0:D, :].rearrange("p (j t) -> p j t", j=4),
                                             ACT.Identity, bias=mix[0:D, B1:B1 + 1]).then_inc(x1_kept, 1)

            def normalise(unit, s):
                i, b = unit
                w = unit_no(unit)
                if s == 10:
                    act.wait_ge(x_ready, x_no(i, b, 1))
                    if not isinstance(i, int) or w > 0:
                        act.wait_ge(xn_ready, w)
                    nc.scalar.activation(scr_r[0:D, :], xs[0:D, bass.ds(x_at(i, b), T)], ACT.Square) \
                        .then_inc(x_squared, 1)
                if s == 17:
                    for half, src in enumerate((p_bank, y_bank[1])):
                        act.wait_ge(prep_mm, prep_no(unit, K_MS, half))
                        nc.scalar.activation(scr_r[0:D, half * H:(half + 1) * H], src[0:D, :], ACT.Ln,
                                             bias=eps[0:D, :]).then_inc(prep_read, 1)
                    act.wait_ge(prep_read, prep_no(unit, K_MS, 1))
                    nc.scalar.activation(scr_r[0:D, :], scr_r[0:D, :], ACT.Exp, scale=-0.5).then_inc(r_ready, 1)

            def prepare(unit, s):
                i, b = unit
                w = unit_no(unit)
                later = not (isinstance(i, int) and w < 2)
                if s == 0:
                    act.wait_ge(prep_mm, prep_no(unit, K_XI, 0))
                    nc.scalar.activation(xi[b][:, 0:H], p_bank[:, :], ACT.Identity,
                                         bias=wraw[:, CONVB:CONVB + 1]).then_inc(prep_read, 1)
                if s == 2:
                    act.wait_ge(prep_mm, prep_no(unit, K_Z, 0))
                    nc.scalar.copy(sz[b][:, 0:H], y_bank[0][:, :]).then_inc(prep_read, 1)
                if s == 5:
                    if later:
                        act.wait_ge(yz_done, 2 * w - 2)
                    act.wait_ge(prep_mm, prep_no(unit, K_XI, 1))
                    nc.scalar.activation(xi[b][:, H:2 * H], p_bank[:, :], ACT.Identity,
                                         bias=wraw[:, CONVB:CONVB + 1]).then_inc(prep_read, 1)
                    act.wait_ge(prep_mm, prep_no(unit, K_Z, 1))
                    nc.scalar.copy(sz[b][:, H:2 * H], y_bank[0][:, :]).then_inc(prep_read, 1)
                if s == 7:
                    if b == 0:
                        act.wait_ge(prep_mm, prep_no(unit, K_DT))
                        nc.scalar.copy(w_dt[:, :], p_bank[:, 0:DI]).then_inc(prep_read, 1)
                    act.wait_ge(prep_read, prep_no(unit, K_Z, 1))
                    nc.scalar.activation(xi[b], xi[b], ACT.Silu).then_inc(xi_ready, 1)
                    nc.scalar.activation(sz[b], sz[b], ACT.Silu).then_inc(z_ready, 1)
                if s == 8 and b == 0 and not isinstance(i, int):
                    nc.scalar.copy(a_next[:, :], neg_a[:, bass.ds(i * NG, NG)]).then_inc(a_fetched, 1)
                if s in (12, 13):
                    half = s - 12
                    src = (p_bank, y_bank[1])[half]
                    act.wait_ge(prep_mm, prep_no(unit, K_DP, half))
                    nc.scalar.activation(scr_a[:, half * H:(half + 1) * H], src[:, :], ACT.Abs,
                                         bias=wraw[:, DTB:DTB + 1]).then_inc(dt_abs, 1)
                    nc.scalar.activation(dl[:, half * H:(half + 1) * H], src[:, :], ACT.Relu,
                                         bias=wraw[:, DTB:DTB + 1]).then_inc(prep_read, 1)
                if s == 14:
                    act.wait_ge(dt_abs, 2 * w + 2)
                    nc.scalar.activation(scr_b[:, :], scr_a[:, :], ACT.Exp, scale=-1.0).then_inc(dt_exp, 1)
                if s == 17:
                    act.wait_ge(dt_exp, w + 1)
                    nc.scalar.activation(scr_c[:, :], scr_b[:, :], ACT.Ln, bias=one).then_inc(dt_log, 1)
                if s in (21, 25):
                    k = (s - 21) // 4
                    act.wait_ge(u_made if k else dt_made, w + 1)
                    if k or not (isinstance(i, int) and w == 0):
                        act.wait_ge(hi_moved, 64 * w + 32 * k)
                        act.wait_ge(lo_made, 2 * w + k)
                    nc.scalar.copy(hi[:, :], uu if k else dl).then_inc(hi_made, 1)
                if s in (24, 26):
                    half = (s - 24) // 2
                    for k, (dst, src) in enumerate(((brep[b], p_bank), (crep[b], y_bank[0]))):
                        act.wait_ge(prep_mm, prep_no(unit, K_BC, 2 * half + k))
                        nc.scalar.copy(dst[:, half * H:(half + 1) * H], src[:, :]).then_inc(prep_read, 1)

            def factor(unit, t):
                if t == 0 and unit[1] == 0 and not isinstance(unit[0], int):
                    act.wait_ge(a_fetched, unit[0])
                    act.wait_ge(dta_ready, step_no(unit, 0))
                    nc.scalar.copy(a_cur[:, :], a_next[:, :]).then_inc(a_copied, 1)
                    act.wait_ge(a_copied, unit[0] + 1)
                elif t == 0 and unit[1] == 0:
                    act.wait_ge(a_copied, 1)
                g = group_of(t % NG)
                n = step_no(unit, t)
                act.wait_ge(da_mm, n + 1)
                if not (isinstance(n, int) and n < DTA_RING):
                    act.wait_ge(scan_done, n + 1 - DTA_RING)
                nc.scalar.activation(dta[t % DTA_RING], da_bank[t % DA_RING][:, :], ACT.Exp,
                                     scale=a_cur[:, g:g + 1]).then_inc(dta_ready, 1)

            def slot(cur, prev, nxt, s):
                for unit, t in factor_steps(cur, nxt, s):
                    factor(unit, t)

            def close(b, k):
                if k == 0:
                    act.wait_ge(x_ready, x_no(BLOCKS + 1, b, 1))
                    act.wait_ge(prep_read, prep_no((BLOCKS - 1, 1), K_BC, 3))
                    nc.scalar.copy(c_cat[b][0:D, :], xs[0:D, x_at(0, b):x_at(0, b) + T]).then_inc(cat_act, 1)
                if k == 5:
                    square(2, b, c_a[b], c_b[b])
                if k == 7:
                    deviation(2, b)
                if k == 12:
                    for half, src in enumerate((p_bank, second_bank(b, k))):
                        act.wait_ge(q_turned, 2 * b + half + 1)
                        nc.scalar.copy(c_feat[b][0:D, half * H:(half + 1) * H], src[0:D, :]).then_inc(q_kept, 1)
                if k == 17:
                    square(3, b, c_x[b], c_mean[b])
                if k == 19:
                    deviation(3, b)
                if k == 22:
                    for half, src in enumerate((p_bank, second_bank(b, k))):
                        act.wait_ge(x3_turned, 2 * b + half + 1)
                        nc.scalar.copy(c_feat[b][0:D, half * H:(half + 1) * H], src[0:D, :]).then_inc(x3_kept, 1)
                        cols = slice((2 * b + half) * H, (2 * b + half + 1) * H)
                        nc.scalar.copy(x_stack[0:D, cols], src[0:D, :]).then_inc(x3_high, 1)
                if k == 27:
                    act.wait_ge(gate_step, 9 * b + 2)
                    nc.scalar.activation(c_mean[b], c_mean[b], ACT.Exp).then_inc(gate_exp, 1)
                if k == 31:
                    for half, src in enumerate((p_bank, second_bank(b, k))):
                        act.wait_ge(gate_turned, 2 * b + half + 1)
                        cols = slice((2 * b + half) * H, (2 * b + half + 1) * H)
                        nc.scalar.copy(gate_stack[0:D, cols], src[0:D, :]).then_inc(gate_high, 1)

            def end(b, k):
                if k == 1:
                    act.wait_ge(z_used, NZB * (b + 1))
                    nc.scalar.copy(c_feat[b][:, 0:H], bank[6 + b][:, :]).then_inc(lat_kept, 1)
                if k == 6:
                    square(4, b, c_a[b], c_b[b])
                if k == 8:
                    deviation(4, b)

            run_slots(act.Fori, slot, prepare, normalise, opening, close)

            for products, parts, closing, ends in FFN_STEPS:
                for k in closing:
                    close(1, k)
                for b, part in parts:
                    dst = srep[part] if part < NE else xrep[part - NE]
                    if (b, part) == (0, 2):
                        act.wait_ge(cat_act, 2)
                        act.wait_ge(cat_dve, 2)
                    if b:
                        products_until(act, (part + 1) * ND if part < NE else NZB - ND + part - NE + 1)
                    for half in range(2):
                        r_ = 2 * SPREADS.index((b, part)) + half
                        act.wait_ge(rep_made, r_ + 1)
                        nc.scalar.copy(dst[:, half * H:(half + 1) * H], bank[r_ % REP_BANKS][:, :]) \
                            .then_inc(rep_kept, 1)
                for b, k in ends:
                    end(b, k)

        @block.vector
        def _(dve):
            def centre(n, b, src, cen):
                nc.vector.tensor_reduce(stat_of(b, 4), tiles(src), AX_X, ALU.add).then_inc(ln_step[b], 1)
                dve.wait_ge(ln_step[b], 5 * n + 1)
                nc.vector.tensor_scalar(stat_of(b, 5), stat_of(b, 4), -1.0 / D, None, ALU.mult).then_inc(ln_step[b], 1)
                dve.wait_ge(ln_step[b], 5 * n + 2)
                nc.vector.tensor_tensor(tiles(cen), tiles(src), of_tile(stat_of(b, 5)), ALU.add).then_inc(ln_step[b], 1)

            def sum_squares(n, b, sq):
                dve.wait_ge(ln_square[b], n + 1)
                nc.vector.tensor_reduce(stat_of(b, 0), tiles(sq), AX_X, ALU.add).then_inc(ln_step[b], 1)

            def scale(n, b, cen, dst):
                dve.wait_ge(ln_rstd[b], n + 1)
                nc.vector.tensor_tensor(tiles(dst), tiles(cen), of_tile(stat_of(b, 2)), ALU.mult).then_inc(ln_step[b], 1)

            dve.wait_ge(ids_in, 16)
            nc.vector.tensor_copy(idx_f[:, :], idx_i[:, :]).then_inc(idx_step, 1)
            dve.wait_ge(idx_step, 1)
            nc.vector.tensor_scalar(idx_g[:, :], idx_f[:, :], 0.0, float(V), ALU.is_lt, ALU.mult).then_inc(idx_step, 1)
            dve.wait_ge(idx_step, 2)
            nc.vector.tensor_tensor(idx_f[:, :], idx_f[:, :], idx_g[:, :], ALU.add).then_inc(idx_step, 1)
            dve.wait_ge(idx_step, 3)
            nc.vector.tensor_scalar(idx_g[:, :], idx_f[:, :], 0.0, float(V - 1), ALU.max, ALU.min).then_inc(idx_step, 1)
            dve.wait_ge(idx_step, 4)
            nc.vector.tensor_copy(idx_u[:, :], idx_g[:, :]).then_inc(idx_step, 1)
            nc.vector.memset(xn2[:, :], 0.0).then_inc(xn_zero, 1)
            nc.vector.memset(x1p[:, :], 0.0).then_inc(x1_zero, 1)
            dve.wait_ge(res_in, 16)
            nc.vector.tensor_scalar(alog[:, :].rearrange("p (i g) -> p i g", g=NG),
                                    reside[:, :].rearrange("p (i g) -> p i g", g=RES)[:, :, 0:NG],
                                    LOG_MOST, None, ALU.min).then_inc(a_capped, 1)
            dve.wait_ge(a_exp, 1)
            nc.vector.tensor_scalar(neg_a[:, :], alog[:, :], -1.0, None, ALU.mult).then_inc(a_neg, 1)

            def opening(b, k):
                mine = slice(b * J * D, (b + 1) * J * D)
                g, whole, k0 = tok_of(b)[:, :, D], whole_i[:, b * J:(b + 1) * J], 9 * b
                if k == 0:
                    dve.wait_ge(gathered[b], 16 * J)
                    nc.vector.tensor_scalar(stat_of(b, 6), g, GATE_L, 2.0 ** 23, ALU.mult, ALU.min) \
                        .then_inc(hard_step, 1)
                    dve.wait_ge(hard_step, k0 + 1)
                    nc.vector.tensor_scalar(stat_of(b, 6), stat_of(b, 6), -2.0 ** 23, None, ALU.max) \
                        .then_inc(hard_step, 1)
                    dve.wait_ge(hard_step, k0 + 2)
                    nc.vector.tensor_copy(whole, stat_of(b, 6)).then_inc(hard_step, 1)
                    dve.wait_ge(hard_step, k0 + 3)
                    nc.vector.tensor_copy(stat_of(b, 7), whole).then_inc(hard_step, 1)
                    dve.wait_ge(hard_step, k0 + 4)
                    nc.vector.tensor_tensor(stat_of(b, 6), stat_of(b, 6), stat_of(b, 7), ALU.subtract) \
                        .then_inc(hard_step, 1)
                    dve.wait_ge(hard_step, k0 + 5)
                    nc.vector.scalar_tensor_tensor(stat_of(b, 7), stat_of(b, 6), 0.0, stat_of(b, 6), ALU.is_lt,
                                                   ALU.add).then_inc(hard_step, 1)
                    dve.wait_ge(hard_step, k0 + 6)
                    dve.wait_ge(tanh_done, b + 1)
                    nc.vector.scalar_tensor_tensor(stat_of(b, 8), stat_of(b, 7), 1.0 / GATE_L, stat_of(b, 3),
                                                   ALU.mult, ALU.mult).then_inc(hard_step, 1)
                    dve.wait_ge(cst_in, 16)
                    nc.vector.tensor_tensor(tiles(o_a[b]), cst[:, IOTA:IOTA + D].unsqueeze(1).to_broadcast([P, J, D]),
                                            of_tile(g), ALU.is_lt).then_inc(hard_step, 1)
                if k == 1:
                    dve.wait_ge(hard_step, k0 + 8)
                    nc.vector.tensor_tensor(tiles(o_b[b]), tiles(o_a[b]), of_tile(stat_of(b, 8)), ALU.add) \
                        .then_inc(hard_step, 1)
                    dve.wait_ge(hard_step, k0 + 9)
                    nc.vector.tensor_tensor(tiles(h[:, mine]), tok_of(b)[:, :, 0:D], tiles(o_b[b]), ALU.mult) \
                        .then_inc(h_done, 1)
                if k == 2:
                    dve.wait_ge(h_done, b + 1)
                    centre(0, b, h[:, mine], o_a[b])
                if k in (4, 9):
                    sum_squares((k - 4) // 5, b, o_b[b])
                if k == 6:
                    scale(0, b, o_a[b], hn[:, mine])
                if k == 7:
                    dve.wait_ge(ln_step[b], 5)
                    centre(1, b, hn[:, mine], o_a[b])
                if k == 11:
                    scale(1, b, o_a[b], o_b[b])
                if k == 12:
                    dve.wait_ge(row_in, 16)
                    nc.vector.tensor_tensor(tiles(h[:, mine]), tiles(h[:, mine]), row_of(R_B3, J), ALU.add) \
                        .then_inc(h_more, 1)
                    dve.wait_ge(h_more, 2 * b + 1)
                    nc.vector.tensor_tensor(h[:, mine], h[:, mine], hn[:, mine], ALU.add).then_inc(h_more, 1)
                if k == 15:
                    x1_v = x1p[D:2 * D, b * (T + 2):b * (T + 2) + T].rearrange("p (t j) -> p j t", j=J)
                    for half in range(2):
                        dve.wait_ge(x1_kept, 2 * b + half + 1)
                        nc.vector.tensor_scalar(x1_v[:, 4 * half:4 * half + 4, :],
                                                bank[2 + half][0:D, :].rearrange("p (j t) -> p j t", j=4),
                                                mix[0:D, B1:B1 + 1], None, ALU.add).then_inc(x1_again, 1)
                    dve.wait_ge(row_in, 16)
                    dve.wait_ge(x2_made, b + 1)
                    nc.vector.tensor_tensor(tiles(x2[:, mine]), tiles(bank[4][:, :]), row_of(R_B2, J), ALU.add) \
                        .then_inc(x2_kept, 1)
                if k == 17:
                    for half in range(2):
                        q = 2 * b + half
                        dve.wait_ge(conv_made, q + 1)
                        nc.vector.tensor_scalar(xs[0:D, q * H:(q + 1) * H], bank[half][0:D, :],
                                                mix[0:D, HB:HB + 1], None, ALU.add).then_inc(x_ready, 1)
                    dve.wait_ge(x_ready, 2 * b + 2)
                    back = nc.vector.tensor_copy(xs[0:D, (NB + b) * T:(NB + b + 1) * T],
                                                 xs[0:D, b * T:(b + 1) * T][:, ::-1])
                    if b == 1:
                        back.then_inc(x_ready, 4)

            def prepare(unit, s):
                i, b = unit
                w = unit_no(unit)
                if isinstance(i, int) and w == 0:
                    pool_share(dve, nc.vector, unit, s)
                if s in (22, 26):
                    k = (s - 22) // 4
                    dve.wait_ge(hi_made, 2 * w + k + 1)
                    if k or not (isinstance(i, int) and w == 0):
                        dve.wait_ge(lo_moved, 64 * w + 32 * k)
                    nc.vector.tensor_tensor(lo[:, :], uu if k else dl, hi[:, :].bitcast(F32), ALU.subtract) \
                        .then_inc(lo_made, 1)

            def normalise(unit, s):
                i, b = unit
                if s == 31 and b == 0:
                    dve.wait_ge(w_in, 16 * i + 16)
                    nc.vector.scalar_tensor_tensor(
                        w_xi[:, :].rearrange("p (a d) -> p a d", a=2),
                        wraw[:, WX:WX + DI].unsqueeze(1).to_broadcast([P, 2, DI]), wraw[:, RMS:RMS + 1],
                        wraw[:, CW:CW + 2 * DI].rearrange("p (a d) -> p a d", a=2), ALU.mult, ALU.mult)
                    nc.vector.tensor_scalar(w_z[:, :], wraw[0:D, WZ:WZ + DI], wraw[0:D, RMS:RMS + 1], None,
                                            ALU.mult).then_inc(w_scaled, 1)
                if isinstance(unit[0], int) and unit == (0, 0):
                    pool_share_of_norm(dve, nc.vector, unit, s)

            def finish(unit, half):
                i, b = unit
                cols = slice(half * H, (half + 1) * H)
                n = 2 * unit_no(unit) + half
                dve.wait_ge(hc_summed, step_no(unit, NG * (half + 1)))
                if half == 0:
                    dve.wait_ge(z_ready, unit_no(unit) + 1)
                nc.vector.scalar_tensor_tensor(yz[half], xi[b][:, cols],
                                               reside[:, bass.ds(i * RES + NG, 1)], y_bank[half][:, :],
                                               ALU.mult, ALU.add).then_inc(yd_done, 1)
                dve.wait_ge(yd_done, n + 1)
                nc.vector.tensor_tensor(yz[half], yz[half], sz[b][:, cols], ALU.mult).then_inc(yz_done, 1)

            def add_out(unit, half):
                i, b = unit
                dve.wait_ge(out_mm, 2 * unit_no(unit) + half + 1)
                nc.vector.tensor_tensor(xs[0:D, bass.ds(x_at(i, b) + half * H, H)],
                                        xs[0:D, bass.ds(x_at(i, b) + half * H, H)], y_bank[half][0:D, :],
                                        ALU.add).then_inc(x_ready, 1)

            def scan(unit, t):
                half, k = divmod(t, NG)
                n = step_no(unit, t)
                if not (isinstance(n, int) and n < H_RING):
                    dve.wait_ge(hc_done, n + 1 - H_RING)
                if half == 1:
                    initial = last_h[:, k:k + 1]
                    dve.wait_ge(last_saved, 4 * unit_no(unit) + k // 4 + 1)
                else:
                    initial = 0.0
                dve.wait_ge(bx_done, n + 1)
                dve.wait_ge(dta_ready, n + 1)
                nc.vector.tensor_tensor_scan(hst[t % H_RING], dta[t % DTA_RING], u_bank[t % U_RING][:, :], initial,
                                             ALU.mult, ALU.add).then_inc(scan_done, 1)

            def slot(cur, prev, nxt, s):
                if s < 0:
                    return
                if s >= 1 and cur is not None:
                    scan(cur, s - 1)
                if s == 0 and prev is not None:
                    scan(prev, STEPS - 1)
                if cur is not None:
                    n = step_no(cur, s)
                    half = s // NG
                    dve.wait_ge(u_mm, n + 1)
                    nc.vector.tensor_tensor(u_bank[s % U_RING][:, :], u_bank[s % U_RING][:, :],
                                            brep[cur[1]][:, half * H:(half + 1) * H], ALU.mult).then_inc(bx_done, 1)
                if 5 <= s <= NG + 1 and s % 4 == 1 and cur is not None:
                    k = s - 5
                    dve.wait_ge(scan_done, step_no(cur, k + 4))
                    nc.vector.tensor_copy(
                        last_h[:, k:k + 4],
                        hst_all.rearrange("p (k t) -> p k t", t=H)[:, k % H_RING:k % H_RING + 4, H - 1]) \
                        .then_inc(last_saved, 1)
                if s == 20 and cur is not None:
                    finish(cur, 0)
                if s == 22 and cur is not None:
                    add_out(cur, 0)
                if s == 4 and prev is not None:
                    finish(prev, 1)
                if s == 6 and prev is not None:
                    add_out(prev, 1)

            def close(b, k):
                mine = slice(b * J * D, (b + 1) * J * D)
                n, d0, g0 = 2, 5 * b, 9 * b
                if k == 0:
                    dve.wait_ge(x_ready, x_no(BLOCKS + 1, b, 1))
                    dve.wait_ge(prep_read, prep_no((BLOCKS - 1, 1), K_BC, 3))
                    nc.vector.tensor_copy(c_cat[b][D:2 * D, :], xs[0:D, x_at(1, b):x_at(1, b) + T][:, ::-1]) \
                        .then_inc(cat_dve, 1)
                if k == 2:
                    dve.wait_ge(down_made, b + 1)
                    nc.vector.tensor_tensor(tiles(c_b[b]), tiles(p_bank[:, :]), row_of(R_DOWNB, J), ALU.add) \
                        .then_inc(down_step, 1)
                if k == 3:
                    dve.wait_ge(down_step, d0 + 1)
                    centre(n, b, c_b[b], c_a[b])
                if k == 6:
                    sum_squares(n, b, c_b[b])
                if k == 8:
                    scale(n, b, c_a[b], c_b[b])
                    dve.wait_ge(ln_step[b], 5 * n + 5)
                    nc.vector.tensor_tensor(tiles(c_a[b]), tiles(c_b[b]), row_of(R_LNG, J), ALU.mult) \
                        .then_inc(down_step, 1)
                if k == 9:
                    dve.wait_ge(down_step, d0 + 2)
                    nc.vector.tensor_tensor(tiles(c_b[b]), tiles(c_a[b]), row_of(R_LNB, J), ALU.add) \
                        .then_inc(down_step, 1)
                if k == 10:
                    dve.wait_ge(down_step, d0 + 3)
                    nc.vector.tensor_tensor(c_a[b], c_b[b], x2[:, mine], ALU.mult).then_inc(down_step, 1)
                if k == 14:
                    dve.wait_ge(y3_made, b + 1)
                    dve.wait_ge(h_more, 2 * b + 2)
                    nc.vector.tensor_tensor(h[:, mine], h[:, mine], p_bank[:, :], ALU.add).then_inc(down_step, 1)
                if k == 15:
                    dve.wait_ge(down_step, d0 + 5)
                    centre(n + 1, b, h[:, mine], c_x[b])
                if k == 18:
                    sum_squares(n + 1, b, c_mean[b])
                if k == 20:
                    scale(n + 1, b, c_x[b], c_x[b])
                if k == 23:
                    for half, src in enumerate((p_bank, second_bank(b, k))):
                        cols = slice((2 * b + half) * H, (2 * b + half + 1) * H)
                        dve.wait_ge(x3_high, 2 * b + half + 1)
                        nc.vector.tensor_tensor(x_stack[D:2 * D, cols], src[0:D, :], x_stack[0:D, cols].bitcast(F32),
                                                ALU.subtract).then_inc(x3_low, 1)
                top = top8[:, b * J * 8:(b + 1) * J * 8]
                top_v = top.rearrange("p (c k) -> p c k", k=8)
                if k == 25:
                    dve.wait_ge(gate_made, b + 1)
                    nc.vector.tensor_copy(c_gate[b], p_bank[:, :]).then_inc(gate_step, 1)
                    dve.wait_ge(gate_step, g0 + 1)
                    for c in range(J):
                        last = nc.vector.max(top[:, 8 * c:8 * c + 8], c_gate[b][:, c * D:(c + 1) * D])
                    last.then_inc(top_done, 1)
                if k == 26:
                    dve.wait_ge(top_done, b + 1)
                    nc.vector.tensor_tensor(tiles(c_mean[b]), tiles(c_gate[b]),
                                            top_v[:, :, 0:1].to_broadcast([P, J, D]), ALU.subtract) \
                        .then_inc(gate_step, 1)
                    dve.wait_ge(gate_step, g0 + 2)
                    nc.vector.memset(top_v[:, :, TOPK:8], BIG).then_inc(gate_step, 1)
                    dve.wait_ge(gate_step, g0 + 3)
                    for c in range(J):
                        last = nc.vector.match_replace(c_rest[b][:, c * D:(c + 1) * D], top[:, 8 * c:8 * c + 8],
                                                       c_gate[b][:, c * D:(c + 1) * D], -BIG)
                    last.then_inc(gate_step, 1)
                if k == 27:
                    dve.wait_ge(gate_step, g0 + 4)
                    nc.vector.tensor_tensor(c_b[b], c_rest[b], c_gate[b], ALU.not_equal).then_inc(gate_step, 1)
                if k == 28:
                    dve.wait_ge(gate_step, g0 + 5)
                    dve.wait_ge(gate_exp, b + 1)
                    nc.vector.tensor_tensor(c_weighed[b], c_b[b], c_mean[b], ALU.mult).then_inc(gate_step, 1)
                    dve.wait_ge(gate_step, g0 + 6)
                    nc.vector.tensor_reduce(stat_of(b, 9), tiles(c_weighed[b]), AX_X, ALU.add).then_inc(gate_step, 1)
                if k == 29:
                    dve.wait_ge(gate_step, g0 + 7)
                    nc.vector.reciprocal(stat_of(b, 10), stat_of(b, 9)).then_inc(gate_step, 1)
                    dve.wait_ge(gate_step, g0 + 8)
                    nc.vector.tensor_tensor(tiles(c_gate[b]), tiles(c_weighed[b]), of_tile(stat_of(b, 10)),
                                            ALU.mult).then_inc(gate_step, 1)
                if k == 32:
                    for half, src in enumerate((p_bank, second_bank(b, k))):
                        cols = slice((2 * b + half) * H, (2 * b + half + 1) * H)
                        dve.wait_ge(gate_high, 2 * b + half + 1)
                        nc.vector.tensor_tensor(gate_stack[D:2 * D, cols], src[0:D, :],
                                                gate_stack[0:D, cols].bitcast(F32), ALU.subtract) \
                            .then_inc(gate_low, 1)

            def end(b, k):
                mine = slice(b * J * D, (b + 1) * J * D)
                e0, n = 5 * b, 4
                if k == 0:
                    nc.vector.tensor_tensor(tiles(c_x[b]), tiles(c_x[b]), row_of(R_OUTB, J), ALU.add) \
                        .then_inc(end_step, 1)
                if k == 4:
                    dve.wait_ge(end_step, e0 + 1)
                    for half, src in enumerate((bank[6 + b], bank[5])):
                        cols = slice(half * HALF // 2, (half + 1) * HALF // 2)
                        dve.wait_ge(proj_made, 2 * b + half + 1)
                        nc.vector.tensor_tensor(c_rest[b][:, cols], c_x[b][:, cols], src[:, 0:HALF // 2], ALU.add) \
                            .then_inc(end_step, 1)
                if k == 5:
                    dve.wait_ge(end_step, e0 + 3)
                    centre(n, b, c_rest[b], c_a[b])
                if k == 7:
                    sum_squares(n, b, c_b[b])
                if k == 9:
                    scale(n, b, c_a[b], c_b[b])
                    dve.wait_ge(ln_step[b], 5 * n + 5)
                    nc.vector.tensor_tensor(tiles(c_rest[b]), tiles(c_b[b]), row_of(R_FG, J), ALU.mult) \
                        .then_inc(end_step, 1)
                if k == 10:
                    dve.wait_ge(end_step, e0 + 4)
                    nc.vector.tensor_tensor(tiles(c_a[b]), tiles(c_rest[b]), row_of(R_FB, J), ALU.add) \
                        .then_inc(end_step, 1)
                if k == 11:
                    dve.wait_ge(end_step, e0 + 5)
                    nc.vector.tensor_tensor(c_mean[b], c_a[b], h[:, mine], ALU.add).then_inc(out_ready, 1)

            run_slots(dve.Fori, slot, prepare, normalise, opening, close)

            for products, parts, closing, ends in FFN_STEPS:
                for m in products:
                    if m in dve_z:
                        x, scores, after = factors(m)
                        dve.wait_ge(rep_kept, after)
                        if m >= ZRING:
                            dve.wait_ge(z_used, m + 1 - ZRING)
                        nc.vector.tensor_tensor(zring[m % ZRING], x, scores, ALU.mult).then_inc(z_dve, 1)
                for k in closing:
                    close(1, k)
                for b, k in ends:
                    end(b, k)

        @block.tensor
        def _(pe):
            ident = cst[:, IDN:IDN + P]

            pe.wait_ge(cst_in, 16)
            pe.wait_ge(mix_in, 16)
            pe.wait_ge(sel_done, 1)

            def turn_batch(src, banks, made):
                for half, dst in enumerate(banks):
                    for m in range(4):
                        c = 4 * half + m
                        last = nc.tensor.transpose(dst[0:D, m * P:(m + 1) * P], src[:, c * D:(c + 1) * D], ident)
                    last.then_inc(made, 1)

            def opening(b, k):
                if k == 12:
                    pe.wait_ge(ln_step[b], 10)
                    if b:
                        pe.wait_ge(x_ready, 2)
                    turn_batch(o_b[b], bank[0:2], xl_turned)
                if k == 14:
                    if b:
                        pe.wait_ge(x1_kept, 2)
                        pe.wait_ge(x1_again, 2)
                    for half in range(2):
                        q = 2 * b + half
                        pe.wait_ge(xl_kept, q + 1)
                        nc.tensor.matmul(bank[2 + half][0:D, :], mix[0:D, W1:W1 + D], feat_t[0:D, q * H:(q + 1) * H],
                                         start=True, stop=True).then_inc(x1_made, 1)
                    if b:
                        pe.wait_ge(x2_kept, 1)
                    for m in range(J):
                        c = J * b + m
                        last = nc.tensor.matmul(bank[4][:, m * D:(m + 1) * D], feat_t[0:D, c * P:(c + 1) * P],
                                                mix[0:D, W2:W2 + D], start=True, stop=True)
                    last.then_inc(x2_made, 1)
                if k == 16:
                    pe.wait_ge(x1_kept, 2 * b + 2)
                    pe.wait_ge(x1_again, 2 * b + 2)
                    pe.wait_ge(x1_zero, 1)
                    for half in range(2):
                        first = b * (T + 2) + half * H
                        nc.tensor.matmul(bank[half][0:D, :], mix[:, HCONV:HCONV + D], x1p[:, first:first + H],
                                         start=True, stop=False)
                        nc.tensor.matmul(bank[half][0:D, :], mix[0:D, HCONV + D:HCONV + 2 * D],
                                         x1p[0:D, first + 2:first + 2 + H], start=False, stop=True) \
                            .then_inc(conv_made, 1)

            def product(n, dst, lhs, rhs, more=None, back=2):
                if not (isinstance(n, int) and n <= back):
                    pe.wait_ge(prep_read, n - back)
                if more is None:
                    nc.tensor.matmul(dst, lhs, rhs, start=True, stop=True).then_inc(prep_mm, 1)
                else:
                    nc.tensor.matmul(dst, lhs, rhs, start=True, stop=False)
                    nc.tensor.matmul(dst, more[0], more[1], start=False, stop=True).then_inc(prep_mm, 1)

            def inner_product(unit, half):
                o = half * H
                product(prep_no(unit, K_XI, half), p_bank[:, :], w_xi[:, 0:DI], xn2[:, o:o + H],
                        (w_xi[:, DI:2 * DI], xn2[:, o + 2:o + 2 + H]))

            def normalise(unit, s):
                w = unit_no(unit)
                if s == 31:
                    if unit[1] == 0:
                        pe.wait_ge(w_scaled, unit[0] + 1)
                    pe.wait_ge(xn_ready, w + 1)
                    pe.wait_ge(shifted, 16 * w + 16)
                    inner_product(unit, 0)
                if s in (14, 15):
                    half = s - 14
                    pe.wait_ge(x_squared, w + 1)
                    product(prep_no(unit, K_MS, half), (p_bank, y_bank[1])[half][:, :], cst[0:D, ONE:ONE + P],
                            scr_r[0:D, half * H:(half + 1) * H])

            def prepare(unit, s):
                i, b = unit
                w = unit_no(unit)
                if s == 1:
                    inner_product(unit, 1)
                if s in (0, 3):
                    half = s // 3
                    o = half * H + 3
                    product(prep_no(unit, K_Z, half), y_bank[0][:, :], w_z[:, :], xn2[0:D, o:o + H])
                if s == 6 and b == 0:
                    product(prep_no(unit, K_DT), p_bank[:, 0:DI], wraw[0:RANK, X4:X4 + DI],
                            wraw[0:RANK, DTW:DTW + DI])
                if s in (10, 11):
                    half = s - 10
                    o = half * H
                    if half == 0:
                        pe.wait_ge(xi_ready, w + 1)
                    elif not (isinstance(i, int) and w == 0):
                        pe.wait_ge(x_ready, x_no(i + 1, b, 1))
                    product(prep_no(unit, K_DP, half), (p_bank, y_bank[1])[half][:, :], w_dt[:, :],
                            xi[b][:, o:o + H], back=1 if b == 0 and half == 0 else 2)
                if s in (23, 25):
                    half = (s - 23) // 2
                    o = half * H
                    product(prep_no(unit, K_BC, 2 * half), p_bank[:, :], wraw[:, XB:XB + P], xi[b][:, o:o + H])
                    if half == 0 and not (isinstance(i, int) and w == 0):
                        last = (i, 0) if b else (i - 1, 1)
                        pe.wait_ge(x_ready, x_no(last[0] + 2, last[1], 0))
                    product(prep_no(unit, K_BC, 2 * half + 1), y_bank[0][:, :], wraw[:, XC:XC + P],
                            xi[b][:, o:o + H])

            def spread_step(unit, which, t, dst):
                half, k = divmod(t, NG)
                side, g = divmod(group_of(k), NG // 2)
                first = (2 * which + side) * T + half * H
                return nc.tensor.matmul(dst[:, :], sel[:, SEL + g * P:SEL + (g + 1) * P],
                                        stack[unit[1]][:, first:first + H], start=True, stop=True)

            def sum_states(unit, t0):
                half, k0 = divmod(t0, NG)
                n = step_no(unit, t0 + 3)
                pe.wait_ge(hc_done, n + 1)
                if k0 == 0:
                    if not (isinstance(unit[0], int) and unit_no(unit) == 0):
                        last = (unit[0], 0) if unit[1] else (unit[0] - 1, 1)
                        pe.wait_ge(x_ready, x_no(last[0] + 2, last[1], half))
                    if isinstance(unit[0], int) and unit == (BLOCKS - 1, 1):
                        pe.wait_ge(prep_read, prep_no(unit, K_BC, 3))
                        if half == 1:
                            pe.wait_ge(q_kept, 2)
                    else:
                        nxt = (unit[0] + 1, 0) if unit[1] else (unit[0], 1)
                        kind = K_Z if half == 0 else K_DP if isinstance(nxt[0], int) and nxt == (BLOCKS - 1, 1) else K_MS
                        after = nxt if kind != K_MS else (nxt[0] + 1, 0) if nxt[1] else (nxt[0], 1)
                        pe.wait_ge(prep_read, prep_no(after, kind, 1))
                for k in range(k0, k0 + 4):
                    q, m = divmod(group_of(k), 4)
                    last = nc.tensor.matmul(y_bank[half][32 * q:32 * q + 32, :],
                                            cst[:, SUM + m * 32:SUM + (m + 1) * 32], hcr[(t0 + k - k0) % HC_RING],
                                            start=(k0 == 0), stop=(k0 == NG - 4), tile_position=(0, 32 * q))
                last.then_inc(hc_summed, 4)

            def out_product(unit, half):
                pe.wait_ge(yz_done, 2 * unit_no(unit) + half + 1)
                if unit[1] == 0 and half == 0:
                    pe.wait_ge(outw_in, 16 * unit[0] + 16)
                nc.tensor.matmul(y_bank[half][0:D, :], out_w[:, :], yz[half], start=True, stop=True) \
                    .then_inc(out_mm, 1)

            def slot(cur, prev, nxt, s):
                if s == -AHEAD:
                    pe.wait_ge(x_ready, 8)
                    pe.wait_ge(x1_kept, 4)
                    pe.wait_ge(x1_again, 4)
                    pe.wait_ge(x2_kept, 2)
                unit, t = (cur, s + 1) if s + 1 < STEPS else (nxt, 0)
                if unit is not None and s + 1 >= 0:
                    n = step_no(unit, t)
                    if t == 0:
                        pe.wait_ge(hi_moved, 64 * unit_no(unit) + 64)
                        pe.wait_ge(lo_moved, 64 * unit_no(unit) + 64)
                    back = U_RING if t >= U_RING else t + STEPS - (STEPS - 1 - (STEPS - 1 - t) % U_RING)
                    if not (isinstance(n, int) and n < U_RING):
                        pe.wait_ge(scan_done, n + 1 - back)
                    spread_step(unit, 1, t, u_bank[t % U_RING]).then_inc(u_mm, 1)
                for unit, t in factor_steps(cur, nxt, s):
                    n = step_no(unit, t)
                    if t == 0:
                        pe.wait_ge(hi_moved, 64 * unit_no(unit) + 32)
                        pe.wait_ge(lo_moved, 64 * unit_no(unit) + 32)
                    if not (isinstance(n, int) and n < DA_RING):
                        pe.wait_ge(dta_ready, n + 1 - DA_RING)
                    spread_step(unit, 0, t, da_bank[t % DA_RING]).then_inc(da_mm, 1)
                if s >= 6 and s % 4 == 2 and cur is not None:
                    sum_states(cur, s - 6)
                if s == 2 and prev is not None:
                    sum_states(prev, STEPS - 4)
                if s == 21 and cur is not None:
                    out_product(cur, 0)
                if s == 5 and prev is not None:
                    out_product(prev, 1)

            def close(b, k):
                if k == 1:
                    pe.wait_ge(cat_act, b + 1)
                    pe.wait_ge(cat_dve, b + 1)
                    if b == 0:
                        pe.wait_ge(prep_read, prep_no((BLOCKS - 1, 1), K_BC, 3))
                    else:
                        pe.wait_ge(gate_low, 2)
                    cat_v = c_cat[b].rearrange("p (t j) -> p j t", j=J)
                    for m in range(J):
                        last = nc.tensor.matmul(p_bank[:, m * D:(m + 1) * D], cat_v[:, m, :],
                                                mix[:, DOWN:DOWN + D], start=True, stop=True)
                    last.then_inc(down_made, 1)
                if k == 11:
                    pe.wait_ge(down_step, 5 * b + 4)
                    turn_batch(c_a[b], (p_bank, second_bank(b, k)), q_turned)
                if k == 13:
                    pe.wait_ge(q_kept, 2 * b + 2)
                    for m in range(J):
                        last = nc.tensor.matmul(p_bank[:, m * D:(m + 1) * D], c_feat[b][0:D, m * P:(m + 1) * P],
                                                mix[0:D, W3:W3 + D], start=True, stop=True)
                    last.then_inc(y3_made, 1)
                if k == 21:
                    if b == 0:
                        pe.wait_ge(x_ready, x_no(BLOCKS + 1, 1, 0))
                    pe.wait_ge(ln_step[b], 20)
                    turn_batch(c_x[b], (p_bank, second_bank(b, k)), x3_turned)
                if k == 24:
                    pe.wait_ge(x3_kept, 2 * b + 2)
                    pe.wait_ge(x3_low, 2 * b + 1)
                    for m in range(J):
                        last = nc.tensor.matmul(p_bank[:, m * D:(m + 1) * D], c_feat[b][0:D, m * P:(m + 1) * P],
                                                mix[0:D, GATEW:GATEW + D], start=True, stop=True)
                    last.then_inc(gate_made, 1)
                if k == 30:
                    pe.wait_ge(gate_step, 9 * b + 9)
                    pe.wait_ge(x3_low, 2 * b + 2)
                    turn_batch(c_gate[b], (p_bank, second_bank(b, k)), gate_turned)

            def end(b, k):
                if k == 3:
                    pe.wait_ge(lat_kept, b + 1)
                    if b:
                        pe.wait_ge(end_step, 3)
                    for half, dst in enumerate((bank[6 + b], bank[5])):
                        r_ = slice(half * D, (half + 1) * D)
                        for m in range(4):
                            last = nc.tensor.matmul(dst[:, m * D:(m + 1) * D], c_feat[b][r_, m * P:(m + 1) * P],
                                                    mix[r_, OUTW:OUTW + D], start=True, stop=True)
                        last.then_inc(proj_made, 1)

            run_slots(pe.Fori, slot, prepare, normalise, opening, close)

            def use_product(m):
                b, n = divmod(m, NZB)
                if m in pool_z:
                    pe.wait_ge(z_pool, pool_z.index(m) + 1)
                else:
                    pe.wait_ge(z_dve, dve_z.index(m) + 1)
                for half in range(2):
                    last = nc.tensor.matmul(bank[6 + b][half * D:(half + 1) * D, :], lat[:, n * D:(n + 1) * D],
                                            zring[m % ZRING][:, half * H:(half + 1) * H],
                                            start=(n == 0), stop=(n == NZB - 1), tile_position=(0, half * D))
                last.then_inc(z_used, 1)

            pe.wait_ge(x_ready, x_no(BLOCKS + 1, 1, 1))
            pe.wait_ge(x3_low, 2)
            pe.wait_ge(gate_low, 2)
            pe.wait_ge(lat_in, 16)
            used = 0
            for products, parts, closing, ends in FFN_STEPS:
                for b, part in parts:
                    if (b, part) == (1, NE):
                        pe.wait_ge(x3_low, 4)
                    if (b, part) == (1, 0):
                        pe.wait_ge(gate_low, 4)
                    first, src = (SELE + part * P, gate_stack) if part < NE else (SEL + (part - NE) * P, x_stack)
                    for half in range(2):
                        r_ = 2 * SPREADS.index((b, part)) + half
                        if r_ >= REP_BANKS:
                            pe.wait_ge(rep_kept, r_ + 1 - REP_BANKS)
                        q = 2 * b + half
                        nc.tensor.matmul(bank[r_ % REP_BANKS][:, :], sel[:, first:first + P],
                                         src[:, q * H:(q + 1) * H], start=True, stop=True).then_inc(rep_made, 1)
                until = products[0] if products else NZ if ends and ends[0][0] else used
                for m in range(used, until):
                    use_product(m)
                used = until
                for k in closing:
                    close(1, k)
                for b, k in ends:
                    end(b, k)


def _block_weights(np, w, l):
    inproj, convw, xproj = w["inproj"][l], w["convw"][l], w["xproj"][l]
    pack = np.zeros((P, WPACK), np.float32)
    for a in range(2):
        r = slice(a * D, (a + 1) * D)
        pack[r, WX:WX + DI] = inproj[:DI].T
        pack[r, CW:CW + DI] = convw[:, a]
        pack[r, CW + DI:CW + 2 * DI] = convw[:, 2 + a]
        pack[r, RMS] = w["rms"][l]
    pack[:D, WZ:WZ + DI] = inproj[DI:].T
    pack[:, XB:XB + P] = np.repeat(xproj[RANK:RANK + NS].T, GR, axis=1)
    pack[:, XC:XC + P] = np.repeat(xproj[RANK + NS:].T, GR, axis=1)
    pack[:RANK, X4:X4 + DI] = xproj[:RANK]
    pack[:RANK, DTW:DTW + DI] = w["dtw"][l].T
    pack[:, CONVB], pack[:, DTB] = w["convb"][l], w["dtb"][l]
    res = np.zeros((P, RES), np.float32)
    res[:, :NG] = w["Alog"][l].reshape(NG, GR, NS).transpose(2, 1, 0).reshape(P, NG)
    res[:, NG] = w["D"][l]
    return pack, w["outw"][l].T, res


def kernel(**inputs):
    import numpy as np
    import concourse.bacc as bacc
    from concourse.bass_utils import run_bass_kernel_spmd as run

    a = {k: np.asarray(v) for k, v in inputs.items()}
    parts = []
    for l in range(2):
        for d in "fb":
            pre = f"L0_attn_{d}_"
            parts.append(_block_weights(np, {k[len(pre):]: v for k, v in a.items() if k.startswith(pre)}, l))
    consts = np.zeros((P, CPACK), np.float32)
    consts[:, IDN:IDN + P] = np.eye(P)
    spack = np.zeros((P, SPACK), np.float32)
    for r in range(P):
        for k in range(4):
            consts[r, SUM + k * 32 + k * GR + r % GR] = 1.0
        g, d = divmod(r % D, GR)
        spack[r, SEL + g * P + d:SEL + (g + 1) * P:GR] = 1.0
        k, e = divmod(r % D, ES)
        spack[r, SELE + k * P + e * DS:SELE + k * P + (e + 1) * DS] = 1.0
    consts[:, ONE:ONE + P] = 1.0 / D
    consts[:, IOTA:IOTA + D] = np.arange(D)
    consts[:, CEPS], consts[:, C1] = EPS, 1.0
    mp = np.zeros((P, MPACK), np.float32)
    t = "L0_attn_"
    mp[:D, W1:W1 + D], mp[:D, W2:W2 + D], mp[:D, W3:W3 + D] = a[t + "w1"].T, a[t + "w2"].T, a[t + "w3"].T
    mp[:, DOWN:DOWN + D] = a[t + "down_w"].T
    mp[:D, GATEW:GATEW + E] = a["L0_ffn_gate_w"].T
    mp[:D, OUTW:OUTW + D] = mp[D:, OUTW:OUTW + D] = a["L0_ffn_out_w"].T
    for k, (rows_, at) in enumerate(((slice(0, D), HCONV), (slice(D, 2 * D), HCONV), (slice(0, D), HCONV + D))):
        mp[rows_, at:at + D] = a[t + "hconv_w"][:, :, k].T
    mp[:D, LNG], mp[:D, LNB], mp[:D, B1], mp[:D, HB] = a[t + "ln_g"], a[t + "ln_b"], a[t + "b1"], a[t + "hconv_b"]
    rows = np.concatenate([a[t + "b2"], a[t + "down_b"], a[t + "ln_g"], a[t + "ln_b"], a[t + "b3"],
                           a["L0_ffn_out_b"], a["L0_ffn_ln_g"], a["L0_ffn_ln_b"]])
    arrays = {
        "ids": np.ascontiguousarray(a["x"]),
        "table": np.concatenate([a["L0_tok_embedding"], a["L0_tok_gates"][:, None]], axis=1),
        "wpack": np.concatenate([p[0] for p in parts]),
        "outw": np.ascontiguousarray(np.concatenate([p[1] for p in parts])),
        "res": np.concatenate([p[2] for p in parts], axis=1),
        "consts": consts,
        "spack": spack,
        "mpack": mp,
        "rows": np.ascontiguousarray(np.broadcast_to(rows[None], (P, 8 * D))),
        "lattice": np.ascontiguousarray(a["L0_ffn_lattice_weights"].reshape(NE, ES, ND, DS, D)
                                        .transpose(1, 3, 0, 2, 4).reshape(P, NE * ND * D)),
    }
    nc = bacc.Bacc("TRN2", target_bir_lowering=False, num_devices=1)
    aps = [nc.dram_tensor("in_" + k, v.shape, mybir.dt.from_np(v.dtype), kind="ExternalInput").ap()
           for k, v in arrays.items()]
    out = nc.dram_tensor("out_0", (NB, T, D), F32, kind="ExternalOutput").ap()
    tower_kernel(nc, *aps, out)
    r = run(nc, [{"in_" + k: v for k, v in arrays.items()}], core_ids=[0])
    return r.results[0]["out_0"]
```
